# Optimizing a Trainium2 kernel written in Bass

```python
import numpy as np
import jax
import jax.numpy as jnp

def _softmax(x, axis=-1):
    return jax.nn.softmax(x, axis=axis)

def _gelu(x):
    return jax.nn.gelu(x, approximate=True)

def _silu(x):
    return jax.nn.silu(x)

def _sigmoid(x):
    return jax.nn.sigmoid(x)

def _layernorm(x, axis=-1, eps=1e-05):
    m = jnp.mean(x, axis=axis, keepdims=True)
    v = jnp.var(x, axis=axis, keepdims=True)
    return (x - m) / jnp.sqrt(v + eps)

def _scatter_add(tgt, idx, src, axis=0):
    return tgt.at[idx].add(src)

def _segment_sum(src, seg, n):
    return jax.ops.segment_sum(src, seg, n)
kernel_name = 'mk_adaln_attn_ffn_d2_seqx_r4_0cb072'

def setup_inputs(seed: int=0):
    np.random.seed(seed)
    _w = jnp.asarray

    def _rec_inputs():
        import jax
        import jax.numpy as jnp
        _rk = jax.random.key(seed)
        x = 7.22e-05 + 1 * jax.random.normal(jax.random.fold_in(_rk, 1), (8, 512, 256), jnp.float32)
        _lenS = 512 - jax.random.randint(jax.random.fold_in(_rk, 7), (8,), 0, max(1, 512 // 4) + 1, jnp.int32)
        _lenS2 = 512 - jax.random.randint(jax.random.fold_in(_rk, 8), (8,), 0, max(1, 512 // 4) + 1, jnp.int32)
        condB_tauraws = -5.74692 + 0.777674 * jax.random.normal(jax.random.fold_in(_rk, 11), (8,), jnp.float32)
        cond_256 = -0.000235209 + 0.019331 * jax.random.normal(jax.random.fold_in(_rk, 12), (8, 64), jnp.float32)
        condB_bn2 = jnp.zeros((8,), jnp.float32)
        cond_1024 = -4.10585e-05 + 0.0199478 * jax.random.normal(jax.random.fold_in(_rk, 14), (8, 256), jnp.float32)
        itok_B_0_7 = jax.random.randint(jax.random.fold_in(_rk, 15), (8,), 0, 8, jnp.int32)
        itok_B_0_6 = jax.random.randint(jax.random.fold_in(_rk, 16), (8,), 0, 7, jnp.int32)
        return (x, condB_tauraws, cond_256, condB_bn2, cond_1024, itok_B_0_7, itok_B_0_6)
    x, condB_tauraws, cond_256, condB_bn2, cond_1024, itok_B_0_7, itok_B_0_6 = _rec_inputs()

    def _L0_cond_setup():
        import jax, jax.numpy as jnp
        import numpy as np
        import math
        B, T, E, D = (4, 512, 256, 4)

        def _tau_init(t):
            a = 0.1 ** (1.0 / max(t - 1, 1))
            tt = -math.log(max(a, 1e-10))
            return math.log(math.exp(tt) - 1 + 1e-10)

        def causal_ema(b, tau_raw):
            alpha = jnp.exp(-jax.nn.softplus(tau_raw)).astype(b.dtype)

            def step(h, bt):
                h = alpha * h + bt
                return (h, h)
            h0 = jnp.zeros((b.shape[0], b.shape[2]), b.dtype)
            _, hs = jax.lax.scan(step, h0, jnp.swapaxes(b, 0, 1))
            return jnp.swapaxes(hs, 0, 1)
        key = jax.random.key(seed)
        ks = jax.random.split(key, 10)
        s = 0.02
        return {'x': jax.random.normal(ks[0], (B, T, E), jnp.float32), 'tau_ctx': jnp.float32(_tau_init(max(T // 2, 4))), 'tau_raws': jnp.array([_tau_init(max(T // 2 ** i, 2)) for i in range(D)], jnp.float32), 'Wg': jax.random.normal(ks[1], (E, 2 * E), jnp.float32) * s, 'bg': jnp.full((E,), -0.5, jnp.float32), 'Wn1': jax.random.normal(ks[2], (E // 4, E), jnp.float32) * s, 'bn1': jnp.zeros((E // 4,), jnp.float32), 'Wn2': jax.random.normal(ks[3], (D, E // 4), jnp.float32) * s, 'bn2': jnp.zeros((D,), jnp.float32), 'blend': jax.random.normal(ks[4], (D, E), jnp.float32) * s, 'Wsoma': jax.random.normal(ks[5], (E, E), jnp.float32) * s, 'bsoma': jnp.zeros((E,), jnp.float32), 'Wtemp': jax.random.normal(ks[6], (E, E), jnp.float32) * s, 'btemp': jnp.zeros((E,), jnp.float32), 'Wout': jax.random.normal(ks[7], (E, E), jnp.float32) * s, 'gamma': jnp.ones((E,), jnp.float32), 'beta': jnp.zeros((E,), jnp.float32)}
    _L0_cond_all = _L0_cond_setup()
    _L0_cond_in = {k: v for k, v in _L0_cond_all.items() if k in ('tau_ctx', 'Wg', 'bg', 'Wn1', 'bn1', 'Wsoma', 'bsoma', 'Wtemp', 'btemp', 'Wout', 'gamma', 'beta')}
    del _L0_cond_all

    def _L0_attn_setup():
        import jax, jax.numpy as jnp
        import numpy as np
        D_MODEL, D_STATE, D_CONV, D_INNER, DT_RANK = (256, 16, 4, 512, 64)
        BATCH, LENGTH = (4, 512)

        def _mamba_fwd(x, W_in, conv_w, conv_b, W_x, W_dt, b_dt, A_raw, D, W_out):
            b, l, _ = x.shape
            d_inner = W_in.shape[0] // 2
            d_state = A_raw.shape[0]
            dt_rank = W_dt.shape[1]
            xz = jnp.einsum('bld,ed->ble', x, W_in)
            xc, z = jnp.split(xz, 2, axis=-1)
            xc = xc.transpose(0, 2, 1)
            k = conv_w.shape[-1]
            xc = jax.lax.conv_general_dilated(xc, conv_w, (1,), [(k - 1, 0)], dimension_numbers=('NCH', 'OIH', 'NCH'), feature_group_count=d_inner) + conv_b[None, :, None]
            xc = jax.nn.silu(xc).transpose(0, 2, 1)
            dbc = jnp.einsum('bld,ed->ble', xc, W_x)
            dt, B, C = jnp.split(dbc, [dt_rank, dt_rank + d_state], axis=-1)
            delta = jax.nn.softplus(jnp.einsum('blr,dr->bld', dt, W_dt) + b_dt)
            A = -jnp.exp(A_raw)

            def step(h, inp):
                x_t, dlt, B_t, C_t = inp
                dA = jnp.exp(dlt[:, None, :] * A[None])
                h = dA * h + dlt[:, None, :] * B_t[:, :, None] * x_t[:, None, :]
                y_t = jnp.einsum('bn,bnd->bd', C_t, h) + D * x_t
                return (h, y_t)
            h0 = jnp.zeros((b, d_state, d_inner), x.dtype)
            xs = (xc.transpose(1, 0, 2), delta.transpose(1, 0, 2), B.transpose(1, 0, 2), C.transpose(1, 0, 2))
            _, ys = jax.lax.scan(step, h0, xs)
            y = ys.transpose(1, 0, 2) * jax.nn.silu(z)
            return jnp.einsum('bld,md->blm', y, W_out)
        key = jax.random.key(seed)
        ks = jax.random.split(key, 10)
        dt_init_std = DT_RANK ** (-0.5)
        dt_min, dt_max, dt_floor = (0.001, 0.1, 0.0001)
        u = jax.random.uniform(ks[9], (D_INNER,))
        dt = jnp.clip(jnp.exp(u * (np.log(dt_max) - np.log(dt_min)) + np.log(dt_min)), dt_floor, None)
        b_dt = dt + jnp.log(-jnp.expm1(-dt))
        return {'x': jax.random.normal(ks[0], (BATCH, LENGTH, D_MODEL), jnp.float32), 'W_in': jax.random.normal(ks[1], (2 * D_INNER, D_MODEL), jnp.float32) * D_MODEL ** (-0.5), 'conv_w': jax.random.normal(ks[2], (D_INNER, 1, D_CONV), jnp.float32) * D_CONV ** (-0.5), 'conv_b': jax.random.normal(ks[3], (D_INNER,), jnp.float32) * 0.01, 'W_x': jax.random.normal(ks[4], (DT_RANK + 2 * D_STATE, D_INNER), jnp.float32) * D_INNER ** (-0.5), 'W_dt': jax.random.uniform(ks[5], (D_INNER, DT_RANK), jnp.float32, -dt_init_std, dt_init_std), 'b_dt': b_dt.astype(jnp.float32), 'A_raw': jax.random.normal(ks[6], (D_STATE, D_INNER), jnp.float32), 'D': jax.random.normal(ks[7], (D_INNER,), jnp.float32), 'W_out': jax.random.normal(ks[8], (D_MODEL, D_INNER), jnp.float32) * D_INNER ** (-0.5)}
    _L0_attn_all = _L0_attn_setup()
    _L0_attn_in = {k: v for k, v in _L0_attn_all.items() if k in ('W_in', 'conv_w', 'conv_b', 'W_x', 'W_dt', 'b_dt', 'A_raw', 'D', 'W_out')}
    del _L0_attn_all

    def _L0_cond2_setup():
        import jax, jax.numpy as jnp
        import numpy as np
        S, O, H = (8, 256, 256)
        B, N = (32, 128)
        key = jax.random.key(seed)
        k1, k2, k3, k4 = jax.random.split(key, 4)
        x = jax.random.normal(k1, (B, N, H), dtype=jnp.float32)
        subject_id = jax.random.randint(k2, (B,), 0, S)
        wbound = jnp.sqrt(2.0 / 6.0) * jnp.sqrt(3.0 / H)
        weight = jax.random.uniform(k3, (S, O, H), minval=-wbound, maxval=wbound, dtype=jnp.float32)
        bbound = 1.0 / jnp.sqrt(H)
        bias = jax.random.uniform(k4, (S, O), minval=-bbound, maxval=bbound, dtype=jnp.float32)
        return {'x': x, 'subject_id': subject_id, 'weight': weight, 'bias': bias}
    _L0_cond2_all = _L0_cond2_setup()
    _L0_cond2_in = {k: v for k, v in _L0_cond2_all.items() if k in ('weight', 'bias')}
    del _L0_cond2_all

    def _L0_ffn_setup():
        import jax, jax.numpy as jnp
        import numpy as np
        B, S, D, H, E, K = (4, 512, 256, 512, 8, 2)
        TEMP = 5.0
        EPS = 1e-09
        key = jax.random.key(seed)
        k_x, k_wg, k_w1, k_w2 = jax.random.split(key, 4)
        scale = 0.02
        return {'x': jax.random.normal(k_x, (B, S, D), dtype=jnp.float32), 'Wg': jax.random.normal(k_wg, (D, E), dtype=jnp.float32) * scale, 'bg': jnp.zeros((E,), dtype=jnp.float32), 'W1': jax.random.normal(k_w1, (E, D, H), dtype=jnp.float32) * scale, 'b1': jnp.zeros((E, H), dtype=jnp.float32), 'W2': jax.random.normal(k_w2, (E, H, D), dtype=jnp.float32) * scale, 'b2': jnp.zeros((E, D), dtype=jnp.float32)}
    _L0_ffn_all = _L0_ffn_setup()
    _L0_ffn_in = {k: v for k, v in _L0_ffn_all.items() if k in ('Wg', 'bg', 'W1', 'b1', 'W2', 'b2')}
    del _L0_ffn_all

    def _L1_cond_setup():
        import jax, jax.numpy as jnp
        import numpy as np
        B, S, D, F = (32, 128, 256, 1024)
        R_COMMON, R_DOMAIN, E = (16, 16, 8)
        ALPHA = 2.0

        def _expert_lora(x, expert_ids, Wa, Wb):
            Ab = Wa[expert_ids]
            Bb = Wb[expert_ids]
            low = jnp.einsum('bsd,brd->bsr', x, Ab)
            return ALPHA * jnp.einsum('bsr,bor->bso', low, Bb)
        key = jax.random.key(seed)
        ks = jax.random.split(key, 12)
        sd = lambda k, shape: jax.random.normal(k, shape, dtype=jnp.float32) * (1.0 / np.sqrt(shape[-1]))
        return {'hidden_states': jax.random.normal(ks[0], (B, S, D), dtype=jnp.float32), 'expert_ids': jax.random.randint(ks[1], (B,), 0, E, dtype=jnp.int32), 'wi': sd(ks[2], (F, D)), 'wo': sd(ks[3], (D, F)), 'common_wi_a': sd(ks[4], (R_COMMON, D)), 'common_wi_b': sd(ks[5], (F, R_COMMON)), 'common_wo_a': sd(ks[6], (R_COMMON, F)), 'common_wo_b': sd(ks[7], (D, R_COMMON)), 'experts_wi_a': sd(ks[8], (E, R_DOMAIN, D)), 'experts_wi_b': sd(ks[9], (F, R_DOMAIN)) * jnp.ones((E, 1, 1)) * 0.0 + sd(ks[9], (E, F, R_DOMAIN)), 'experts_wo_a': sd(ks[10], (E, R_DOMAIN, F)), 'experts_wo_b': sd(ks[11], (E, D, R_DOMAIN))}
    _L1_cond_all = _L1_cond_setup()
    _L1_cond_in = {k: v for k, v in _L1_cond_all.items() if k in ('wi', 'wo', 'common_wi_a', 'common_wi_b', 'common_wo_a', 'common_wo_b', 'experts_wi_a', 'experts_wi_b', 'experts_wo_a', 'experts_wo_b')}
    del _L1_cond_all

    def _L1_attn_setup():
        import jax, jax.numpy as jnp
        import numpy as np
        B, N = (2, 512)
        H, R = (8, 64)
        IN_DIM, OUT_DIM = (128, 128)
        D = IN_DIM + OUT_DIM
        INIT = 1.0
        key = jax.random.key(seed)
        k1, k2, k3, k4 = jax.random.split(key, 4)
        x = jax.random.normal(k1, (B, N, D), dtype=jnp.float32)
        Wq = jax.random.normal(k2, (H * R, D), dtype=jnp.float32) * (INIT / np.sqrt(H * R * D))
        Wk = jax.random.normal(k3, (H * R, D), dtype=jnp.float32) * (INIT / np.sqrt(H * R * D))
        Wv = jax.random.normal(k4, (H * D, D), dtype=jnp.float32) * (INIT / np.sqrt(H * D * D))
        Wk = Wk.at[:, -1].set(0.0)
        rows = np.arange(1, H + 1) * D - 1
        Wv = Wv.at[rows, :IN_DIM].set(0.0)
        return {'x': x, 'Wq': Wq, 'Wk': Wk, 'Wv': Wv}
    _L1_attn_all = _L1_attn_setup()
    _L1_attn_in = {k: v for k, v in _L1_attn_all.items() if k in ('Wq', 'Wk', 'Wv')}
    del _L1_attn_all

    def _L1_cond2_setup():
        import jax, jax.numpy as jnp
        import numpy as np
        N_PROFILES = 8
        HIDDEN = 256
        BOTTLENECK = 128
        EPS = 1e-05
        key = jax.random.key(seed)
        ks = jax.random.split(key, 8)
        B, S, H, K, P = (16, 512, HIDDEN, BOTTLENECK, N_PROFILES)
        down_w = jax.random.normal(ks[0], (P, H, K), dtype=jnp.float32) * (1.0 / np.sqrt(H))
        down_b = jax.random.normal(ks[1], (P, K), dtype=jnp.float32) * 0.01
        up_w = jax.random.normal(ks[2], (P, K, H), dtype=jnp.float32) * (1.0 / np.sqrt(K))
        up_b = jax.random.normal(ks[3], (P, H), dtype=jnp.float32) * 0.01
        ln_g = jnp.ones((P, H), dtype=jnp.float32)
        ln_b = jnp.zeros((P, H), dtype=jnp.float32)
        hidden = jax.random.normal(ks[4], (B, S, H), dtype=jnp.float32)
        profile_ids = jax.random.randint(ks[5], (B,), 0, P)
        return {'hidden': hidden, 'profile_ids': profile_ids, 'down_w': down_w, 'down_b': down_b, 'up_w': up_w, 'up_b': up_b, 'ln_g': ln_g, 'ln_b': ln_b}
    _L1_cond2_all = _L1_cond2_setup()
    _L1_cond2_in = {k: v for k, v in _L1_cond2_all.items() if k in ('down_w', 'down_b', 'up_w', 'up_b', 'ln_g', 'ln_b')}
    del _L1_cond2_all

    def _L1_ffn_setup():
        import jax, jax.numpy as jnp
        import numpy as np
        TOP_K = 4
        CAP_FACTOR = 4

        def swiglu(x, w1, w2, w3):
            return jax.nn.silu(x @ w1) * (x @ w3) @ w2
        key = jax.random.key(seed)
        ks = jax.random.split(key, 8)
        B, S, D, H, E = (2, 512, 256, 128, 32)
        Hs = 2 * H
        sd = lambda *sh: 1.0 / np.sqrt(sh[-2])
        x = jax.random.normal(ks[0], (B, S, D), dtype=jnp.float32)
        Wg = jax.random.normal(ks[1], (D, E), dtype=jnp.float32) * (1.0 / np.sqrt(D))
        W1 = jax.random.normal(ks[2], (E, D, H), dtype=jnp.float32) * (1.0 / np.sqrt(D))
        W3 = jax.random.normal(ks[3], (E, D, H), dtype=jnp.float32) * (1.0 / np.sqrt(D))
        W2 = jax.random.normal(ks[4], (E, H, D), dtype=jnp.float32) * (1.0 / np.sqrt(H))
        Ws1 = jax.random.normal(ks[5], (D, Hs), dtype=jnp.float32) * (1.0 / np.sqrt(D))
        Ws3 = jax.random.normal(ks[6], (D, Hs), dtype=jnp.float32) * (1.0 / np.sqrt(D))
        Ws2 = jax.random.normal(ks[7], (Hs, D), dtype=jnp.float32) * (1.0 / np.sqrt(Hs))
        return {'x': x, 'Wg': Wg, 'W1': W1, 'W2': W2, 'W3': W3, 'Ws1': Ws1, 'Ws2': Ws2, 'Ws3': Ws3}
    _L1_ffn_all = _L1_ffn_setup()
    _L1_ffn_in = {k: v for k, v in _L1_ffn_all.items() if k in ('Wg', 'W1', 'W2', 'W3', 'Ws1', 'Ws2', 'Ws3')}
    del _L1_ffn_all
    return {'x': x, 'condB_tauraws': condB_tauraws, 'cond_256': cond_256, 'condB_bn2': condB_bn2, 'cond_1024': cond_1024, 'itok_B_0_7': itok_B_0_7, 'itok_B_0_6': itok_B_0_6, 'L0_cond_tau_ctx': _L0_cond_in['tau_ctx'], 'L0_cond_Wg': _L0_cond_in['Wg'], 'L0_cond_bg': _L0_cond_in['bg'], 'L0_cond_Wn1': _L0_cond_in['Wn1'], 'L0_cond_bn1': _L0_cond_in['bn1'], 'L0_cond_Wsoma': _L0_cond_in['Wsoma'], 'L0_cond_bsoma': _L0_cond_in['bsoma'], 'L0_cond_Wtemp': _L0_cond_in['Wtemp'], 'L0_cond_btemp': _L0_cond_in['btemp'], 'L0_cond_Wout': _L0_cond_in['Wout'], 'L0_cond_gamma': _L0_cond_in['gamma'], 'L0_cond_beta': _L0_cond_in['beta'], 'L0_attn_W_in': _L0_attn_in['W_in'], 'L0_attn_conv_w': _L0_attn_in['conv_w'], 'L0_attn_conv_b': _L0_attn_in['conv_b'], 'L0_attn_W_x': _L0_attn_in['W_x'], 'L0_attn_W_dt': _L0_attn_in['W_dt'], 'L0_attn_b_dt': _L0_attn_in['b_dt'], 'L0_attn_A_raw': _L0_attn_in['A_raw'], 'L0_attn_D': _L0_attn_in['D'], 'L0_attn_W_out': _L0_attn_in['W_out'], 'L0_cond2_weight': _L0_cond2_in['weight'], 'L0_cond2_bias': _L0_cond2_in['bias'], 'L0_ffn_Wg': _L0_ffn_in['Wg'], 'L0_ffn_bg': _L0_ffn_in['bg'], 'L0_ffn_W1': _L0_ffn_in['W1'], 'L0_ffn_b1': _L0_ffn_in['b1'], 'L0_ffn_W2': _L0_ffn_in['W2'], 'L0_ffn_b2': _L0_ffn_in['b2'], 'L1_cond_wi': _L1_cond_in['wi'], 'L1_cond_wo': _L1_cond_in['wo'], 'L1_cond_common_wi_a': _L1_cond_in['common_wi_a'], 'L1_cond_common_wi_b': _L1_cond_in['common_wi_b'], 'L1_cond_common_wo_a': _L1_cond_in['common_wo_a'], 'L1_cond_common_wo_b': _L1_cond_in['common_wo_b'], 'L1_cond_experts_wi_a': _L1_cond_in['experts_wi_a'], 'L1_cond_experts_wi_b': _L1_cond_in['experts_wi_b'], 'L1_cond_experts_wo_a': _L1_cond_in['experts_wo_a'], 'L1_cond_experts_wo_b': _L1_cond_in['experts_wo_b'], 'L1_attn_Wq': _L1_attn_in['Wq'], 'L1_attn_Wk': _L1_attn_in['Wk'], 'L1_attn_Wv': _L1_attn_in['Wv'], 'L1_cond2_down_w': _L1_cond2_in['down_w'], 'L1_cond2_down_b': _L1_cond2_in['down_b'], 'L1_cond2_up_w': _L1_cond2_in['up_w'], 'L1_cond2_up_b': _L1_cond2_in['up_b'], 'L1_cond2_ln_g': _L1_cond2_in['ln_g'], 'L1_cond2_ln_b': _L1_cond2_in['ln_b'], 'L1_ffn_Wg': _L1_ffn_in['Wg'], 'L1_ffn_W1': _L1_ffn_in['W1'], 'L1_ffn_W2': _L1_ffn_in['W2'], 'L1_ffn_W3': _L1_ffn_in['W3'], 'L1_ffn_Ws1': _L1_ffn_in['Ws1'], 'L1_ffn_Ws2': _L1_ffn_in['Ws2'], 'L1_ffn_Ws3': _L1_ffn_in['Ws3']}

def reference(x, condB_tauraws, cond_256, condB_bn2, cond_1024, itok_B_0_7, itok_B_0_6, L0_cond_tau_ctx, L0_cond_Wg, L0_cond_bg, L0_cond_Wn1, L0_cond_bn1, L0_cond_Wsoma, L0_cond_bsoma, L0_cond_Wtemp, L0_cond_btemp, L0_cond_Wout, L0_cond_gamma, L0_cond_beta, L0_attn_W_in, L0_attn_conv_w, L0_attn_conv_b, L0_attn_W_x, L0_attn_W_dt, L0_attn_b_dt, L0_attn_A_raw, L0_attn_D, L0_attn_W_out, L0_cond2_weight, L0_cond2_bias, L0_ffn_Wg, L0_ffn_bg, L0_ffn_W1, L0_ffn_b1, L0_ffn_W2, L0_ffn_b2, L1_cond_wi, L1_cond_wo, L1_cond_common_wi_a, L1_cond_common_wi_b, L1_cond_common_wo_a, L1_cond_common_wo_b, L1_cond_experts_wi_a, L1_cond_experts_wi_b, L1_cond_experts_wo_a, L1_cond_experts_wo_b, L1_attn_Wq, L1_attn_Wk, L1_attn_Wv, L1_cond2_down_w, L1_cond2_down_b, L1_cond2_up_w, L1_cond2_up_b, L1_cond2_ln_g, L1_cond2_ln_b, L1_ffn_Wg, L1_ffn_W1, L1_ffn_W2, L1_ffn_W3, L1_ffn_Ws1, L1_ffn_Ws2, L1_ffn_Ws3):
    import jax
    import jax.numpy as jnp

    def _L0_cond_ref(x, tau_ctx, tau_raws, Wg, bg, Wn1, bn1, Wn2, bn2, blend, Wsoma, bsoma, Wtemp, btemp, Wout, gamma, beta):
        import jax, jax.numpy as jnp
        import numpy as np
        import math
        B, T, E, D = (4, 512, 256, 4)

        def _tau_init(t):
            a = 0.1 ** (1.0 / max(t - 1, 1))
            tt = -math.log(max(a, 1e-10))
            return math.log(math.exp(tt) - 1 + 1e-10)

        def causal_ema(b, tau_raw):
            alpha = jnp.exp(-jax.nn.softplus(tau_raw)).astype(b.dtype)

            def step(h, bt):
                h = alpha * h + bt
                return (h, h)
            h0 = jnp.zeros((b.shape[0], b.shape[2]), b.dtype)
            _, hs = jax.lax.scan(step, h0, jnp.swapaxes(b, 0, 1))
            return jnp.swapaxes(hs, 0, 1)
        ctx = causal_ema(x, tau_ctx)
        gate_in = jnp.concatenate([x, ctx], axis=-1)
        wg = jax.nn.sigmoid(jnp.einsum('btc,ec->bte', gate_in, Wg) + bg)
        gated = x * wg
        h1 = jax.nn.gelu(jnp.einsum('btc,hc->bth', x, Wn1) + bn1, approximate=False)
        mod = 0.5 + jax.nn.sigmoid(jnp.einsum('bth,dh->btd', h1, Wn2) + bn2)
        traces = jax.vmap(lambda tau, m: causal_ema(gated * m[..., None], tau))(tau_raws, jnp.moveaxis(mod, -1, 0))
        blend_w = jax.nn.softmax(blend, axis=0)
        temporal = jnp.einsum('dbtc,dc->btc', traces, blend_w)
        gate = jax.nn.sigmoid(jnp.einsum('btc,ec->bte', temporal, Wtemp) + btemp)
        soma = jax.nn.gelu(jnp.einsum('btc,ec->bte', x, Wsoma) + bsoma, approximate=False)
        out = jnp.einsum('btc,ec->bte', soma * gate, Wout)
        mu = out.mean(-1, keepdims=True)
        var = out.var(-1, keepdims=True)
        return (out - mu) / jnp.sqrt(var + 1e-05) * gamma + beta

    def _L0_attn_ref(x, W_in, conv_w, conv_b, W_x, W_dt, b_dt, A_raw, D, W_out):
        import jax, jax.numpy as jnp
        import numpy as np
        D_MODEL, D_STATE, D_CONV, D_INNER, DT_RANK = (256, 16, 4, 512, 64)
        BATCH, LENGTH = (4, 512)

        def _mamba_fwd(x, W_in, conv_w, conv_b, W_x, W_dt, b_dt, A_raw, D, W_out):
            b, l, _ = x.shape
            d_inner = W_in.shape[0] // 2
            d_state = A_raw.shape[0]
            dt_rank = W_dt.shape[1]
            xz = jnp.einsum('bld,ed->ble', x, W_in)
            xc, z = jnp.split(xz, 2, axis=-1)
            xc = xc.transpose(0, 2, 1)
            k = conv_w.shape[-1]
            xc = jax.lax.conv_general_dilated(xc, conv_w, (1,), [(k - 1, 0)], dimension_numbers=('NCH', 'OIH', 'NCH'), feature_group_count=d_inner) + conv_b[None, :, None]
            xc = jax.nn.silu(xc).transpose(0, 2, 1)
            dbc = jnp.einsum('bld,ed->ble', xc, W_x)
            dt, B, C = jnp.split(dbc, [dt_rank, dt_rank + d_state], axis=-1)
            delta = jax.nn.softplus(jnp.einsum('blr,dr->bld', dt, W_dt) + b_dt)
            A = -jnp.exp(A_raw)

            def step(h, inp):
                x_t, dlt, B_t, C_t = inp
                dA = jnp.exp(dlt[:, None, :] * A[None])
                h = dA * h + dlt[:, None, :] * B_t[:, :, None] * x_t[:, None, :]
                y_t = jnp.einsum('bn,bnd->bd', C_t, h) + D * x_t
                return (h, y_t)
            h0 = jnp.zeros((b, d_state, d_inner), x.dtype)
            xs = (xc.transpose(1, 0, 2), delta.transpose(1, 0, 2), B.transpose(1, 0, 2), C.transpose(1, 0, 2))
            _, ys = jax.lax.scan(step, h0, xs)
            y = ys.transpose(1, 0, 2) * jax.nn.silu(z)
            return jnp.einsum('bld,md->blm', y, W_out)
        return _mamba_fwd(x, W_in, conv_w, conv_b, W_x, W_dt, b_dt, A_raw, D, W_out)

    def _L0_cond2_ref(x, subject_id, weight, bias):
        import jax, jax.numpy as jnp
        import numpy as np
        S, O, H = (8, 256, 256)
        B, N = (32, 128)
        W = weight[subject_id]
        b = bias[subject_id]
        y = jnp.einsum('bnh,boh->bno', x, W) + b[:, None, :]
        return y

    def _L0_ffn_ref(x, Wg, bg, W1, b1, W2, b2):
        import jax, jax.numpy as jnp
        import numpy as np
        B, S, D, H, E, K = (4, 512, 256, 512, 8, 2)
        TEMP = 5.0
        EPS = 1e-09
        logits = jnp.einsum('bsd,de->bse', x, Wg) + bg
        probs = jax.nn.softmax(logits / TEMP, axis=-1)
        vals, idx = jax.lax.top_k(probs, K)
        onehot = jax.nn.one_hot(idx, E, dtype=x.dtype)
        mask = jnp.einsum('bske,bsk->bse', onehot, vals)
        gates = mask / (jnp.sum(mask, axis=-1, keepdims=True) + EPS)
        h = jax.nn.gelu(jnp.einsum('bsd,edh->besh', x, W1) + b1[None, :, None, :], approximate=False)
        out = jnp.einsum('besh,ehd->besd', h, W2) + b2[None, :, None, :]
        y = jnp.einsum('bse,besd->bsd', gates, out)
        return y

    def _L1_cond_ref(hidden_states, expert_ids, wi, wo, common_wi_a, common_wi_b, common_wo_a, common_wo_b, experts_wi_a, experts_wi_b, experts_wo_a, experts_wo_b):
        import jax, jax.numpy as jnp
        import numpy as np
        B, S, D, F = (32, 128, 256, 1024)
        R_COMMON, R_DOMAIN, E = (16, 16, 8)
        ALPHA = 2.0

        def _expert_lora(x, expert_ids, Wa, Wb):
            Ab = Wa[expert_ids]
            Bb = Wb[expert_ids]
            low = jnp.einsum('bsd,brd->bsr', x, Ab)
            return ALPHA * jnp.einsum('bsr,bor->bso', low, Bb)
        x = hidden_states
        hidden_i = jnp.einsum('bsd,fd->bsf', x, wi)
        hidden_i += ALPHA * jnp.einsum('bsr,fr->bsf', jnp.einsum('bsd,rd->bsr', x, common_wi_a), common_wi_b)
        hidden_i += _expert_lora(x, expert_ids, experts_wi_a, experts_wi_b)
        hidden_i = jax.nn.relu(hidden_i)
        hidden_o = jnp.einsum('bsf,df->bsd', hidden_i, wo)
        hidden_o += ALPHA * jnp.einsum('bsr,dr->bsd', jnp.einsum('bsf,rf->bsr', hidden_i, common_wo_a), common_wo_b)
        hidden_o += _expert_lora(hidden_i, expert_ids, experts_wo_a, experts_wo_b)
        return hidden_o

    def _L1_attn_ref(x, Wq, Wk, Wv):
        import jax, jax.numpy as jnp
        import numpy as np
        B, N = (2, 512)
        H, R = (8, 64)
        IN_DIM, OUT_DIM = (128, 128)
        D = IN_DIM + OUT_DIM
        INIT = 1.0
        b, n, d = x.shape
        Q = (x @ Wq.T).reshape(b, n, H, R)
        K = (x @ Wk.T).reshape(b, n, H, R)
        V = (x @ Wv.T).reshape(b, n, H, d)
        attn = jnp.einsum('bnhr,bmhr->bhnm', Q, K)
        attn = jax.nn.softmax(attn, axis=-1)
        out = jnp.einsum('bhnm,bmhd->bnd', attn, V)
        return out

    def _L1_cond2_ref(hidden, profile_ids, down_w, down_b, up_w, up_b, ln_g, ln_b):
        import jax, jax.numpy as jnp
        import numpy as np
        N_PROFILES = 8
        HIDDEN = 256
        BOTTLENECK = 128
        EPS = 1e-05
        Wd = down_w[profile_ids]
        bd = down_b[profile_ids][:, None]
        Wu = up_w[profile_ids]
        bu = up_b[profile_ids][:, None]
        g = ln_g[profile_ids][:, None]
        b = ln_b[profile_ids][:, None]
        z = jax.nn.relu(jnp.einsum('bsh,bhk->bsk', hidden, Wd) + bd)
        y = hidden + jnp.einsum('bsk,bkh->bsh', z, Wu) + bu
        mu = jnp.mean(y, axis=-1, keepdims=True)
        var = jnp.mean(jnp.square(y - mu), axis=-1, keepdims=True)
        return (y - mu) * jax.lax.rsqrt(var + EPS) * g + b

    def _L1_ffn_ref(x, Wg, W1, W2, W3, Ws1, Ws2, Ws3):
        import jax, jax.numpy as jnp
        import numpy as np
        TOP_K = 4
        CAP_FACTOR = 4

        def swiglu(x, w1, w2, w3):
            return jax.nn.silu(x @ w1) * (x @ w3) @ w2
        B, S, D = x.shape
        E = Wg.shape[1]
        T = B * S
        xf = x.reshape(T, D)
        scores = jax.nn.softmax(xf @ Wg, axis=-1)
        weights, indices = jax.lax.top_k(scores, TOP_K)
        P = T * TOP_K
        pair_expert = indices.reshape(-1)
        pair_token = jnp.repeat(jnp.arange(T), TOP_K)
        pair_weight = weights.reshape(-1).astype(xf.dtype)
        C = CAP_FACTOR * P // E
        y = jnp.zeros_like(xf)
        for e in range(E):
            pos = jnp.nonzero(pair_expert == e, size=C, fill_value=P)[0]
            valid = pos < P
            safe = jnp.minimum(pos, P - 1)
            tok = jnp.where(valid, pair_token[safe], 0)
            w = jnp.where(valid, pair_weight[safe], 0.0)
            xg = xf[tok]
            out = swiglu(xg, W1[e], W2[e], W3[e]) * w[:, None]
            y = y.at[tok].add(out)
        z = swiglu(xf, Ws1, Ws2, Ws3)
        return (y + z).reshape(B, S, D)
    x = x + _L0_attn_ref(_L0_cond_ref(x, L0_cond_tau_ctx, condB_tauraws, L0_cond_Wg, L0_cond_bg, L0_cond_Wn1, L0_cond_bn1, cond_256, condB_bn2, cond_1024, L0_cond_Wsoma, L0_cond_bsoma, L0_cond_Wtemp, L0_cond_btemp, L0_cond_Wout, L0_cond_gamma, L0_cond_beta), L0_attn_W_in, L0_attn_conv_w, L0_attn_conv_b, L0_attn_W_x, L0_attn_W_dt, L0_attn_b_dt, L0_attn_A_raw, L0_attn_D, L0_attn_W_out)
    x = x + _L0_ffn_ref(_L0_cond2_ref(x, itok_B_0_7, L0_cond2_weight, L0_cond2_bias), L0_ffn_Wg, L0_ffn_bg, L0_ffn_W1, L0_ffn_b1, L0_ffn_W2, L0_ffn_b2)
    x = x + _L1_attn_ref(_L1_cond_ref(x, itok_B_0_7, L1_cond_wi, L1_cond_wo, L1_cond_common_wi_a, L1_cond_common_wi_b, L1_cond_common_wo_a, L1_cond_common_wo_b, L1_cond_experts_wi_a, L1_cond_experts_wi_b, L1_cond_experts_wo_a, L1_cond_experts_wo_b), L1_attn_Wq, L1_attn_Wk, L1_attn_Wv)
    x = x + _L1_ffn_ref(_L1_cond2_ref(x, itok_B_0_6, L1_cond2_down_w, L1_cond2_down_b, L1_cond2_up_w, L1_cond2_up_b, L1_cond2_ln_g, L1_cond2_ln_b), L1_ffn_Wg, L1_ffn_W1, L1_ffn_W2, L1_ffn_W3, L1_ffn_Ws1, L1_ffn_Ws2, L1_ffn_Ws3)
    return x

_drawn_inputs = setup_inputs


def setup_inputs(seed=0):
    import zlib

    import numpy as np

    out = dict(_drawn_inputs(seed))
    spreads = {'condB_bn2': (0.0, 2.0),
     'L0_cond_bg': (-0.5, 0.6),
     'L0_cond_bn1': (0.0, 2.0),
     'L0_cond_bsoma': (0.0, 0.1),
     'L0_cond_btemp': (0.0, 0.268),
     'L0_cond_gamma': (1.0, 0.2),
     'L0_cond_beta': (0.0, 0.1),
     'L0_ffn_bg': (0.0, 0.1),
     'L0_ffn_b1': (0.0, 0.401),
     'L0_ffn_b2': (0.0, 0.1),
     'L1_cond2_ln_g': (1.0, 0.2),
     'L1_cond2_ln_b': (0.0, 0.1)}
    factors = {'condB_tauraws': 8.0,
     'cond_256': 8.0,
     'cond_1024': 29.51,
     'L0_cond_Wn1': 8.0,
     'L0_attn_conv_b': 5.866,
     'L0_cond2_bias': 3.169,
     'L1_cond2_down_b': 8.0,
     'L1_cond2_up_b': 7.422}
    for name, (base, spread) in spreads.items():
        noise = np.random.default_rng([zlib.crc32(name.encode()), seed]).standard_normal(out[name].shape)
        drawn = base * np.exp(spread * noise) if base else spread * noise
        out[name] = jnp.asarray(drawn.astype(out[name].dtype))
    for name, factor in factors.items():
        out[name] = (out[name] * factor).astype(out[name].dtype)
    return out
```

```python
from contextlib import ExitStack

import numpy as np

import concourse.bass as bass
from concourse import mybir

F32 = mybir.dt.float32
BF16 = mybir.dt.bfloat16
I32 = mybir.dt.int32
ALU = mybir.AluOpType
ACT = mybir.ActivationFunctionType
X = mybir.AxisListType.X

P = 128
B = 8
T = 512
TT = T // P
D = 256
DC = D // P
NTR = 8
HN = 64
DI = 512
JI = DI // P
NS = 16
DTR = 64
E0, K0, H0 = 8, 2, 512
JH = H0 // P
FF = 1024
JF = FF // P
R = 16
NH, RH = 8, 64
E1, K1, H1 = 32, 4, 128
ES = 2
CAP = 4 * (B * T * K1) // E1
NW0, NW1 = 3, 6
EPS = 1e-5
GATE_EPS = 1e-9
TEMP = 5.0


class Chain:

    def __init__(self, eng, sem):
        self.eng, self.sem, self.n = eng, sem, 0

    def step(self, ins):
        ins.then_inc(self.sem, 1)
        self.n += 1

    def all_but(self, k):
        if self.n > k:
            self.eng.wait_ge(self.sem, self.n - k)

    def link(self, ins):
        self.step(ins)
        self.eng.wait_ge(self.sem, self.n)


def build(nc, a, out):
    with ExitStack() as ctx:
        def sb(name, shape, dt=F32, scope=ctx):
            return scope.enter_context(nc.sbuf_tensor(name, shape, dt))

        sems = []

        def sem(name):
            s = ctx.enter_context(nc.semaphore(name))
            sems.append(s)
            return s

        ps = ctx.enter_context(nc.psum_tensor("ps", [P, 8, 512], F32))

        Wg = sb("Wg", [P, 4, D])
        Wn1 = sb("Wn1", [P, DC, HN])
        Wn2 = sb("Wn2", [P, NTR])
        Wn2r = sb("Wn2r", [P, NTR, P])
        Wsoma = sb("Wsoma", [P, DC, D])
        Wtemp = sb("Wtemp", [P, DC, D])
        WoutC = sb("WoutC", [P, DC, D])
        Win = sb("Win", [P, DC, 2 * DI])
        Wxd = sb("Wxd", [P, JI, DTR])
        Wxbc = sb("Wxbc", [P, JI, 3, 2 * NS])
        Wdt = sb("Wdt", [P, DI])
        Wo = sb("Wo", [P, JI, D])
        wi = sb("wi", [P, DC, FF])
        wo = sb("wo", [P, JF, D])
        Ai = sb("Ai", [P, DC, 2 * R])
        Bi = sb("Bi", [P, FF])
        Ao = sb("Ao", [P, JF, 2 * R])
        Bo = sb("Bo", [P, D])
        Wg0 = sb("Wg0", [P, DC, E0])
        Wg1 = sb("Wg1", [P, DC, E1])
        b2p = sb("b2p", [P, D])
        b1e = sb("b1e", [P, E0, JH])
        bg0 = sb("bg0", [P, E0])
        vec = sb("vec", [P, 11 + 3 * JI])
        bg, bsoma, btemp, gamma, beta = (vec[:, 2 * i:2 * i + 2] for i in range(5))
        bn1 = vec[:, 10:11]
        convb, bdt, Dv = (vec[:, 11 + JI * i:11 + JI * (i + 1)] for i in range(3))
        cw = sb("cw", [P, JI, 4])
        An = sb("An", [P, JI, NS])
        tau = sb("tau", [P, NTR + 1])
        alpha = sb("alpha", [P, NTR + 1])
        bn2 = sb("bn2", [P, NTR])
        blend = sb("blend", [P, DC, NTR])
        bl1 = sb("bl1", [P, DC])
        epst = sb("epst", [P, 1])
        ident = sb("ident", [P, P])
        ones = sb("ones", [P, P])
        mean = sb("mean", [P, P])
        tri = sb("tri", [P, P])
        sel = sb("sel", [96, 2 * NS, P], BF16)
        h1 = sb("h1", [P, T])
        dts = sb("dts", [P, T])
        gT = sb("gT", [P, T])
        low = sb("low", [P, 2, T])
        carry = sb("carry", [P, E1])
        wgt = sb("wgt", [P, TT, E1 + ES])
        x = sb("x", [P, DC, T])
        y = sb("y", [P, DC, T])
        ids = sb("ids", [1, 2], I32)

        ld = sem("weights_loaded")
        masks = sem("masks_made")
        su = sem("setup_step")
        exps = sem("setup_exps")
        loads = [(Wg, "Wg"), (Wn1, "Wn1"), (Wsoma, "Wsoma"), (Wtemp, "Wtemp"), (WoutC, "Wout"), (Win, "Win"),
                 (Wxd, "Wxd"), (Wxbc[:, :, 0, :], "Wxbc"), (Wo, "Wo"), (wi, "wi"), (wo, "wo"),
                 (Ai[:, :, 0:R], "Aic"), (Ao[:, :, 0:R], "Aoc"), (Wg0, "Wg0"),
                 (Wg1, "Wg1"), (b1e, "b1e"), (vec, "vec"), (cw, "cw"), (An, "Araw"), (blend, "blend")]
        with nc.Block() as block:
            zeroed = ((Wn2, 0.0), (Wdt, 0.0), (Bi, 0.0), (Bo, 0.0), (b2p, 0.0), (h1, 0.0), (dts, 0.0),
                      (gT, 0.0), (low, 0.0), (carry, 0.0), (wgt, 1.0), (epst, EPS), (ones, 1.0), (mean, 1.0 / D))

            @block.gpsimd
            def _(pool):
                for t, v in zeroed:
                    pool.memset(t[:], v).then_inc(masks, 1)
                pool.memset(ident[:, :], 0.0).then_inc(masks, 1)
                pool.memset(tri[:, :], 1.0).then_inc(masks, 1)
                pool.memset(sel[:, :, :], 0.0).then_inc(masks, 1)
                n = len(zeroed) + 3
                pool.wait_ge(masks, n)
                pool.affine_select(out=ident[:, :], in_=ident[:, :], compare_op=ALU.not_equal, fill=1.0,
                                   base=0, pattern=[[-1, P]], channel_multiplier=1).then_inc(masks, 1)
                pool.affine_select(out=tri[:, :], in_=tri[:, :], compare_op=ALU.is_ge, fill=0.0,
                                   base=0, pattern=[[1, P]], channel_multiplier=-1).then_inc(masks, 1)
                n += 2
                for g in range(3):
                    pool.affine_select(out=sel[:, :, :], in_=sel[:, :, :], compare_op=ALU.not_equal, fill=1.0,
                                       base=-32 * g, pattern=[[-1, 2 * NS], [0, P]],
                                       channel_multiplier=1).then_inc(masks, 1)
                    n += 1
                    pool.wait_ge(masks, n)

            @block.sync
            def _(sp):
                for t, name in loads:
                    dst = t if isinstance(t, bass.AP) else t[:]
                    sp.dma_start(dst, a[name]).then_inc(ld, 16)
                sp.dma_start(tau[:, 0:NTR], a["tau"].partition_broadcast(P)).then_inc(ld, 16)
                sp.dma_start(tau[:, NTR:NTR + 1], a["tau_ctx"].partition_broadcast(P)).then_inc(ld, 16)
                sp.dma_start(bn2[:, :], a["bn2"].partition_broadcast(P)).then_inc(ld, 16)
                sp.dma_start(bg0[:, :], a["bg0"].partition_broadcast(P)).then_inc(ld, 16)
                sp.wait_ge(masks, len(zeroed))
                sp.dma_start(Wn2[0:HN, :], a["Wn2"]).then_inc(ld, 16)
                sp.dma_start(Wdt[0:DTR, :], a["Wdt"]).then_inc(ld, 16)
                sp.dma_start(Bi[0:R, :], a["Bic"]).then_inc(ld, 16)
                sp.dma_start(Bo[0:R, :], a["Boc"]).then_inc(ld, 16)
                sp.dma_start(b2p[0:E0, :], a["b2"]).then_inc(ld, 16)
                sp.wait_ge(ld, 16 * (len(loads) + 9))

            @block.scalar
            def _(act):
                act.wait_ge(ld, 16 * (len(loads) + 9))
                act.wait_ge(exps, 1)
                act.activation(alpha[:, :], tau[:, :], ACT.Exp).then_inc(exps, 1)
                act.activation(An[:, :, :], An[:, :, :], ACT.Exp).then_inc(exps, 1)
                act.wait_ge(exps, 4)
                act.activation(blend[:, :, :], blend[:, :, :], ACT.Exp).then_inc(exps, 1)

            @block.vector
            def _(dve):
                ch = Chain(dve, su)
                dve.wait_ge(ld, 16 * (len(loads) + 9))
                dve.tensor_scalar(tau[:, :], tau[:, :], 87.0, None, ALU.min).then_inc(exps, 1)
                for k in (1, 2):
                    ch.step(dve.tensor_copy(Wxbc[:, :, k, :], Wxbc[:, :, 0, :]))
                ch.step(dve.tensor_copy(Wn2r[:, :, :], Wn2[:, :].unsqueeze(2).to_broadcast([P, NTR, P])))
                ch.link(dve.tensor_reduce(bl1[:, :], WoutC[:, :, :], X, ALU.add))
                ch.link(dve.tensor_scalar(bl1[:, :], bl1[:, :], 1.0 / D, None, ALU.mult))
                for j in range(DC):
                    ch.link(dve.tensor_scalar(WoutC[:, j, :], WoutC[:, j, :], bl1[:, j:j + 1], None, ALU.subtract))
                ch.link(dve.tensor_reduce(bl1[:, :], blend[:, :, :], X, ALU.max))
                dve.wait_ge(exps, 3)
                dve.tensor_tensor(blend[:, :, :], blend[:, :, :], bl1[:, :].unsqueeze(2).to_broadcast([P, DC, NTR]),
                                  ALU.subtract).then_inc(exps, 1)
                ch.link(dve.tensor_scalar(alpha[:, :], alpha[:, :], 1.0, None, ALU.add))
                ch.link(dve.reciprocal(alpha[:, :], alpha[:, :]))
                ch.link(dve.tensor_scalar(An[:, :, :], An[:, :, :], -1.0, None, ALU.mult))
                dve.wait_ge(exps, 5)
                ch.link(dve.tensor_reduce(bl1[:, :], blend[:, :, :], X, ALU.add))
                ch.link(dve.reciprocal(bl1[:, :], bl1[:, :]))
                ch.link(dve.tensor_tensor(blend[:, :, :], blend[:, :, :],
                                          bl1[:, :].unsqueeze(2).to_broadcast([P, DC, NTR]), ALU.mult))


        SETUP_SEMS = len(sems)
        c_in = sem("cond_x_loaded")
        c_ctx = sem("cond_context_ready")
        c_h1, c_soma, c_gate, c_mod, c_tg, c_out, c_var = (
            sem("cond_" + n) for n in ("hidden_product", "soma_product", "gate_product", "mod_product",
                                       "temporal_product", "out_product", "variance_product"))
        c_act = sem("cond_act_step")
        c_dve = sem("cond_dve_step")
        c_tempo = sem("cond_temporal_ready")
        c_sg = sem("cond_soma_gated")
        m_xz, m_dt, m_bc, m_dl = (sem("mix_" + n) for n in ("in_product", "dt_product", "bc_product", "delta_product"))
        m_act = sem("mix_act_step")
        m_dve = sem("mix_dve_step")
        m_conv = sem("mix_conv_ready")
        m_split = sem("mix_bc_split")
        s_b, s_c = sem("scan_b_spread"), sem("scan_c_spread")
        s_cc = sem("scan_c_copied")
        s_da = sem("scan_decay_ready")
        s_bm, s_h = sem("scan_input_ready"), sem("scan_state_ready")
        s_pd, s_pp = sem("scan_product_dve"), sem("scan_product_pool")
        s_acc = sem("scan_accumulated")
        s_y = sem("scan_y_ready")
        s_yd = sem("scan_y_step")
        s_o = sem("scan_out_product")
        f_id, f_w = sem("f_subject_loaded"), sem("f_subject_weights")
        f_e = [sem(f"f_expert_weights_{i}") for i in range(NW0)]
        f_y, f_ya = sem("f_y_product"), sem("f_y_ready")
        f_lg, f_st, f_ex, f_gt = sem("f_logits"), sem("f_gate_step"), sem("f_gate_exp"), sem("f_gates_turned")
        f_gc, f_b2, f_yi = sem("f_gates_copied"), sem("f_bias_product"), sem("f_sum_started")
        f_up, f_g, f_dn, f_acc, f_tr = (sem("f_" + n) for n in ("up", "gelu", "down", "accumulated", "turned"))
        l_w, l_lo, l_lc, l_h, l_r = (sem("l_" + n) for n in ("lora_loaded", "low_product", "low_copied", "hidden_product",
                                                             "hidden_relu"))
        l_o, l_oc = sem("l_out_product"), sem("l_out_copied")
        a_pj, a_ea, a_ev = sem("a_projected"), sem("a_copied_act"), sem("a_copied_dve")
        a_s, a_mx, a_ex, a_nm, a_st = (sem("a_" + n) for n in ("scores", "maxima", "exps", "normalised", "dve_step"))
        a_tp, a_ta, a_td, a_pv = (sem("a_" + n) for n in ("probs_turned", "turned_copied_act", "turned_copied_dve",
                                                          "values_summed"))
        d_id, d_w, d_z, d_za, d_u, d_y = (sem("d_" + n) for n in ("profile_loaded", "weights", "down_product", "relu",
                                                                 "up_product", "sum_ready"))
        d_mn, d_yc, d_sq, d_var, d_sd, d_st = (sem("d_" + n) for n in ("mean", "centred", "squares", "variance",
                                                                      "deviation", "dve_step"))
        g_e = [sem(f"g_expert_weights_{i}") for i in range(NW1)]
        g_lg, g_st, g_ex = (sem("g_" + n) for n in ("logits", "gate_step", "gate_exp"))
        g_sel, g_cum = sem("g_selected"), sem("g_counted")
        g_up, g_si, g_hh, g_dn, g_acc, g_tr = (sem("g_" + n) for n in ("up", "silu", "hidden", "down", "accumulated",
                                                                     "turned"))
        g_o, g_out = sem("g_out_ready"), sem("g_out_stored")

        def product(pe, dst, pairs, done=None):
            for i, (lhsT, rhs) in enumerate(pairs):
                last = pe.matmul(dst, lhsT, rhs, start=(i == 0), stop=(i == len(pairs) - 1))
            if done is not None:
                last.then_inc(done, 1)

        def choose(dve, act, ch, gate_exp, logits, probs, tmp, srt, small, E, K, scale):
            def wide(t):
                return t.unsqueeze(2).to_broadcast([P, TT, E])
            ch.link(dve.tensor_reduce(small[:, 0, :], logits, X, ALU.max))
            dve.tensor_tensor(probs, logits, wide(small[:, 0, :]), ALU.subtract).then_inc(gate_exp, 1)
            dve.wait_ge(gate_exp, 2)
            ch.link(dve.tensor_reduce(small[:, 1, :], probs, X, ALU.add))
            ch.link(dve.reciprocal(small[:, 1, :], small[:, 1, :]))
            ch.link(dve.tensor_tensor(probs, probs, wide(small[:, 1, :]), ALU.mult))
            for t in range(TT):
                ch.step(dve.max(srt[:, t, :], probs[:, t, :]))
            ch.all_but(0)
            kth = srt[:, :, K - 1:K].to_broadcast([P, TT, E])
            ch.link(dve.tensor_tensor(tmp[:, 0], probs, kth, ALU.is_gt))
            ch.link(dve.tensor_tensor(tmp[:, 1], probs, kth, ALU.is_equal))
            ch.link(dve.tensor_reduce(small[:, 2, :], tmp[:, 0], X, ALU.add))
            for t in range(TT):
                ch.step(dve.tensor_tensor_scan(tmp[:, 2, t, :], tmp[:, 1, t, :], tmp[:, 1, t, :], 0.0,
                                               ALU.add, ALU.max))
            ch.all_but(0)

        def conditioner(b):
            with ExitStack() as st:
                cx = sb("cx", [P, DC, T], scope=st)
                soma = sb("soma", [P, DC, T], scope=st)
                wg = sb("wg", [P, DC, T], scope=st)
                gated = sb("gated", [P, DC, T], scope=st)
                mod = sb("mod", [P, NTR, T], scope=st)
                gm = sb("gm", [P, DC, T], scope=st)
                tr = sb("tr", [P, DC, T], scope=st)
                tempo = sb("tempo", [P, DC, T], scope=st)
                tg = sb("tg", [P, DC, T], scope=st)
                sg = sb("sg", [P, DC, T], scope=st)
                sq = sb("sq", [P, DC, T], scope=st)
                std = sb("std", [P, T], scope=st)
                rstd = sb("rstd", [P, T], scope=st)
                MODB = [5, 6, 7, 0]
                with nc.Block() as block:
                    @block.sync
                    def _(sp):
                        sp.dma_start(x[:, :, :], a["x"][b]).then_inc(c_in, 16)

                    @block.tensor
                    def _(pe):
                        pe.wait_ge(c_in, 16)
                        product(pe, ps[0:HN, 0, :], [(Wn1[:, k, :], x[:, k, :]) for k in range(DC)], c_h1)
                        for j in range(DC):
                            product(pe, ps[:, 1 + j, :], [(Wsoma[:, k, j * P:(j + 1) * P], x[:, k, :])
                                                          for k in range(DC)], c_soma)
                        pe.wait_ge(c_ctx, DC)
                        for j in range(DC):
                            product(pe, ps[:, 3 + j, :],
                                    [(Wg[:, k, j * P:(j + 1) * P], x[:, k, :]) for k in range(DC)]
                                    + [(Wg[:, DC + k, j * P:(j + 1) * P], cx[:, k, :]) for k in range(DC)], c_gate)
                        pe.wait_ge(c_act, 1)
                        for d in range(NTR):
                            if d >= 4:
                                pe.wait_ge(c_act, 5 + d - 3)
                            product(pe, ps[:, MODB[d % 4], :], [(Wn2r[:, d, :], h1[:, :])], c_mod)
                        pe.wait_ge(c_tempo, DC)
                        for j in range(DC):
                            product(pe, ps[:, 1 + j, :], [(Wtemp[:, k, j * P:(j + 1) * P], tempo[:, k, :])
                                                          for k in range(DC)], c_tg)
                        pe.wait_ge(c_sg, DC)
                        for j in range(DC):
                            product(pe, ps[:, 3 + j, :], [(WoutC[:, k, j * P:(j + 1) * P], sg[:, k, :])
                                                          for k in range(DC)], c_out)
                        pe.wait_ge(c_act, 5 + NTR + DC + DC)
                        product(pe, ps[:, 5, :], [(mean[:, :], sq[:, k, :]) for k in range(DC)], c_var)

                    @block.scalar
                    def _(act):
                        act.wait_ge(c_h1, 1)
                        act.activation(h1[0:HN, :], ps[0:HN, 0, :], ACT.Gelu, bias=bn1[0:HN, :]).then_inc(c_act, 1)
                        for j in range(DC):
                            act.wait_ge(c_soma, j + 1)
                            act.activation(soma[:, j, :], ps[:, 1 + j, :], ACT.Gelu,
                                           bias=bsoma[:, j:j + 1]).then_inc(c_act, 1)
                        for j in range(DC):
                            act.wait_ge(c_gate, j + 1)
                            act.activation(wg[:, j, :], ps[:, 3 + j, :], ACT.Sigmoid,
                                           bias=bg[:, j:j + 1]).then_inc(c_act, 1)
                        for d in range(NTR):
                            act.wait_ge(c_mod, d + 1)
                            act.activation(mod[:, d, :], ps[:, MODB[d % 4], :], ACT.Sigmoid,
                                           bias=bn2[:, d:d + 1]).then_inc(c_act, 1)
                        for j in range(DC):
                            act.wait_ge(c_tg, j + 1)
                            act.activation(tg[:, j, :], ps[:, 1 + j, :], ACT.Sigmoid,
                                           bias=btemp[:, j:j + 1]).then_inc(c_act, 1)
                        for j in range(DC):
                            act.wait_ge(c_out, j + 1)
                            act.activation(sq[:, j, :], ps[:, 3 + j, :], ACT.Square).then_inc(c_act, 1)
                        act.wait_ge(c_var, 1)
                        act.activation(std[:, :], ps[:, 5, :], ACT.Sqrt, bias=epst[:, :]).then_inc(c_act, 1)

                    @block.vector
                    def _(dve):
                        ch = Chain(dve, c_dve)
                        dve.wait_ge(c_in, 16)
                        for j in range(DC):
                            dve.tensor_tensor_scan(cx[:, j, :], alpha[:, NTR:NTR + 1].to_broadcast([P, T]), x[:, j, :],
                                                   0.0, ALU.mult, ALU.add).then_inc(c_ctx, 1)
                        dve.wait_ge(c_act, 3 + DC)
                        for j in range(DC):
                            ch.step(dve.tensor_tensor(gated[:, j, :], x[:, j, :], wg[:, j, :], ALU.mult))
                        for d in range(NTR):
                            dve.wait_ge(c_act, 5 + d + 1)
                            for j in range(DC):
                                ch.all_but(1)
                                ch.step(dve.scalar_tensor_tensor(out=gm[:, j, :], in0=mod[:, d, :], scalar=0.5,
                                                                 in1=gated[:, j, :], op0=ALU.add, op1=ALU.mult))
                            for j in range(DC):
                                ch.all_but(1)
                                ch.step(dve.tensor_tensor_scan(tr[:, j, :], alpha[:, d:d + 1].to_broadcast([P, T]),
                                                               gm[:, j, :], 0.0, ALU.mult, ALU.add))
                            for j in range(DC):
                                ch.all_but(1 if d < NTR - 1 or j == 0 else 0)
                                if d == 0:
                                    ins = dve.tensor_scalar(tempo[:, j, :], tr[:, j, :], blend[:, j, d:d + 1], None,
                                                            ALU.mult)
                                else:
                                    ins = dve.scalar_tensor_tensor(out=tempo[:, j, :], in0=tr[:, j, :],
                                                                   scalar=blend[:, j, d:d + 1], in1=tempo[:, j, :],
                                                                   op0=ALU.mult, op1=ALU.add)
                                if d < NTR - 1:
                                    ch.step(ins)
                                else:
                                    ins.then_inc(c_tempo, 1)
                        for j in range(DC):
                            dve.wait_ge(c_act, 5 + NTR + j + 1)
                            dve.tensor_tensor(sg[:, j, :], soma[:, j, :], tg[:, j, :], ALU.mult).then_inc(c_sg, 1)
                        dve.wait_ge(c_act, 5 + NTR + 2 * DC + 1)
                        ch.link(dve.reciprocal(rstd[:, :], std[:, :]))
                        for j in range(DC):
                            ch.step(dve.scalar_tensor_tensor(out=y[:, j, :], in0=ps[:, 3 + j, :], scalar=gamma[:, j:j + 1],
                                                             in1=rstd[:, :], op0=ALU.mult, op1=ALU.mult))
                        for j in range(DC):
                            ch.all_but(1)
                            ch.step(dve.tensor_scalar(y[:, j, :], y[:, j, :], beta[:, j:j + 1], None, ALU.add))

        def mixer(b):
            with ExitStack() as st:
                xs = sb("xs", [P, JI, T], scope=st)
                sz = sb("sz", [P, JI, T], scope=st)
                dl = sb("dl", [P, JI, T], scope=st)
                u = sb("u", [P, JI, T], scope=st)
                bc = sb("bc", [96, T], BF16, scope=st)
                with ExitStack() as st1:
                    cv = sb("cv", [P, JI, T], scope=st1)
                    r1 = sb("r1", [P, T], scope=st1)
                    pre = sb("pre", [P, JI, T], scope=st1)
                    ab = sb("ab", [P, JI, T], scope=st1)
                    with nc.Block() as block:
                        @block.tensor
                        def _(pe):
                            for j in range(2 * JI):
                                product(pe, ps[:, j, :], [(Win[:, k, j * P:(j + 1) * P], y[:, k, :]) for k in range(DC)],
                                        m_xz)
                            pe.wait_ge(m_act, 3 * JI)
                            product(pe, ps[0:DTR, 0, :], [(Wxd[:, k, :], xs[:, k, :]) for k in range(JI)], m_dt)
                            product(pe, ps[0:96, 1, :], [(Wxbc[:, k, :, :].rearrange("p a b -> p (a b)"), xs[:, k, :])
                                                         for k in range(JI)], m_bc)
                            pe.wait_ge(m_act, 3 * JI + 1)
                            for j in range(JI):
                                product(pe, ps[:, 2 + j, :], [(Wdt[:, j * P:(j + 1) * P], dts[:, :])], m_dl)

                        @block.scalar
                        def _(act):
                            for j in range(JI):
                                act.wait_ge(m_xz, j + 1)
                                act.activation(cv[:, j, :], ps[:, j, :], ACT.Identity, bias=convb[:, j:j + 1],
                                               scale=cw[:, j, 3:4]).then_inc(m_act, 1)
                            for j in range(JI):
                                act.wait_ge(m_xz, JI + j + 1)
                                act.activation(sz[:, j, :], ps[:, JI + j, :], ACT.Silu).then_inc(m_act, 1)
                            for j in range(JI):
                                act.wait_ge(m_conv, j + 1)
                                act.activation(xs[:, j, :], cv[:, j, :], ACT.Silu).then_inc(m_act, 1)
                            act.wait_ge(m_dt, 1)
                            act.activation(dts[0:DTR, :], ps[0:DTR, 0, :], ACT.Copy).then_inc(m_act, 1)
                            act.wait_ge(m_split, 2)
                            act.activation(ab[:, :, :], pre[:, :, :], ACT.Abs).then_inc(m_act, 1)
                            act.wait_ge(m_act, 3 * JI + 2)
                            act.activation(ab[:, :, :], ab[:, :, :], ACT.Exp, scale=-1.0).then_inc(m_act, 1)
                            act.wait_ge(m_act, 3 * JI + 3)
                            act.activation(ab[:, :, :], ab[:, :, :], ACT.Ln, bias=1.0).then_inc(m_act, 1)

                        @block.vector
                        def _(dve):
                            ch = Chain(dve, m_dve)
                            for j0 in range(0, JI, 2):
                                dve.wait_ge(m_act, j0 + 2)
                                for s in (1, 2, 3):
                                    for j in (j0, j0 + 1):
                                        ch.all_but(1 if s < 3 or j == j0 else 0)
                                        ins = dve.scalar_tensor_tensor(
                                            out=cv[:, j, s:T], in0=ps[:, j, 0:T - s], scalar=cw[:, j, 3 - s:4 - s],
                                            in1=cv[:, j, s:T], op0=ALU.mult, op1=ALU.add)
                                        if s < 3:
                                            ch.step(ins)
                                        else:
                                            ins.then_inc(m_conv, 1)
                            dve.wait_ge(m_bc, 1)
                            ch.link(dve.tensor_copy(bc[:, :], ps[0:96, 1, :]))
                            ch.link(dve.tensor_tensor(r1[0:96, :], ps[0:96, 1, :], bc[:, :], ALU.subtract))
                            ch.step(dve.tensor_copy(bc[32:64, :], r1[32:64, :]))
                            ch.link(dve.tensor_copy(bc[64:96, :], r1[64:96, :]))
                            ch.link(dve.tensor_tensor(r1[64:96, :], r1[64:96, :], bc[64:96, :], ALU.subtract))
                            dve.tensor_copy(bc[64:96, :], r1[64:96, :]).then_inc(m_split, 1)
                            for j in range(JI):
                                dve.wait_ge(m_dl, j + 1)
                                ins = dve.tensor_scalar(pre[:, j, :], ps[:, 2 + j, :], bdt[:, j:j + 1], None, ALU.add)
                                if j < JI - 1:
                                    ch.link(ins)
                                else:
                                    ins.then_inc(m_split, 1)
                            dve.wait_ge(m_act, 3 * JI + 4)
                            ch.link(dve.scalar_tensor_tensor(out=dl[:, :, :], in0=pre[:, :, :], scalar=0.0,
                                                             in1=ab[:, :, :], op0=ALU.max, op1=ALU.add))
                            ch.step(dve.tensor_tensor(u[:, :, :], dl[:, :, :], xs[:, :, :], ALU.mult))
                with ExitStack() as st2:
                    dA = sb("dA", [P, 2, JI, T], scope=st2)
                    ub = sb("ub", [P, 2, JI, T], scope=st2)
                    hs = sb("hs", [P, 2, JI, T], scope=st2)
                    pr = sb("pr", [P, 2, JI, T], scope=st2)
                    cb = sb("cb", [P, 2, T], scope=st2)
                    JD = 1

                    with nc.Block() as block:
                        @block.tensor
                        def _(pe):
                            def spread(n):
                                if n >= 2:
                                    pe.wait_ge(s_bm, n - 1)
                                pe.matmul(ps[:, 4 + n % 2, :], sel[:, n, :], bc[:, :], start=True,
                                          stop=True).then_inc(s_b, 1)
                                if n >= 2:
                                    pe.wait_ge(s_cc, n - 1)
                                pe.matmul(ps[:, 6 + n % 2, :], sel[:, NS + n, :], bc[:, :], start=True,
                                          stop=True).then_inc(s_c, 1)

                            def add_up(n):
                                pe.wait_ge(s_pd, n + 1)
                                for j in range(JI):
                                    if j == JD:
                                        pe.wait_ge(s_pp, n + 1)
                                    ins = pe.matmul(ps[:, j, :], ident[:, :], pr[:, n % 2, j, :],
                                                    start=(n == 0), stop=(n == NS - 1))
                                ins.then_inc(s_acc, 1)

                            spread(0)
                            spread(1)
                            for n in range(NS):
                                if n + 2 < NS:
                                    spread(n + 2)
                                add_up(n)
                            pe.wait_ge(s_y, JI)
                            for j in range(DC):
                                product(pe, ps[:, 4 + j, :], [(Wo[:, k, j * P:(j + 1) * P], u[:, k, :])
                                                              for k in range(JI)], s_o)

                        @block.scalar
                        def _(act):
                            for n in range(NS):
                                if n >= 2:
                                    act.wait_ge(s_h, n - 1)
                                for j in range(JI):
                                    act.activation(dA[:, n % 2, j, :], dl[:, j, :], ACT.Exp,
                                                   scale=An[:, j, n:n + 1]).then_inc(s_da, 1)
                                act.wait_ge(s_c, n + 1)
                                if n >= 2:
                                    act.wait_ge(s_pd, n - 1)
                                    act.wait_ge(s_pp, n - 1)
                                act.activation(cb[:, n % 2, :], ps[:, 6 + n % 2, :], ACT.Copy).then_inc(s_cc, 1)

                        @block.vector
                        def _(dve):
                            def into(n):
                                dve.wait_ge(s_b, n + 1)
                                if n >= 2:
                                    dve.wait_ge(s_h, n - 1)
                                dve.tensor_tensor(ub[:, n % 2], u[:, :, :],
                                                  ps[:, 4 + n % 2, :].unsqueeze(1).to_broadcast([P, JI, T]),
                                                  ALU.mult).then_inc(s_bm, 1)

                            def scan(n):
                                dve.wait_ge(s_da, JI * (n + 1))
                                dve.wait_ge(s_bm, n + 1)
                                if n >= 2:
                                    dve.wait_ge(s_pd, n - 1)
                                    dve.wait_ge(s_pp, n - 1)
                                for j in range(JI):
                                    ins = dve.tensor_tensor_scan(hs[:, n % 2, j, :], dA[:, n % 2, j, :],
                                                                 ub[:, n % 2, j, :], 0.0, ALU.mult, ALU.add)
                                ins.then_inc(s_h, 1)

                            def out(n):
                                dve.wait_ge(s_h, n + 1)
                                dve.wait_ge(s_cc, n + 1)
                                if n >= 2:
                                    dve.wait_ge(s_acc, n - 1)
                                dve.tensor_tensor(pr[:, n % 2, 0:JD, :], hs[:, n % 2, 0:JD, :],
                                                  cb[:, n % 2, :].unsqueeze(1).to_broadcast([P, JD, T]),
                                                  ALU.mult).then_inc(s_pd, 1)

                            into(0)
                            for n in range(NS):
                                if n + 1 < NS:
                                    into(n + 1)
                                scan(n)
                                if n >= 1:
                                    out(n - 1)
                            out(NS - 1)
                            dve.wait_ge(s_acc, NS)
                            ch = Chain(dve, s_yd)
                            for j in range(JI):
                                ch.step(dve.scalar_tensor_tensor(out=ub[:, 0, j, :], in0=xs[:, j, :],
                                                                 scalar=Dv[:, j:j + 1], in1=ps[:, j, :],
                                                                 op0=ALU.mult, op1=ALU.add))
                            dve.wait_ge(s_bm, NS)
                            for j in range(JI):
                                dve.wait_ge(s_yd, j + 1)
                                dve.tensor_tensor(u[:, j, :], ub[:, 0, j, :], sz[:, j, :], ALU.mult).then_inc(s_y, 1)
                            for j in range(DC):
                                dve.wait_ge(s_o, j + 1)
                                ch.step(dve.tensor_tensor(x[:, j, :], x[:, j, :], ps[:, 4 + j, :], ALU.add))

                        @block.gpsimd
                        def _(pool):
                            for n in range(NS):
                                pool.wait_ge(s_h, n + 1)
                                pool.wait_ge(s_cc, n + 1)
                                if n >= 2:
                                    pool.wait_ge(s_acc, n - 1)
                                pool.tensor_tensor(pr[:, n % 2, JD:JI, :], hs[:, n % 2, JD:JI, :],
                                                   cb[:, n % 2, :].unsqueeze(1).to_broadcast([P, JI - JD, T]),
                                                   ALU.mult).then_inc(s_pp, 1)

        def first_mixture(b):
            with ExitStack() as st:
                ws = sb("ws", [P, DC * D + DC], scope=st)
                we = sb("we", [P, NW0, DC * H0 + JH * D], scope=st)
                hid = sb("hid", [P, 2, JH, T], scope=st)
                acc = sb("acc", [P, TT, D], scope=st)
                lg = sb("lg", [P, TT, E0], scope=st)
                pb = sb("pb", [P, TT, E0], scope=st)
                tmp = sb("tmp", [P, 3, TT, E0], scope=st)
                srt = sb("srt", [P, TT, 8], scope=st)
                small = sb("small", [P, 4, TT], scope=st)
                gates = sb("gates", [P, TT, E0], scope=st)
                wsub = ws[:, 0:DC * D].rearrange("p (k m) -> p k m", k=DC)
                bsub = ws[:, DC * D:DC * D + DC]
                w1 = [we[:, i, 0:DC * H0].rearrange("p (k m) -> p k m", k=DC) for i in range(NW0)]
                w2 = [we[:, i, DC * H0:].rearrange("p (k m) -> p k m", k=JH) for i in range(NW0)]

                with nc.Block() as block:
                    @block.sync
                    def _(sp):
                        sp.dma_start(ids[0:1, 0:1], a["subject"][b]).then_inc(f_id, 16)
                        for e in range(NW0):
                            sp.dma_start(we[:, e, :], a["E0"][e]).then_inc(f_e[e % NW0], 16)
                        sp.wait_ge(f_id, 16)
                        subject = sp.value_load(ids[0:1, 0:1], min_val=0, max_val=7)
                        sp.dma_start(ws[:, :], a["Wsub"][subject]).then_inc(f_w, 16)
                        for e in range(NW0, E0):
                            sp.wait_ge(f_dn, TT * (e - NW0 + 1))
                            sp.dma_start(we[:, e % NW0, :], a["E0"][e]).then_inc(f_e[e % NW0], 16)

                    @block.tensor
                    def _(pe):
                        pe.wait_ge(f_w, 16)
                        for j in range(DC):
                            product(pe, ps[:, j, :], [(wsub[:, k, j * P:(j + 1) * P], x[:, k, :]) for k in range(DC)],
                                    f_y)
                        pe.wait_ge(f_ya, DC)
                        for t in range(TT):
                            product(pe, ps[:, 6, t * E0:(t + 1) * E0], [(y[:, k, t * P:(t + 1) * P], Wg0[:, k, :])
                                                                        for k in range(DC)], f_lg)
                        def up(e):
                            pe.wait_ge(f_e[e % NW0], 16 * (e // NW0 + 1))
                            for j in range(JH):
                                if e:
                                    pe.wait_ge(f_g, JH * (e - 1) + j + 1)
                                product(pe, ps[:, j, :], [(w1[e % NW0][:, k, j * P:(j + 1) * P], y[:, k, :])
                                                          for k in range(DC)], f_up)

                        def down(e):
                            o = 4 + 2 * (e % 2)
                            pe.wait_ge(f_g, JH * (e + 1))
                            if e >= 2:
                                pe.wait_ge(f_acc, TT * (e - 1))
                            for t in range(TT):
                                product(pe, ps[:, o + t // 2, (t % 2) * D:(t % 2 + 1) * D],
                                        [(hid[:, e % 2, k, t * P:(t + 1) * P], w2[e % NW0][:, k, :])
                                         for k in range(JH)], f_dn)

                        up(0)
                        pe.wait_ge(f_ex, 3)
                        for t in range(TT):
                            pe.transpose(ps[0:E0, 7, t * P:(t + 1) * P], gates[:, t, :], ident[:, :]).then_inc(f_gt, 1)
                        pe.wait_ge(f_gc, 1)
                        for t in range(TT):
                            product(pe, ps[:, 4 + t // 2, (t % 2) * D:(t % 2 + 1) * D],
                                    [(gT[:, t * P:(t + 1) * P], b2p[:, :])], f_b2)
                        up(1)
                        pe.wait_ge(f_yi, 1)
                        for e in range(E0):
                            if e >= 1 and e + 1 < E0:
                                up(e + 1)
                            down(e)
                        pe.wait_ge(f_acc, TT * E0)
                        for t in range(TT):
                            for j in range(DC):
                                pe.transpose(ps[:, j, t * P:(t + 1) * P], acc[:, t, j * P:(j + 1) * P],
                                             ident[:, :]).then_inc(f_tr, 1)

                    @block.scalar
                    def _(act):
                        for j in range(DC):
                            act.wait_ge(f_y, j + 1)
                            act.activation(y[:, j, :], ps[:, j, :], ACT.Identity, bias=bsub[:, j:j + 1]).then_inc(f_ya, 1)
                        act.wait_ge(f_ex, 1)
                        act.activation(pb[:, :, :], pb[:, :, :], ACT.Exp, scale=1.0 / TEMP).then_inc(f_ex, 1)

                        def gelu(e):
                            for j in range(JH):
                                act.wait_ge(f_up, JH * e + j + 1)
                                if e >= 2:
                                    act.wait_ge(f_dn, TT * (e - 1))
                                act.activation(hid[:, e % 2, j, :], ps[:, j, :], ACT.Gelu,
                                               bias=b1e[:, e, j:j + 1]).then_inc(f_g, 1)
                        gelu(0)
                        act.wait_ge(f_gt, TT)
                        act.activation(gT[0:E0, :], ps[0:E0, 7, :], ACT.Copy).then_inc(f_gc, 1)
                        act.wait_ge(f_b2, TT)
                        act.activation(acc[:, :, :], ps[:, 4:6, :], ACT.Copy).then_inc(f_yi, 1)
                        for e in range(1, E0):
                            gelu(e)

                    @block.vector
                    def _(dve):
                        ch = Chain(dve, f_st)
                        dve.wait_ge(f_lg, TT)
                        ch.link(dve.tensor_tensor(lg[:, :, :],
                                                  ps[:, 6, 0:TT * E0].rearrange("p (t e) -> p t e", t=TT),
                                                  bg0[:, :].unsqueeze(1).to_broadcast([P, TT, E0]), ALU.add))
                        choose(dve, None, ch, f_ex, lg[:, :, :], pb[:, :, :], tmp, srt, small, E0, K0, 1.0 / TEMP)
                        finish_choice(dve, ch, tmp, small, E0, K0)
                        ch.link(dve.tensor_tensor(tmp[:, 0], tmp[:, 0], pb[:, :, :], ALU.mult))
                        ch.link(dve.tensor_reduce(small[:, 3, :], tmp[:, 0], X, ALU.add))
                        ch.link(dve.tensor_scalar(small[:, 3, :], small[:, 3, :], GATE_EPS, None, ALU.add))
                        ch.link(dve.reciprocal(small[:, 3, :], small[:, 3, :]))
                        dve.tensor_tensor(gates[:, :, :], tmp[:, 0],
                                          small[:, 3, :].unsqueeze(2).to_broadcast([P, TT, E0]),
                                          ALU.mult).then_inc(f_ex, 1)
                        dve.wait_ge(f_ex, 3)
                        dve.wait_ge(f_yi, 1)
                        for e in range(E0):
                            o = 4 + 2 * (e % 2)
                            for t in range(TT):
                                dve.wait_ge(f_dn, TT * e + 2 * (t // 2) + 2)
                                if e:
                                    dve.wait_ge(f_acc, TT * (e - 1) + t + 1)
                                dve.scalar_tensor_tensor(out=acc[:, t, :],
                                                         in0=ps[:, o + t // 2, (t % 2) * D:(t % 2 + 1) * D],
                                                         scalar=gates[:, t, e:e + 1], in1=acc[:, t, :],
                                                         op0=ALU.mult, op1=ALU.add).then_inc(f_acc, 1)
                        dve.wait_ge(f_tr, TT * DC)
                        for j in range(DC):
                            ch.step(dve.tensor_tensor(x[:, j, :], x[:, j, :], ps[:, j, :], ALU.add))

        def finish_choice(dve, ch, tmp, small, E, K):
            ch.link(dve.tensor_scalar(small[:, 2, :], small[:, 2, :], -1.0, float(K), ALU.mult, ALU.add))
            ch.link(dve.tensor_tensor(tmp[:, 2], tmp[:, 2], small[:, 2, :].unsqueeze(2).to_broadcast([P, TT, E]),
                                      ALU.is_le))
            ch.link(dve.tensor_tensor(tmp[:, 1], tmp[:, 1], tmp[:, 2], ALU.mult))
            ch.link(dve.tensor_tensor(tmp[:, 0], tmp[:, 0], tmp[:, 1], ALU.add))

        def lora_feed_forward(b):
            with ExitStack() as st:
                hid = sb("lhid", [P, JF, T], scope=st)
                with nc.Block() as block:
                    @block.sync
                    def _(sp):
                        subject = sp.value_load(ids[0:1, 0:1], min_val=0, max_val=7)
                        sp.dma_start(Ai[:, :, R:2 * R], a["Aie"][subject]).then_inc(l_w, 16)
                        sp.dma_start(Bi[R:2 * R, :], a["Bie"][subject]).then_inc(l_w, 16)
                        sp.dma_start(Ao[:, :, R:2 * R], a["Aoe"][subject]).then_inc(l_w, 16)
                        sp.dma_start(Bo[R:2 * R, :], a["Boe"][subject]).then_inc(l_w, 16)

                    @block.tensor
                    def _(pe):
                        pe.wait_ge(l_w, 64)
                        product(pe, ps[0:2 * R, 0, :], [(Ai[:, k, :], x[:, k, :]) for k in range(DC)], l_lo)
                        pe.wait_ge(l_lc, 1)
                        for f in range(JF):
                            if f == 7:
                                pe.wait_ge(l_r, 1)
                            product(pe, ps[:, 1 + f % 7, :],
                                    [(wi[:, k, f * P:(f + 1) * P], x[:, k, :]) for k in range(DC)]
                                    + [(Bi[:, f * P:(f + 1) * P], low[:, 0, :])], l_h)
                        pe.wait_ge(l_r, JF)
                        product(pe, ps[0:2 * R, 0, :], [(Ao[:, k, :], hid[:, k, :]) for k in range(JF)], l_lo)
                        pe.wait_ge(l_lc, 2)
                        for j in range(DC):
                            product(pe, ps[:, 2 + j, :],
                                    [(wo[:, k, j * P:(j + 1) * P], hid[:, k, :]) for k in range(JF)]
                                    + [(Bo[:, j * P:(j + 1) * P], low[:, 1, :])], l_o)

                    @block.scalar
                    def _(act):
                        act.wait_ge(l_lo, 1)
                        act.activation(low[0:2 * R, 0, :], ps[0:2 * R, 0, :], ACT.Copy, scale=2.0).then_inc(l_lc, 1)
                        for f in range(JF):
                            act.wait_ge(l_h, f + 1)
                            act.activation(hid[:, f, :], ps[:, 1 + f % 7, :], ACT.Relu).then_inc(l_r, 1)
                        act.wait_ge(l_lo, 2)
                        act.activation(low[0:2 * R, 1, :], ps[0:2 * R, 0, :], ACT.Copy, scale=2.0).then_inc(l_lc, 1)
                        for j in range(DC):
                            act.wait_ge(l_o, j + 1)
                            act.activation(y[:, j, :], ps[:, 2 + j, :], ACT.Copy).then_inc(l_oc, 1)

        def attention(b):
            with ExitStack() as st:
                Wq = sb("Wq", [P, DC, NH * RH], scope=st)
                Wk = sb("Wk", [P, DC, NH * RH], scope=st)
                Qz = sb("Qz", [P, NH, T], scope=st)
                Kt = sb("Kt", [P, NH // 2, T], scope=st)
                V = sb("V", [P, TT, NH * D], scope=st)
                with ExitStack() as st1:
                    Wv = sb("Wv", [P, DC, NH * D], scope=st1)
                    with nc.Block() as block:
                        @block.sync
                        def _(sp):
                            sp.dma_start(Wq[:, :, :], a["Wq"]).then_inc(a_pj, 16)
                            sp.dma_start(Wk[:, :, :], a["Wk"]).then_inc(a_s, 16)
                            sp.dma_start(Wv[:, :, :], a["Wv"]).then_inc(a_pv, 16)

                        @block.gpsimd
                        def _(pool):
                            for h in range(NH):
                                o = RH * (1 - h % 2)
                                pool.memset(Qz[o:o + RH, h, :], 0.0).then_inc(a_mx, 1)

                        @block.tensor
                        def _(pe):
                            pe.wait_ge(a_pj, 16)
                            for j in range(NH // 2):
                                product(pe, ps[:, j, :], [(Wq[:, k, j * P:(j + 1) * P], y[:, k, :])
                                                          for k in range(DC)], a_tp)
                            pe.wait_ge(a_s, 16)
                            for j in range(NH // 2):
                                product(pe, ps[:, 4 + j, :], [(Wk[:, k, j * P:(j + 1) * P], y[:, k, :])
                                                              for k in range(DC)], a_tp)
                            pe.wait_ge(a_pv, 16)
                            for i in range(4 * TT):
                                t, n = i // 4, i % 4
                                if i < 4:
                                    pe.wait_ge(a_ea, 2 * (i + 1))
                                elif i < 8:
                                    pe.wait_ge(a_ev, i - 4 + 1)
                                elif (i - 8) % 2 == 0:
                                    pe.wait_ge(a_ea, NH + (i - 8) // 2 + 1)
                                else:
                                    pe.wait_ge(a_ev, NH // 2 + (i - 8) // 2 + 1)
                                product(pe, ps[:, i % 8, :], [(y[:, k, t * P:(t + 1) * P], Wv[:, k, n * 512:(n + 1) * 512])
                                                              for k in range(DC)], a_tp)

                        @block.scalar
                        def _(act):
                            for h in range(NH):
                                o = RH * (h % 2)
                                act.wait_ge(a_tp, h // 2 + 1)
                                act.activation(Qz[o:o + RH, h, :], ps[o:o + RH, h // 2, :], ACT.Copy).then_inc(a_ea, 1)
                            for i in range(0, 4 * TT, 2):
                                t, n = i // 4, i % 4
                                act.wait_ge(a_tp, NH + i + 1)
                                act.activation(V[:, t, n * 512:(n + 1) * 512], ps[:, i % 8, :], ACT.Copy).then_inc(a_ea, 1)

                        @block.vector
                        def _(dve):
                            for j in range(NH // 2):
                                dve.wait_ge(a_tp, NH // 2 + j + 1)
                                dve.tensor_copy(Kt[:, j, :], ps[:, 4 + j, :]).then_inc(a_ev, 1)
                            for i in range(1, 4 * TT, 2):
                                t, n = i // 4, i % 4
                                dve.wait_ge(a_tp, NH + i + 1)
                                dve.tensor_copy(V[:, t, n * 512:(n + 1) * 512], ps[:, i % 8, :]).then_inc(a_ev, 1)
                with ExitStack() as st2:
                    pp = sb("pp", [P, 2, TT, T], scope=st2)
                    pT = sb("pT", [P, 2, TT, T], scope=st2)
                    mx = sb("mx", [P, 2, TT], scope=st2)
                    nm = sb("nm", [P, 2, TT], scope=st2)
                    sm = sb("sm", [P, 2, TT], scope=st2)
                    rs = sb("rs", [P, 2, TT], scope=st2)
                    with nc.Block() as block:
                        @block.tensor
                        def _(pe):
                            def scores(h):
                                if h:
                                    pe.wait_ge(p_ex, TT * h)
                                for t in range(TT):
                                    product(pe, ps[:, t, :], [(Qz[:, h, t * P:(t + 1) * P], Kt[:, h // 2, :])], p_s)

                            def turn(h, m):
                                i = TT * h + m
                                pe.wait_ge(p_nm, TT * (h + 1))
                                if i >= 2:
                                    pe.wait_ge(p_ta if m % 2 == 0 else p_td, (i - 2) // 2 + 1)
                                for t in range(TT):
                                    ins = pe.transpose(ps[:, 4 + m % 2, t * P:(t + 1) * P],
                                                       pp[:, h % 2, t, m * P:(m + 1) * P], ident[:, :])
                                ins.then_inc(p_tp, 1)

                            def values(h):
                                pe.wait_ge(p_ta, 2 * (h + 1))
                                pe.wait_ge(p_td, 2 * (h + 1))
                                for j in range(DC):
                                    for m in range(TT):
                                        ins = pe.matmul(ps[:, 6 + j, :], V[:, m, h * D + j * P:h * D + (j + 1) * P],
                                                        pT[:, h % 2, m, :], start=(h == 0 and m == 0),
                                                        stop=(h == NH - 1 and m == TT - 1))
                                ins.then_inc(p_pv, 1)

                            scores(0)
                            for h in range(NH):
                                if h + 1 < NH:
                                    scores(h + 1)
                                turn(h, 0)
                                turn(h, 1)
                                if h:
                                    values(h - 1)
                                turn(h, 2)
                                turn(h, 3)
                            values(NH - 1)

                        @block.scalar
                        def _(act):
                            def exps(h):
                                act.wait_ge(p_mx, h + 1)
                                if h >= 2:
                                    act.wait_ge(p_tp, TT * (h - 1))
                                for t in range(TT):
                                    act.activation(pp[:, h % 2, t, :], ps[:, t, :], ACT.Exp, bias=nm[:, h % 2, t:t + 1],
                                                   accum_out=sm[:, h % 2, t:t + 1]).then_inc(p_ex, 1)

                            exps(0)
                            for h in range(NH):
                                if h + 1 < NH:
                                    exps(h + 1)
                                for m in (0, 2):
                                    act.wait_ge(p_tp, TT * h + m + 1)
                                    if h >= 2:
                                        act.wait_ge(p_pv, h - 1)
                                    act.activation(pT[:, h % 2, m, :], ps[:, 4, :], ACT.Copy).then_inc(p_ta, 1)

                        @block.vector
                        def _(dve):
                            ch = Chain(dve, p_st)

                            def maxima(h):
                                dve.wait_ge(p_s, TT * (h + 1))
                                if h >= 2:
                                    dve.wait_ge(p_ex, TT * (h - 1))
                                ch.link(dve.tensor_reduce(mx[:, h % 2, :], ps[:, 0:TT, :], X, ALU.max))
                                dve.tensor_scalar(nm[:, h % 2, :], mx[:, h % 2, :], -1.0, None, ALU.mult).then_inc(p_mx, 1)

                            def normalise(h):
                                dve.wait_ge(p_ex, TT * (h + 1))
                                if h >= 2:
                                    dve.wait_ge(p_nm, TT * (h - 1))
                                ch.link(dve.reciprocal(rs[:, h % 2, :], sm[:, h % 2, :]))
                                for t in range(TT):
                                    dve.tensor_scalar(pp[:, h % 2, t, :], pp[:, h % 2, t, :], rs[:, h % 2, t:t + 1],
                                                      None, ALU.mult).then_inc(p_nm, 1)

                            maxima(0)
                            normalise(0)
                            for h in range(NH):
                                if h + 1 < NH:
                                    maxima(h + 1)
                                dve.wait_ge(p_tp, TT * h + 2)
                                if h >= 2:
                                    dve.wait_ge(p_pv, h - 1)
                                dve.tensor_copy(pT[:, h % 2, 1, :], ps[:, 5, :]).then_inc(p_td, 1)
                                if h + 1 < NH:
                                    normalise(h + 1)
                                dve.wait_ge(p_tp, TT * h + 4)
                                dve.tensor_copy(pT[:, h % 2, 3, :], ps[:, 5, :]).then_inc(p_td, 1)
                            dve.wait_ge(p_pv, NH)
                            for j in range(DC):
                                ch.step(dve.tensor_tensor(x[:, j, :], x[:, j, :], ps[:, 6 + j, :], ALU.add))

        def adapter(b):
            with ExitStack() as st:
                wa = sb("wa", [P, DC * P + D + 7], scope=st)
                z = sb("az", [P, T], scope=st)
                yy = sb("ayy", [P, DC, T], scope=st)
                yc = sb("ayc", [P, DC, T], scope=st)
                sq = sb("asq", [P, DC, T], scope=st)
                sd = sb("asd", [P, T], scope=st)
                rstd = sb("arstd", [P, T], scope=st)
                down = wa[:, 0:DC * P].rearrange("p (k m) -> p k m", k=DC)
                up = wa[:, DC * P:DC * P + D]
                v = wa[:, DC * P + D:]
                bd, bu, lng, lnb = v[:, 0:1], v[:, 1:3], v[:, 3:5], v[:, 5:7]
                with nc.Block() as block:
                    @block.sync
                    def _(sp):
                        sp.dma_start(ids[0:1, 1:2], a["profile"][b]).then_inc(d_id, 16)
                        sp.wait_ge(d_id, 16)
                        profile = sp.value_load(ids[0:1, 1:2], min_val=0, max_val=7)
                        sp.dma_start(wa[:, :], a["Wad"][profile]).then_inc(d_w, 16)

                    @block.tensor
                    def _(pe):
                        pe.wait_ge(d_w, 16)
                        product(pe, ps[:, 0, :], [(down[:, k, :], x[:, k, :]) for k in range(DC)], d_z)
                        pe.wait_ge(d_za, 1)
                        for j in range(DC):
                            product(pe, ps[:, 1 + j, :], [(up[:, j * P:(j + 1) * P], z[:, :])], d_u)
                        pe.wait_ge(d_y, DC)
                        product(pe, ps[:, 3, :], [(mean[:, :], yy[:, k, :]) for k in range(DC)], d_mn)
                        pe.wait_ge(d_sq, DC)
                        product(pe, ps[:, 4, :], [(mean[:, :], sq[:, k, :]) for k in range(DC)], d_var)

                    @block.scalar
                    def _(act):
                        act.wait_ge(d_z, 1)
                        act.activation(z[:, :], ps[:, 0, :], ACT.Relu, bias=bd).then_inc(d_za, 1)
                        for j in range(DC):
                            act.wait_ge(d_yc, j + 1)
                            act.activation(sq[:, j, :], yc[:, j, :], ACT.Square).then_inc(d_sq, 1)
                        act.wait_ge(d_var, 1)
                        act.activation(sd[:, :], ps[:, 4, :], ACT.Sqrt, bias=epst[:, :]).then_inc(d_sd, 1)

                    @block.vector
                    def _(dve):
                        ch = Chain(dve, d_st)
                        for j in range(DC):
                            dve.wait_ge(d_u, j + 1)
                            dve.scalar_tensor_tensor(out=yy[:, j, :], in0=ps[:, 1 + j, :], scalar=bu[:, j:j + 1],
                                                     in1=x[:, j, :], op0=ALU.add, op1=ALU.add).then_inc(d_y, 1)
                        dve.wait_ge(d_mn, 1)
                        for j in range(DC):
                            dve.wait_ge(d_y, j + 1)
                            dve.tensor_tensor(yc[:, j, :], yy[:, j, :], ps[:, 3, :], ALU.subtract).then_inc(d_yc, 1)
                        dve.wait_ge(d_sd, 1)
                        dve.wait_ge(d_yc, DC)
                        ch.link(dve.reciprocal(rstd[:, :], sd[:, :]))
                        for j in range(DC):
                            ch.step(dve.scalar_tensor_tensor(out=y[:, j, :], in0=yc[:, j, :], scalar=lng[:, j:j + 1],
                                                             in1=rstd[:, :], op0=ALU.mult, op1=ALU.mult))
                        for j in range(DC):
                            ch.all_but(1)
                            ch.step(dve.tensor_scalar(y[:, j, :], y[:, j, :], lnb[:, j:j + 1], None, ALU.add))

        def second_mixture(b):
            with ExitStack() as st:
                NE = E1 + ES
                we = sb("gwe", [P, NW1, 2 * DC * H1 + D], scope=st)
                si = sb("gsi", [P, 2, T], scope=st)
                hh = sb("ghh", [P, 2, T], scope=st)
                acc = sb("gacc", [P, TT, D], scope=st)
                pb = sb("gpb", [P, TT, E1], scope=st)
                tmp = sb("gtmp", [P, 3, TT, E1], scope=st)
                srt = sb("gsrt", [P, TT, 8], scope=st)
                small = sb("gsmall", [P, 4, TT], scope=st)
                w1 = [we[:, i, 0:DC * H1].rearrange("p (k m) -> p k m", k=DC) for i in range(NW1)]
                w3 = [we[:, i, DC * H1:2 * DC * H1].rearrange("p (k m) -> p k m", k=DC) for i in range(NW1)]
                w2 = [we[:, i, 2 * DC * H1:] for i in range(NW1)]
                with nc.Block() as block:
                    @block.sync
                    def _(sp):
                        for e in range(NE):
                            if e >= NW1:
                                sp.wait_ge(g_dn, TT * (e - NW1 + 1))
                            sp.dma_start(we[:, e % NW1, :], a["E1"][e]).then_inc(g_e[e % NW1], 16)
                        sp.wait_ge(g_o, DC)
                        sp.dma_start(out[b], x[:, :, :]).then_inc(g_out, 16)
                        sp.wait_ge(g_out, 16)

                    @block.tensor
                    def _(pe):
                        for t in range(TT):
                            product(pe, ps[:, 6, t * E1:(t + 1) * E1], [(y[:, k, t * P:(t + 1) * P], Wg1[:, k, :])
                                                                        for k in range(DC)], g_lg)

                        def up(e):
                            pe.wait_ge(g_e[e % NW1], 16 * (e // NW1 + 1))
                            if e >= 2:
                                pe.wait_ge(g_hh, e - 1)
                            for n, w in enumerate((w1, w3)):
                                product(pe, ps[:, 2 * (e % 2) + n, :], [(w[e % NW1][:, k, :], y[:, k, :])
                                                                        for k in range(DC)], g_up)

                        def down(e):
                            o = 4 + 2 * (e % 2)
                            pe.wait_ge(g_hh, e + 1)
                            if e >= 2:
                                pe.wait_ge(g_acc, TT * (e - 1))
                            for t in range(TT):
                                product(pe, ps[:, o + t // 2, (t % 2) * D:(t % 2 + 1) * D],
                                        [(hh[:, e % 2, t * P:(t + 1) * P], w2[e % NW1])], g_dn)

                        up(0)
                        up(1)
                        pe.wait_ge(g_sel, 1)
                        for t in range(TT):
                            product(pe, ps[:, 7, t * E1:(t + 1) * E1],
                                    [(ones[:, :], tmp[:, 0, q, :]) for q in range(t)] + [(tri[:, :], tmp[:, 0, t, :])])
                        product(pe, ps[:, 7, TT * E1:(TT + 1) * E1],
                                [(ones[:, :], tmp[:, 0, q, :]) for q in range(TT)], g_cum)
                        pe.wait_ge(g_sel, 2)
                        for e in range(NE):
                            down(e)
                            if e + 2 < NE:
                                up(e + 2)
                        pe.wait_ge(g_acc, TT * NE)
                        for t in range(TT):
                            for j in range(DC):
                                pe.transpose(ps[:, j, t * P:(t + 1) * P], acc[:, t, j * P:(j + 1) * P],
                                             ident[:, :]).then_inc(g_tr, 1)

                    @block.scalar
                    def _(act):
                        act.wait_ge(g_ex, 1)
                        act.activation(pb[:, :, :], pb[:, :, :], ACT.Exp).then_inc(g_ex, 1)
                        for e in range(NE):
                            act.wait_ge(g_up, 2 * e + 1)
                            if e >= 2:
                                act.wait_ge(g_hh, e - 1)
                            act.activation(si[:, e % 2, :], ps[:, 2 * (e % 2), :], ACT.Silu).then_inc(g_si, 1)

                    @block.vector
                    def _(dve):
                        ch = Chain(dve, g_st)
                        dve.wait_ge(g_lg, TT)
                        logits = ps[:, 6, 0:TT * E1].rearrange("p (t e) -> p t e", t=TT)
                        choose(dve, None, ch, g_ex, logits, pb[:, :, :], tmp, srt, small, E1, K1, 1.0)
                        finish_choice(dve, ch, tmp, small, E1, K1)
                        dve.wait_ge(g_st, ch.n)
                        dve.tensor_tensor(wgt[:, :, 0:E1], tmp[:, 0], pb[:, :, :], ALU.mult).then_inc(g_sel, 1)
                        dve.wait_ge(g_cum, 1)
                        counts = ps[:, 7, 0:TT * E1].rearrange("p (t e) -> p t e", t=TT)
                        ch.link(dve.tensor_tensor(tmp[:, 1], counts,
                                                  carry[:, :].unsqueeze(1).to_broadcast([P, TT, E1]), ALU.add))
                        ch.link(dve.tensor_scalar(tmp[:, 1], tmp[:, 1], float(CAP), None, ALU.is_le))
                        dve.wait_ge(g_sel, 1)
                        ch.link(dve.tensor_tensor(wgt[:, :, 0:E1], wgt[:, :, 0:E1], tmp[:, 1], ALU.mult))
                        dve.tensor_tensor(carry[:, :], carry[:, :], ps[:, 7, TT * E1:(TT + 1) * E1],
                                          ALU.add).then_inc(g_sel, 1)

                        def hidden(e):
                            dve.wait_ge(g_up, 2 * (e + 1))
                            dve.wait_ge(g_si, e + 1)
                            if e >= 2:
                                dve.wait_ge(g_dn, TT * (e - 1))
                            dve.tensor_tensor(hh[:, e % 2, :], si[:, e % 2, :], ps[:, 2 * (e % 2) + 1, :],
                                              ALU.mult).then_inc(g_hh, 1)

                        def accumulate(e):
                            o = 4 + 2 * (e % 2)
                            for t in range(TT):
                                dve.wait_ge(g_dn, TT * e + 2 * (t // 2) + 2)
                                src = ps[:, o + t // 2, (t % 2) * D:(t % 2 + 1) * D]
                                if e == 0:
                                    ins = dve.tensor_scalar(acc[:, t, :], src, wgt[:, t, e:e + 1], None, ALU.mult)
                                else:
                                    dve.wait_ge(g_acc, TT * (e - 1) + t + 1)
                                    ins = dve.scalar_tensor_tensor(out=acc[:, t, :], in0=src, scalar=wgt[:, t, e:e + 1],
                                                                   in1=acc[:, t, :], op0=ALU.mult, op1=ALU.add)
                                ins.then_inc(g_acc, 1)

                        hidden(0)
                        hidden(1)
                        for e in range(NE):
                            accumulate(e)
                            if e + 2 < NE:
                                hidden(e + 2)
                        dve.wait_ge(g_tr, TT * DC)
                        for j in range(DC):
                            dve.tensor_tensor(x[:, j, :], x[:, j, :], ps[:, j, :], ALU.add).then_inc(g_o, 1)

        p_s, p_mx, p_ex, p_nm, p_st = (sem("p_" + n) for n in ("scores", "maxima", "exps", "normalised", "dve_step"))
        p_tp, p_ta, p_td, p_pv = (sem("p_" + n) for n in ("turned", "copied_act", "copied_dve", "values"))

        with nc.Fori(0, B) as b:
            conditioner(b)
            mixer(b)
            first_mixture(b)
            lora_feed_forward(b)
            attention(b)
            adapter(b)
            second_mixture(b)
            with nc.Block() as block:
                @block.sync
                def _(sp):
                    for s in sems[SETUP_SEMS:]:
                        sp.sem_clear(s)


def kxm(w):
    w = np.asarray(w)
    return np.ascontiguousarray(w.reshape(w.shape[0] // P, P, w.shape[1]).transpose(1, 0, 2))


def cols(v):
    return np.asarray(v).reshape(-1, P).T


def arrays_of(i):
    g = {k: np.asarray(v) for k, v in i.items()}
    pad = lambda v: np.concatenate([v.reshape(-1, 1), np.zeros((P - v.size, 1), np.float32)])
    flat = lambda *ws: np.concatenate([w.reshape(P, -1) for w in ws], 1)
    h = {
        "x": g["x"].transpose(0, 2, 1).reshape(B, DC, P, T).transpose(0, 2, 1, 3),
        "Wg": kxm(g["L0_cond_Wg"].T), "Wn1": kxm(g["L0_cond_Wn1"].T), "Wn2": g["cond_256"].T,
        "Wsoma": kxm(g["L0_cond_Wsoma"].T), "Wtemp": kxm(g["L0_cond_Wtemp"].T), "Wout": kxm(g["L0_cond_Wout"].T),
        "Win": kxm(g["L0_attn_W_in"].T), "Wxd": kxm(g["L0_attn_W_x"][:DTR].T), "Wxbc": kxm(g["L0_attn_W_x"][DTR:].T),
        "Wdt": g["L0_attn_W_dt"].T, "Wo": kxm(g["L0_attn_W_out"].T),
        "wi": kxm(g["L1_cond_wi"].T), "wo": kxm(g["L1_cond_wo"].T),
        "Aic": kxm(g["L1_cond_common_wi_a"].T), "Bic": g["L1_cond_common_wi_b"].T,
        "Aoc": kxm(g["L1_cond_common_wo_a"].T), "Boc": g["L1_cond_common_wo_b"].T,
        "Aie": np.stack([kxm(w.T) for w in g["L1_cond_experts_wi_a"]]),
        "Bie": g["L1_cond_experts_wi_b"].transpose(0, 2, 1),
        "Aoe": np.stack([kxm(w.T) for w in g["L1_cond_experts_wo_a"]]),
        "Boe": g["L1_cond_experts_wo_b"].transpose(0, 2, 1),
        "Wq": kxm(g["L1_attn_Wq"].T), "Wk": kxm(g["L1_attn_Wk"].T), "Wv": kxm(g["L1_attn_Wv"].T),
        "Wg0": kxm(g["L0_ffn_Wg"]), "Wg1": kxm(g["L1_ffn_Wg"]), "b2": g["L0_ffn_b2"],
        "b1e": g["L0_ffn_b1"].reshape(E0, JH, P).transpose(2, 0, 1), "bg0": g["L0_ffn_bg"],
        "vec": np.concatenate([cols(g["L0_cond_" + n]) for n in ("bg", "bsoma", "btemp", "gamma", "beta")]
                              + [pad(g["L0_cond_bn1"])]
                              + [cols(g["L0_attn_" + n]) for n in ("conv_b", "b_dt", "D")], 1),
        "cw": g["L0_attn_conv_w"].reshape(JI, P, 4).transpose(1, 0, 2),
        "Araw": g["L0_attn_A_raw"].reshape(NS, JI, P).transpose(2, 1, 0),
        "tau": g["condB_tauraws"], "tau_ctx": g["L0_cond_tau_ctx"].reshape(1), "bn2": g["condB_bn2"],
        "blend": g["cond_1024"].reshape(NTR, DC, P).transpose(2, 1, 0),
        "subject": g["itok_B_0_7"].reshape(B, 1, 1), "profile": g["itok_B_0_6"].reshape(B, 1, 1),
        "Wsub": np.stack([flat(kxm(w.T), cols(v)) for w, v in zip(g["L0_cond2_weight"], g["L0_cond2_bias"])]),
        "E0": np.stack([flat(kxm(w1), kxm(w2)) for w1, w2 in zip(g["L0_ffn_W1"], g["L0_ffn_W2"])]),
        "Wad": np.stack([flat(kxm(g["L1_cond2_down_w"][e]), g["L1_cond2_up_w"][e],
                              *(cols(g["L1_cond2_" + n][e]) for n in ("down_b", "up_b", "ln_g", "ln_b")))
                         for e in range(8)]),
        "E1": np.stack([flat(kxm(w1), kxm(w3), w2) for w1, w3, w2 in
                        zip(g["L1_ffn_W1"], g["L1_ffn_W3"], g["L1_ffn_W2"])]
                       + [flat(kxm(g["L1_ffn_Ws1"][:, H1 * s:H1 * (s + 1)]), kxm(g["L1_ffn_Ws3"][:, H1 * s:H1 * (s + 1)]),
                               g["L1_ffn_Ws2"][H1 * s:H1 * (s + 1)]) for s in range(ES)]),
    }
    return {k: np.ascontiguousarray(v) for k, v in h.items()}


def kernel(**inputs):
    import concourse.bacc as bacc
    from concourse.bass_utils import run_bass_kernel_spmd

    nc = bacc.Bacc("TRN2", target_bir_lowering=False, num_devices=1)
    arrays = {f"in_{k}": v for k, v in arrays_of(inputs).items()}
    aps = {k[3:]: nc.dram_tensor(k, v.shape, mybir.dt.from_np(v.dtype), kind="ExternalInput").ap()
           for k, v in arrays.items()}
    out = nc.dram_tensor("out", (B, P, DC, T), F32, kind="ExternalOutput").ap()
    build(nc, aps, out)
    r = run_bass_kernel_spmd(nc, [arrays], core_ids=[0])
    o = r.results[0]["out"]
    return np.ascontiguousarray(o.transpose(0, 2, 1, 3).reshape(B, D, T).transpose(0, 2, 1))
```

```python
from contextlib import ExitStack

import numpy as np

import concourse.bass as bass
from concourse import mybir

F32 = mybir.dt.float32
BF16 = mybir.dt.bfloat16
I32 = mybir.dt.int32
ALU = mybir.AluOpType
ACT = mybir.ActivationFunctionType
X = mybir.AxisListType.X

P = 128
B = 8
T = 512
TT = T // P
D = 256
DC = D // P
NTR = 8
HN = 64
DI = 512
JI = DI // P
NS = 16
DTR = 64
E0, K0, H0 = 8, 2, 512
JH = H0 // P
FF = 1024
JF = FF // P
R = 16
NH, RH = 8, 64
E1, K1, H1 = 32, 4, 128
ES = 2
N = B * T
CAP = 4 * (B * T * K1) // E1
EPS = 1e-5
GATE_EPS = 1e-9
TEMP = 5.0


class Mixture:

    def __init__(self, experts, chosen, most):
        self.E, self.K = experts, chosen
        self.cap = most
        self.region = most
        tiles = N * chosen // P + experts
        self.tiles = (tiles + 3) // 4 * 4
        self.spare = experts * most
        self.none = self.spare + self.tiles * P
        self.places = self.none + P
        self.dropped = self.tiles * P


M0 = Mixture(E0, K0, N)
M1 = Mixture(E1, K1, CAP)


class Chain:

    def __init__(self, eng, sem):
        self.eng, self.sem, self.n = eng, sem, 0

    def step(self, ins):
        ins.then_inc(self.sem, 1)
        self.n += 1

    def all_but(self, k):
        if self.n > k:
            self.eng.wait_ge(self.sem, self.n - k)

    def link(self, ins):
        self.step(ins)
        self.eng.wait_ge(self.sem, self.n)


def build(nc, a, out):
    with ExitStack() as ctx:
        uses = {}

        def sb(name, shape, dt=F32, scope=ctx):
            uses[name] = uses.get(name, 0) + 1
            return scope.enter_context(nc.sbuf_tensor(f"{name}_{uses[name]}", shape, dt))

        sems = []

        def sem(name):
            s = ctx.enter_context(nc.semaphore(name))
            sems.append(s)
            return s

        ps = ctx.enter_context(nc.psum_tensor("ps", [P, 8, 512], F32))

        ident = sb("ident", [P, P])
        ones = sb("ones", [P, P])
        mean = sb("mean", [P, P])
        tri = sb("tri", [P, P])
        epst = sb("epst", [P, 1])
        zero_ids = sb("zero_ids", [P, M1.places // P], I32)
        zero_row = sb("zero_row", [1, D])
        off = sb("off", [P, E0 + E1])
        steps = sb("steps", [P, N // P])
        tile_no = sb("tile_no", [P, M1.tiles])
        eno = sb("eno", [P, E1])
        tok = sb("tok", [P, TT])
        closer = sb("closer", [P, E1])
        carry = sb("carry", [P, E1])
        x = sb("x", [P, DC, T])
        y = sb("y", [P, DC, T])
        ids = sb("ids", [1, 2], I32)
        tab_e = sb("tab_e", [1, M1.tiles], I32)
        tab_r = sb("tab_r", [1, M1.tiles], I32)

        def dram(name, shape, dt=F32):
            return nc.dram_tensor(name, shape, dt).ap()

        for M, n in ((M0, "0"), (M1, "1")):
            M.rows = dram("rows" + n, [N, D])
            M.list = dram("list" + n, [M.places, 1], I32)
            M.outs = dram("outs" + n, [M.dropped + 1, D])
            M.place = dram("place" + n, [B, P, TT * M.K])
            M.weight = dram("weight" + n, [B, P, TT * M.K])
        x1d = dram("x1d", [B, P, DC, T])
        resd = dram("resd", [B, P, TT, D])

        masks = sem("masks_made")
        scratch = sem("scratch_cleared")
        with nc.Block() as block:
            @block.gpsimd
            def _(pool):
                for t, v in ((epst, EPS), (ones, 1.0), (mean, 1.0 / D), (ident, 0.0), (tri, 1.0), (carry, 0.0),
                             (zero_row, 0.0)):
                    pool.memset(t[:], v).then_inc(masks, 1)
                pool.memset(zero_ids[:], 0).then_inc(masks, 1)
                pool.wait_ge(masks, 8)
                pool.affine_select(out=ident[:, :], in_=ident[:, :], compare_op=ALU.not_equal, fill=1.0,
                                   base=0, pattern=[[-1, P]], channel_multiplier=1).then_inc(masks, 1)
                pool.affine_select(out=tri[:, :], in_=tri[:, :], compare_op=ALU.is_ge, fill=0.0,
                                   base=0, pattern=[[1, P]], channel_multiplier=-1).then_inc(masks, 1)
                small = dict(allow_small_or_imprecise_dtypes=True)
                pool.iota(off[:, 0:E0], pattern=[[M0.region, E0]], base=-1, channel_multiplier=0, **small).then_inc(masks, 1)
                pool.iota(off[:, E0:], pattern=[[M1.region, E1]], base=-1, channel_multiplier=0, **small).then_inc(masks, 1)
                pool.iota(steps[:, :], pattern=[[P, N // P]], base=0, channel_multiplier=0, **small).then_inc(masks, 1)
                pool.iota(tile_no[:, :], pattern=[[1, M1.tiles]], base=0, channel_multiplier=0, **small).then_inc(masks, 1)
                pool.iota(eno[:, :], pattern=[[1, E1]], base=0, channel_multiplier=0, **small).then_inc(masks, 1)
                pool.iota(tok[:, :], pattern=[[P, TT]], base=0, channel_multiplier=1, **small).then_inc(masks, 1)

            @block.sync
            def _(sp):
                sp.wait_ge(masks, 8)
                for M in (M0, M1):
                    sp.dma_start(M.list.rearrange("(p f) o -> p (f o)", p=P),
                                 zero_ids[:, 0:M.places // P]).then_inc(scratch, 16)
                    sp.dma_start(M.outs[M.dropped:M.dropped + 1, :], zero_row[:, :]).then_inc(scratch, 16)
                sp.wait_ge(scratch, 64)

        def load_first(st):
            def sb(name, shape, dt=F32):
                return st.enter_context(nc.sbuf_tensor("w_" + name, shape, dt))
            Wg = sb("Wg", [P, 4, D])
            Wn1 = sb("Wn1", [P, DC, HN])
            Wn2 = sb("Wn2", [P, NTR])
            Wn2r = sb("Wn2r", [P, NTR, P])
            Wsoma = sb("Wsoma", [P, DC, D])
            Wtemp = sb("Wtemp", [P, DC, D])
            WoutC = sb("WoutC", [P, DC, D])
            Win = sb("Win", [P, DC, 2 * DI])
            Wxd = sb("Wxd", [P, JI, DTR])
            Wxbc = sb("Wxbc", [P, JI, 3, 2 * NS])
            Wdt = sb("Wdt", [P, DI])
            Wo = sb("Wo", [P, JI, D])
            Wg0 = sb("Wg0", [P, DC, E0])
            bg0 = sb("bg0", [P, E0])
            vec = sb("vec", [P, 11 + 3 * JI])
            cw = sb("cw", [P, JI, 4])
            An = sb("An", [P, JI, NS])
            tau = sb("tau", [P, NTR + 1])
            alpha = sb("alpha", [P, NTR + 1])
            bn2 = sb("bn2", [P, NTR])
            blend = sb("blend", [P, DC, NTR])
            bl1 = sb("bl1", [P, DC])
            sel = sb("sel", [96, 2 * NS, P], BF16)
            h1 = sb("h1", [P, T])
            dts = sb("dts", [P, T])
            loads = [(Wg, "Wg"), (Wn1, "Wn1"), (Wsoma, "Wsoma"), (Wtemp, "Wtemp"), (WoutC, "Wout"), (Win, "Win"),
                     (Wxd, "Wxd"), (Wxbc[:, :, 0, :], "Wxbc"), (Wo, "Wo"), (Wg0, "Wg0"),
                     (vec, "vec"), (cw, "cw"), (An, "Araw"), (blend, "blend")]
            ld = sem("weights_loaded")
            clear = sem("padding_cleared")
            su = sem("setup_step")
            exps = sem("setup_exps")
            with nc.Block() as block:
                @block.gpsimd
                def _(pool):
                    for t in (Wn2, Wdt, h1, dts, sel):
                        pool.memset(t[:], 0.0).then_inc(clear, 1)
                    for g in range(3):
                        pool.wait_ge(clear, 5 + g)
                        pool.affine_select(out=sel[:, :, :], in_=sel[:, :, :], compare_op=ALU.not_equal, fill=1.0,
                                           base=-32 * g, pattern=[[-1, 2 * NS], [0, P]],
                                           channel_multiplier=1).then_inc(clear, 1)

                @block.sync
                def _(sp):
                    for t, name in loads:
                        sp.dma_start(t if isinstance(t, bass.AP) else t[:], a[name]).then_inc(ld, 16)
                    sp.dma_start(tau[:, 0:NTR], a["tau"].partition_broadcast(P)).then_inc(ld, 16)
                    sp.dma_start(tau[:, NTR:NTR + 1], a["tau_ctx"].partition_broadcast(P)).then_inc(ld, 16)
                    sp.dma_start(bn2[:, :], a["bn2"].partition_broadcast(P)).then_inc(ld, 16)
                    sp.dma_start(bg0[:, :], a["bg0"].partition_broadcast(P)).then_inc(ld, 16)
                    sp.wait_ge(clear, 2)
                    sp.dma_start(Wn2[0:HN, :], a["Wn2"]).then_inc(ld, 16)
                    sp.dma_start(Wdt[0:DTR, :], a["Wdt"]).then_inc(ld, 16)
                    sp.wait_ge(ld, 16 * (len(loads) + 6))

                @block.scalar
                def _(act):
                    act.wait_ge(ld, 16 * (len(loads) + 6))
                    act.wait_ge(exps, 1)
                    act.activation(alpha[:, :], tau[:, :], ACT.Exp).then_inc(exps, 1)
                    act.activation(An[:, :, :], An[:, :, :], ACT.Exp).then_inc(exps, 1)
                    act.wait_ge(exps, 4)
                    act.activation(blend[:, :, :], blend[:, :, :], ACT.Exp).then_inc(exps, 1)

                @block.vector
                def _(dve):
                    ch = Chain(dve, su)
                    dve.wait_ge(ld, 16 * (len(loads) + 6))
                    dve.tensor_scalar(tau[:, :], tau[:, :], 87.0, None, ALU.min).then_inc(exps, 1)
                    for k in (1, 2):
                        ch.step(dve.tensor_copy(Wxbc[:, :, k, :], Wxbc[:, :, 0, :]))
                    ch.step(dve.tensor_copy(Wn2r[:, :, :], Wn2[:, :].unsqueeze(2).to_broadcast([P, NTR, P])))
                    ch.link(dve.tensor_reduce(bl1[:, :], WoutC[:, :, :], X, ALU.add))
                    ch.link(dve.tensor_scalar(bl1[:, :], bl1[:, :], 1.0 / D, None, ALU.mult))
                    for j in range(DC):
                        ch.link(dve.tensor_scalar(WoutC[:, j, :], WoutC[:, j, :], bl1[:, j:j + 1], None, ALU.subtract))
                    ch.link(dve.tensor_reduce(bl1[:, :], blend[:, :, :], X, ALU.max))
                    dve.wait_ge(exps, 3)
                    dve.tensor_tensor(blend[:, :, :], blend[:, :, :],
                                      bl1[:, :].unsqueeze(2).to_broadcast([P, DC, NTR]), ALU.subtract).then_inc(exps, 1)
                    ch.link(dve.tensor_scalar(alpha[:, :], alpha[:, :], 1.0, None, ALU.add))
                    ch.link(dve.reciprocal(alpha[:, :], alpha[:, :]))
                    ch.link(dve.tensor_scalar(An[:, :, :], An[:, :, :], -1.0, None, ALU.mult))
                    dve.wait_ge(exps, 5)
                    ch.link(dve.tensor_reduce(bl1[:, :], blend[:, :, :], X, ALU.add))
                    ch.link(dve.reciprocal(bl1[:, :], bl1[:, :]))
                    ch.link(dve.tensor_tensor(blend[:, :, :], blend[:, :, :],
                                              bl1[:, :].unsqueeze(2).to_broadcast([P, DC, NTR]), ALU.mult))
            return (Wg, Wn1, Wn2r, Wsoma, Wtemp, WoutC, Win, Wxd, Wxbc, Wdt, Wo, Wg0, bg0, vec, cw, An, alpha, bn2,
                    blend, sel, h1, dts)

        def load_second(st):
            def sb(name, shape, dt=F32):
                return st.enter_context(nc.sbuf_tensor("w_" + name, shape, dt))
            wi = sb("wi", [P, DC, FF])
            wo = sb("wo", [P, JF, D])
            Ai = sb("Ai", [P, DC, 2 * R])
            Bi = sb("Bi", [P, FF])
            Ao = sb("Ao", [P, JF, 2 * R])
            Bo = sb("Bo", [P, D])
            Wg1 = sb("Wg1", [P, DC, E1])
            Wq = sb("Wq", [P, DC, NH * RH])
            Wk = sb("Wk", [P, DC, NH * RH])
            Wv = sb("Wv", [P, DC, NH * D])
            Wsh = sb("Wsh", [P, ES, 2 * DC * H1 + D])
            low = sb("low", [P, 2, T])
            ld = sem("second_weights_loaded")
            clear = sem("second_padding_cleared")
            with nc.Block() as block:
                @block.gpsimd
                def _(pool):
                    for t in (Bi, Bo, low, carry):
                        pool.memset(t[:], 0.0).then_inc(clear, 1)
                    pool.iota(tok[:, :], pattern=[[P, TT]], base=0, channel_multiplier=1,
                              allow_small_or_imprecise_dtypes=True).then_inc(clear, 1)

                @block.sync
                def _(sp):
                    for t, name in ((wi, "wi"), (wo, "wo"), (Ai[:, :, 0:R], "Aic"), (Ao[:, :, 0:R], "Aoc"), (Wg1, "Wg1"),
                                    (Wq, "Wq"), (Wk, "Wk"), (Wv, "Wv"), (Wsh, "Wsh")):
                        sp.dma_start(t if isinstance(t, bass.AP) else t[:], a[name]).then_inc(ld, 16)
                    sp.wait_ge(clear, 2)
                    sp.dma_start(Bi[0:R, :], a["Bic"]).then_inc(ld, 16)
                    sp.dma_start(Bo[0:R, :], a["Boc"]).then_inc(ld, 16)
                    sp.wait_ge(ld, 16 * 11)
            return wi, wo, Ai, Bi, Ao, Bo, Wg1, Wq, Wk, Wv, Wsh, low

        for M, n in ((M0, "first"), (M1, "second")):
            M.listed = sem(f"tokens_listed_{n}")
            M.gathered = [sem(f"rows_gathered_{n}_{i}") for i in range(4)]
            M.fetched = [sem(f"outputs_fetched_{n}_{t}") for t in range(TT)]

        first_sem = len(sems)
        c_in = sem("cond_x_loaded")
        c_ctx = sem("cond_context_ready")
        c_h1, c_soma, c_gate, c_mod, c_tg, c_out, c_var = (
            sem("cond_" + n) for n in ("hidden_product", "soma_product", "gate_product", "mod_product",
                                       "temporal_product", "out_product", "variance_product"))
        c_act = sem("cond_act_step")
        c_dve = sem("cond_dve_step")
        c_tempo = sem("cond_temporal_ready")
        c_sg = sem("cond_soma_gated")
        m_xz, m_dt, m_bc, m_dl = (sem("mix_" + n) for n in ("in_product", "dt_product", "bc_product", "delta_product"))
        m_act = sem("mix_act_step")
        m_dve = sem("mix_dve_step")
        m_conv = sem("mix_conv_ready")
        m_split = sem("mix_bc_split")
        s_b, s_c = sem("scan_b_spread"), sem("scan_c_spread")
        s_da = sem("scan_decay_ready")
        s_bm, s_h = sem("scan_input_ready"), sem("scan_state_ready")
        s_pd = sem("scan_product_ready")
        s_acc = sem("scan_accumulated")
        s_y = sem("scan_y_ready")
        s_yd = sem("scan_y_step")
        s_o = sem("scan_out_product")
        f_id, f_w, f_y, f_ya = (sem("subject_" + n) for n in ("loaded", "weights", "product", "ready"))
        f_st = sem("subject_x_stored")
        r_lg, r_st, r_ex, r_sel, r_cum = (sem("route_" + n) for n in ("logits", "dve_step", "exp", "selected", "counted"))
        r_tr, r_ra, r_rd, r_out = (sem("route_" + n) for n in ("rows_turned", "rows_copied_act", "rows_copied_dve", "stored"))
        r_pl = sem("route_places_ready")
        h_up, h_si, h_hh, h_dn, h_acc, h_xt, h_st = (sem("shared_" + n) for n in ("up", "silu", "hidden", "down", "accumulated",
                                                                            "x_turned", "stored"))
        t_ld, t_st, t_tb, t_rg = (sem("tiles_" + n) for n in ("weights_loaded", "table_step", "table_ready", "table_read"))
        e_id = [sem(f"tile_tokens_{i}") for i in range(4)]
        e_o = [sem(f"tile_stored_{i}") for i in range(4)]
        e_hold, e_tx, e_cx, e_up, e_pre, e_act, e_hid, e_th, e_ch, e_dn, e_od = (
            sem("tile_" + n) for n in ("gather_step", "rows_turned", "rows_copied", "up", "biased", "activated", "hidden",
                                       "hidden_turned", "hidden_copied", "down", "out_ready"))
        q_pl, q_row, q_ld, q_acc, q_tr, q_st = (sem("combine_" + n) for n in ("places_loaded", "rows_found", "loaded", "summed", "turned", "stored"))
        l_w, l_lo, l_lc, l_h, l_r = (sem("l_" + n) for n in ("lora_loaded", "low_product", "low_copied", "hidden_product",
                                                             "hidden_relu"))
        l_o, l_oc = sem("l_out_product"), sem("l_out_copied")
        a_pj, a_ea, a_ev = sem("a_projected"), sem("a_copied_act"), sem("a_copied_dve")
        a_z = sem("a_padding_cleared")
        d_id, d_w, d_z, d_za, d_u, d_y = (sem("d_" + n) for n in ("profile_loaded", "weights", "down_product", "relu",
                                                                 "up_product", "sum_ready"))
        d_mn, d_yc, d_sq, d_var, d_sd, d_st = (sem("d_" + n) for n in ("mean", "centred", "squares", "variance",
                                                                      "deviation", "dve_step"))
        p_s, p_mx, p_ex, p_nm, p_st = (sem("p_" + n) for n in ("scores", "maxima", "exps", "normalised", "dve_step"))
        p_tp, p_ta, p_td, p_pv = (sem("p_" + n) for n in ("turned", "copied_act", "copied_dve", "values"))

        def product(pe, dst, pairs, done=None):
            for i, (lhsT, rhs) in enumerate(pairs):
                last = pe.matmul(dst, lhsT, rhs, start=(i == 0), stop=(i == len(pairs) - 1))
            if done is not None:
                last.then_inc(done, 1)

        def choose(dve, ch, gate_exp, logits, probs, tmp, srt, small, E, K):
            def wide(t):
                return t.unsqueeze(2).to_broadcast([P, TT, E])
            ch.link(dve.tensor_reduce(small[:, 0, :], logits, X, ALU.max))
            dve.tensor_tensor(probs, logits, wide(small[:, 0, :]), ALU.subtract).then_inc(gate_exp, 1)
            dve.wait_ge(gate_exp, 2)
            ch.link(dve.tensor_reduce(small[:, 1, :], probs, X, ALU.add))
            ch.link(dve.reciprocal(small[:, 1, :], small[:, 1, :]))
            ch.link(dve.tensor_tensor(probs, probs, wide(small[:, 1, :]), ALU.mult))
            for t in range(TT):
                ch.step(dve.max(srt[:, t, :], probs[:, t, :]))
            ch.all_but(0)
            kth = srt[:, :, K - 1:K].to_broadcast([P, TT, E])
            ch.link(dve.tensor_tensor(tmp[:, 0], probs, kth, ALU.is_gt))
            ch.link(dve.tensor_tensor(tmp[:, 1], probs, kth, ALU.is_equal))
            ch.link(dve.tensor_reduce(small[:, 2, :], tmp[:, 0], X, ALU.add))
            for t in range(TT):
                ch.step(dve.tensor_tensor_scan(tmp[:, 2, t, :], tmp[:, 1, t, :], tmp[:, 1, t, :], 0.0,
                                               ALU.add, ALU.max))
            ch.all_but(0)

        def conditioner(b):
            with ExitStack() as st:
                cx = sb("cx", [P, DC, T], scope=st)
                soma = sb("soma", [P, DC, T], scope=st)
                wg = sb("wg", [P, DC, T], scope=st)
                gated = sb("gated", [P, DC, T], scope=st)
                mod = sb("mod", [P, NTR, T], scope=st)
                gm = sb("gm", [P, DC, T], scope=st)
                tr = sb("tr", [P, DC, T], scope=st)
                tempo = sb("tempo", [P, DC, T], scope=st)
                tg = sb("tg", [P, DC, T], scope=st)
                sg = sb("sg", [P, DC, T], scope=st)
                sq = sb("sq", [P, DC, T], scope=st)
                std = sb("std", [P, T], scope=st)
                rstd = sb("rstd", [P, T], scope=st)
                MODB = [5, 6, 7, 0]
                with nc.Block() as block:
                    @block.sync
                    def _(sp):
                        sp.dma_start(x[:, :, :], a["x"][b]).then_inc(c_in, 16)

                    @block.tensor
                    def _(pe):
                        pe.wait_ge(c_in, 16)
                        product(pe, ps[0:HN, 0, :], [(Wn1[:, k, :], x[:, k, :]) for k in range(DC)], c_h1)
                        for j in range(DC):
                            product(pe, ps[:, 1 + j, :], [(Wsoma[:, k, j * P:(j + 1) * P], x[:, k, :])
                                                          for k in range(DC)], c_soma)
                        pe.wait_ge(c_ctx, DC)
                        for j in range(DC):
                            product(pe, ps[:, 3 + j, :],
                                    [(Wg[:, k, j * P:(j + 1) * P], x[:, k, :]) for k in range(DC)]
                                    + [(Wg[:, DC + k, j * P:(j + 1) * P], cx[:, k, :]) for k in range(DC)], c_gate)
                        pe.wait_ge(c_act, 1)
                        for d in range(NTR):
                            if d >= 4:
                                pe.wait_ge(c_act, 5 + d - 3)
                            product(pe, ps[:, MODB[d % 4], :], [(Wn2r[:, d, :], h1[:, :])], c_mod)
                        pe.wait_ge(c_tempo, DC)
                        for j in range(DC):
                            product(pe, ps[:, 1 + j, :], [(Wtemp[:, k, j * P:(j + 1) * P], tempo[:, k, :])
                                                          for k in range(DC)], c_tg)
                        pe.wait_ge(c_sg, DC)
                        for j in range(DC):
                            product(pe, ps[:, 3 + j, :], [(WoutC[:, k, j * P:(j + 1) * P], sg[:, k, :])
                                                          for k in range(DC)], c_out)
                        pe.wait_ge(c_act, 5 + NTR + DC + DC)
                        product(pe, ps[:, 5, :], [(mean[:, :], sq[:, k, :]) for k in range(DC)], c_var)

                    @block.scalar
                    def _(act):
                        act.wait_ge(c_h1, 1)
                        act.activation(h1[0:HN, :], ps[0:HN, 0, :], ACT.Gelu, bias=bn1[0:HN, :]).then_inc(c_act, 1)
                        for j in range(DC):
                            act.wait_ge(c_soma, j + 1)
                            act.activation(soma[:, j, :], ps[:, 1 + j, :], ACT.Gelu,
                                           bias=bsoma[:, j:j + 1]).then_inc(c_act, 1)
                        for j in range(DC):
                            act.wait_ge(c_gate, j + 1)
                            act.activation(wg[:, j, :], ps[:, 3 + j, :], ACT.Sigmoid,
                                           bias=bg[:, j:j + 1]).then_inc(c_act, 1)
                        for d in range(NTR):
                            act.wait_ge(c_mod, d + 1)
                            act.activation(mod[:, d, :], ps[:, MODB[d % 4], :], ACT.Sigmoid,
                                           bias=bn2[:, d:d + 1]).then_inc(c_act, 1)
                        for j in range(DC):
                            act.wait_ge(c_tg, j + 1)
                            act.activation(tg[:, j, :], ps[:, 1 + j, :], ACT.Sigmoid,
                                           bias=btemp[:, j:j + 1]).then_inc(c_act, 1)
                        for j in range(DC):
                            act.wait_ge(c_out, j + 1)
                            act.activation(sq[:, j, :], ps[:, 3 + j, :], ACT.Square).then_inc(c_act, 1)
                        act.wait_ge(c_var, 1)
                        act.activation(std[:, :], ps[:, 5, :], ACT.Sqrt, bias=epst[:, :]).then_inc(c_act, 1)

                    @block.vector
                    def _(dve):
                        ch = Chain(dve, c_dve)
                        dve.wait_ge(c_in, 16)
                        for j in range(DC):
                            dve.tensor_tensor_scan(cx[:, j, :], alpha[:, NTR:NTR + 1].to_broadcast([P, T]), x[:, j, :],
                                                   0.0, ALU.mult, ALU.add).then_inc(c_ctx, 1)
                        dve.wait_ge(c_act, 3 + DC)
                        for j in range(DC):
                            ch.step(dve.tensor_tensor(gated[:, j, :], x[:, j, :], wg[:, j, :], ALU.mult))
                        for d in range(NTR):
                            dve.wait_ge(c_act, 5 + d + 1)
                            for j in range(DC):
                                ch.all_but(1)
                                ch.step(dve.scalar_tensor_tensor(out=gm[:, j, :], in0=mod[:, d, :], scalar=0.5,
                                                                 in1=gated[:, j, :], op0=ALU.add, op1=ALU.mult))
                            for j in range(DC):
                                ch.all_but(1)
                                ch.step(dve.tensor_tensor_scan(tr[:, j, :], alpha[:, d:d + 1].to_broadcast([P, T]),
                                                               gm[:, j, :], 0.0, ALU.mult, ALU.add))
                            for j in range(DC):
                                ch.all_but(1 if d < NTR - 1 or j == 0 else 0)
                                if d == 0:
                                    ins = dve.tensor_scalar(tempo[:, j, :], tr[:, j, :], blend[:, j, d:d + 1], None,
                                                            ALU.mult)
                                else:
                                    ins = dve.scalar_tensor_tensor(out=tempo[:, j, :], in0=tr[:, j, :],
                                                                   scalar=blend[:, j, d:d + 1], in1=tempo[:, j, :],
                                                                   op0=ALU.mult, op1=ALU.add)
                                if d < NTR - 1:
                                    ch.step(ins)
                                else:
                                    ins.then_inc(c_tempo, 1)
                        for j in range(DC):
                            dve.wait_ge(c_act, 5 + NTR + j + 1)
                            dve.tensor_tensor(sg[:, j, :], soma[:, j, :], tg[:, j, :], ALU.mult).then_inc(c_sg, 1)
                        dve.wait_ge(c_act, 5 + NTR + 2 * DC + 1)
                        ch.link(dve.reciprocal(rstd[:, :], std[:, :]))
                        for j in range(DC):
                            ch.step(dve.scalar_tensor_tensor(out=y[:, j, :], in0=ps[:, 3 + j, :], scalar=gamma[:, j:j + 1],
                                                             in1=rstd[:, :], op0=ALU.mult, op1=ALU.mult))
                        for j in range(DC):
                            ch.all_but(1)
                            ch.step(dve.tensor_scalar(y[:, j, :], y[:, j, :], beta[:, j:j + 1], None, ALU.add))

        def mixer(b):
            with ExitStack() as st:
                xs = sb("xs", [P, JI, T], scope=st)
                sz = sb("sz", [P, JI, T], scope=st)
                dl = sb("dl", [P, JI, T], scope=st)
                u = sb("u", [P, JI, T], scope=st)
                bc = sb("bc", [96, T], BF16, scope=st)
                with ExitStack() as st1:
                    cv = sb("cv", [P, JI, T], scope=st1)
                    r1 = sb("r1", [P, T], scope=st1)
                    pre = sb("pre", [P, JI, T], scope=st1)
                    ab = sb("ab", [P, JI, T], scope=st1)
                    with nc.Block() as block:
                        @block.tensor
                        def _(pe):
                            for j in range(2 * JI):
                                product(pe, ps[:, j, :], [(Win[:, k, j * P:(j + 1) * P], y[:, k, :]) for k in range(DC)],
                                        m_xz)
                            pe.wait_ge(m_act, 3 * JI)
                            product(pe, ps[0:DTR, 0, :], [(Wxd[:, k, :], xs[:, k, :]) for k in range(JI)], m_dt)
                            product(pe, ps[0:96, 1, :], [(Wxbc[:, k, :, :].rearrange("p a b -> p (a b)"), xs[:, k, :])
                                                         for k in range(JI)], m_bc)
                            pe.wait_ge(m_act, 3 * JI + 1)
                            for j in range(JI):
                                product(pe, ps[:, 2 + j, :], [(Wdt[:, j * P:(j + 1) * P], dts[:, :])], m_dl)

                        @block.scalar
                        def _(act):
                            for j in range(JI):
                                act.wait_ge(m_xz, j + 1)
                                act.activation(cv[:, j, :], ps[:, j, :], ACT.Identity, bias=convb[:, j:j + 1],
                                               scale=cw[:, j, 3:4]).then_inc(m_act, 1)
                            for j in range(JI):
                                act.wait_ge(m_xz, JI + j + 1)
                                act.activation(sz[:, j, :], ps[:, JI + j, :], ACT.Silu).then_inc(m_act, 1)
                            for j in range(JI):
                                act.wait_ge(m_conv, j + 1)
                                act.activation(xs[:, j, :], cv[:, j, :], ACT.Silu).then_inc(m_act, 1)
                            act.wait_ge(m_dt, 1)
                            act.activation(dts[0:DTR, :], ps[0:DTR, 0, :], ACT.Copy).then_inc(m_act, 1)
                            act.wait_ge(m_split, 2)
                            act.activation(ab[:, :, :], pre[:, :, :], ACT.Abs).then_inc(m_act, 1)
                            act.wait_ge(m_act, 3 * JI + 2)
                            act.activation(ab[:, :, :], ab[:, :, :], ACT.Exp, scale=-1.0).then_inc(m_act, 1)
                            act.wait_ge(m_act, 3 * JI + 3)
                            act.activation(ab[:, :, :], ab[:, :, :], ACT.Ln, bias=1.0).then_inc(m_act, 1)

                        @block.vector
                        def _(dve):
                            ch = Chain(dve, m_dve)
                            for j0 in range(0, JI, 2):
                                dve.wait_ge(m_act, j0 + 2)
                                for s in (1, 2, 3):
                                    for j in (j0, j0 + 1):
                                        ch.all_but(1 if s < 3 or j == j0 else 0)
                                        ins = dve.scalar_tensor_tensor(
                                            out=cv[:, j, s:T], in0=ps[:, j, 0:T - s], scalar=cw[:, j, 3 - s:4 - s],
                                            in1=cv[:, j, s:T], op0=ALU.mult, op1=ALU.add)
                                        if s < 3:
                                            ch.step(ins)
                                        else:
                                            ins.then_inc(m_conv, 1)
                            dve.wait_ge(m_bc, 1)
                            ch.link(dve.tensor_copy(bc[:, :], ps[0:96, 1, :]))
                            ch.link(dve.tensor_tensor(r1[0:96, :], ps[0:96, 1, :], bc[:, :], ALU.subtract))
                            ch.step(dve.tensor_copy(bc[32:64, :], r1[32:64, :]))
                            ch.link(dve.tensor_copy(bc[64:96, :], r1[64:96, :]))
                            ch.link(dve.tensor_tensor(r1[64:96, :], r1[64:96, :], bc[64:96, :], ALU.subtract))
                            dve.tensor_copy(bc[64:96, :], r1[64:96, :]).then_inc(m_split, 1)
                            for j in range(JI):
                                dve.wait_ge(m_dl, j + 1)
                                ins = dve.tensor_scalar(pre[:, j, :], ps[:, 2 + j, :], bdt[:, j:j + 1], None, ALU.add)
                                if j < JI - 1:
                                    ch.link(ins)
                                else:
                                    ins.then_inc(m_split, 1)
                            dve.wait_ge(m_act, 3 * JI + 4)
                            ch.link(dve.scalar_tensor_tensor(out=dl[:, :, :], in0=pre[:, :, :], scalar=0.0,
                                                             in1=ab[:, :, :], op0=ALU.max, op1=ALU.add))
                            ch.step(dve.tensor_tensor(u[:, :, :], dl[:, :, :], xs[:, :, :], ALU.mult))
                with ExitStack() as st2:
                    dA = sb("dA", [P, 2, JI, T], scope=st2)
                    ub = sb("ub", [P, 2, JI, T], scope=st2)
                    hs = sb("hs", [P, 2, JI, T], scope=st2)
                    pr = sb("pr", [P, 2, JI, T], scope=st2)
                    with nc.Block() as block:
                        @block.tensor
                        def _(pe):
                            def spread_b(n):
                                if n >= 2:
                                    pe.wait_ge(s_bm, n - 1)
                                pe.matmul(ps[:, 4 + n % 2, :], sel[:, n, :], bc[:, :], start=True,
                                          stop=True).then_inc(s_b, 1)

                            def spread_c(n):
                                if n >= 2:
                                    pe.wait_ge(s_pd, n - 1)
                                pe.matmul(ps[:, 6 + n % 2, :], sel[:, NS + n, :], bc[:, :], start=True,
                                          stop=True).then_inc(s_c, 1)

                            def add_up(n):
                                pe.wait_ge(s_pd, n + 1)
                                for j in range(JI):
                                    ins = pe.matmul(ps[:, j, :], ident[:, :], pr[:, n % 2, j, :],
                                                    start=(n == 0), stop=(n == NS - 1))
                                ins.then_inc(s_acc, 1)

                            for n in range(2):
                                spread_b(n)
                                spread_c(n)
                            spread_b(2)
                            for n in range(NS):
                                if n + 3 < NS:
                                    spread_b(n + 3)
                                if n + 2 < NS:
                                    spread_c(n + 2)
                                add_up(n)
                            pe.wait_ge(s_y, JI)
                            for j in range(DC):
                                product(pe, ps[:, 4 + j, :], [(Wo[:, k, j * P:(j + 1) * P], u[:, k, :])
                                                              for k in range(JI)], s_o)

                        @block.scalar
                        def _(act):
                            for n in range(NS):
                                if n >= 2:
                                    act.wait_ge(s_h, n - 1)
                                for j in range(JI):
                                    act.activation(dA[:, n % 2, j, :], dl[:, j, :], ACT.Exp,
                                                   scale=An[:, j, n:n + 1]).then_inc(s_da, 1)

                        @block.vector
                        def _(dve):
                            def into(n):
                                dve.wait_ge(s_b, n + 1)
                                if n >= 2:
                                    dve.wait_ge(s_h, n - 1)
                                dve.tensor_tensor(ub[:, n % 2], u[:, :, :],
                                                  ps[:, 4 + n % 2, :].unsqueeze(1).to_broadcast([P, JI, T]),
                                                  ALU.mult).then_inc(s_bm, 1)

                            def scan(n):
                                dve.wait_ge(s_da, JI * (n + 1))
                                dve.wait_ge(s_bm, n + 1)
                                if n >= 2:
                                    dve.wait_ge(s_pd, n - 1)
                                for j in range(JI):
                                    ins = dve.tensor_tensor_scan(hs[:, n % 2, j, :], dA[:, n % 2, j, :],
                                                                 ub[:, n % 2, j, :], 0.0, ALU.mult, ALU.add)
                                ins.then_inc(s_h, 1)

                            def out(n):
                                dve.wait_ge(s_h, n + 1)
                                dve.wait_ge(s_c, n + 1)
                                if n >= 2:
                                    dve.wait_ge(s_acc, n - 1)
                                dve.tensor_tensor(pr[:, n % 2], hs[:, n % 2],
                                                  ps[:, 6 + n % 2, :].unsqueeze(1).to_broadcast([P, JI, T]),
                                                  ALU.mult).then_inc(s_pd, 1)

                            into(0)
                            for n in range(NS):
                                if n + 1 < NS:
                                    into(n + 1)
                                scan(n)
                                if n >= 1:
                                    out(n - 1)
                            out(NS - 1)
                            dve.wait_ge(s_acc, NS)
                            ch = Chain(dve, s_yd)
                            for j in range(JI):
                                ch.step(dve.scalar_tensor_tensor(out=ub[:, 0, j, :], in0=xs[:, j, :],
                                                                 scalar=Dv[:, j:j + 1], in1=ps[:, j, :],
                                                                 op0=ALU.mult, op1=ALU.add))
                            dve.wait_ge(s_bm, NS)
                            for j in range(JI):
                                dve.wait_ge(s_yd, j + 1)
                                dve.tensor_tensor(u[:, j, :], ub[:, 0, j, :], sz[:, j, :], ALU.mult).then_inc(s_y, 1)
                            for j in range(DC):
                                dve.wait_ge(s_o, j + 1)
                                ch.step(dve.tensor_tensor(x[:, j, :], x[:, j, :], ps[:, 4 + j, :], ALU.add))

        def finish_choice(dve, ch, tmp, small, E, K):
            ch.link(dve.tensor_scalar(small[:, 2, :], small[:, 2, :], -1.0, float(K), ALU.mult, ALU.add))
            ch.link(dve.tensor_tensor(tmp[:, 2], tmp[:, 2], small[:, 2, :].unsqueeze(2).to_broadcast([P, TT, E]),
                                      ALU.is_le))
            ch.link(dve.tensor_tensor(tmp[:, 1], tmp[:, 1], tmp[:, 2], ALU.mult))
            ch.link(dve.tensor_tensor(tmp[:, 0], tmp[:, 0], tmp[:, 1], ALU.add))

        def subject_layer(b):
            with ExitStack() as st:
                ws = sb("ws", [P, DC * D + DC], scope=st)
                wsub = ws[:, 0:DC * D].rearrange("p (k m) -> p k m", k=DC)
                bsub = ws[:, DC * D:DC * D + DC]
                with nc.Block() as block:
                    @block.sync
                    def _(sp):
                        sp.dma_start(ids[0:1, 0:1], a["subject"][b]).then_inc(f_id, 16)
                        sp.wait_ge(f_id, 16)
                        subject = sp.value_load(ids[0:1, 0:1], min_val=0, max_val=7)
                        sp.dma_start(ws[:, :], a["Wsub"][subject]).then_inc(f_w, 16)
                        sp.dma_start(x1d[b], x[:, :, :]).then_inc(f_st, 16)
                        sp.wait_ge(f_st, 16)

                    @block.tensor
                    def _(pe):
                        pe.wait_ge(f_w, 16)
                        for j in range(DC):
                            product(pe, ps[:, j, :], [(wsub[:, k, j * P:(j + 1) * P], x[:, k, :]) for k in range(DC)],
                                    f_y)

                    @block.scalar
                    def _(act):
                        for j in range(DC):
                            act.wait_ge(f_y, j + 1)
                            act.activation(y[:, j, :], ps[:, j, :], ACT.Identity, bias=bsub[:, j:j + 1]).then_inc(f_ya, 1)

        def route(b, M, Wr, scale, bias=None, limit=False, renorm=False, shared=None):
            E, K = M.E, M.K
            base = off[:, 0:E0] if M is M0 else off[:, E0:]
            with ExitStack() as st:
                pb = sb("pb", [P, TT, E], scope=st)
                lg = sb("lg", [P, TT, E], scope=st)
                wgt = sb("wgt", [P, TT, E], scope=st)
                tmp = sb("tmp", [P, 3, TT, E], scope=st)
                srt = sb("srt", [P, TT, 8], scope=st)
                small = sb("small", [P, 4, TT], scope=st)
                pl = sb("pl", [P, TT, K], scope=st)
                pli = sb("pli", [P, TT, K], I32, scope=st)
                pw = sb("pw", [P, TT, K], scope=st)
                toki = sb("toki", [P, TT], I32, scope=st)
                rows = sb("rows", [P, TT, D], scope=st)
                if shared is not None:
                    si = sb("si", [P, ES, T], scope=st)
                    hh = sb("hh", [P, ES, T], scope=st)
                    res = sb("res", [P, TT, D], scope=st)
                with nc.Block() as block:
                    @block.tensor
                    def _(pe):
                        for t in range(TT):
                            product(pe, ps[:, 6, t * E:(t + 1) * E], [(y[:, k, t * P:(t + 1) * P], Wr[:, k, :])
                                                                      for k in range(DC)], r_lg)
                        for t in range(TT):
                            for j in range(DC):
                                pe.transpose(ps[:, t // 2, (t % 2) * D + j * P:(t % 2) * D + (j + 1) * P],
                                             y[:, j, t * P:(t + 1) * P], ident[:, :]).then_inc(r_tr, 1)
                        if shared is not None:
                            for e in range(ES):
                                for n in range(2):
                                    w = shared[:, e, n * DC * H1:(n + 1) * DC * H1].rearrange("p (k m) -> p k m", k=DC)
                                    product(pe, ps[:, 2 + 2 * e + n, :], [(w[:, k, :], y[:, k, :]) for k in range(DC)],
                                            h_up)
                            pe.wait_ge(r_ra, 1)
                            pe.wait_ge(r_rd, 1)
                            for t in range(TT):
                                for j in range(DC):
                                    pe.transpose(ps[:, t // 2, (t % 2) * D + j * P:(t % 2) * D + (j + 1) * P],
                                                 x[:, j, t * P:(t + 1) * P], ident[:, :]).then_inc(h_xt, 1)
                            pe.wait_ge(h_hh, ES)
                            for t in range(TT):
                                product(pe, ps[:, 4 + t // 2, (t % 2) * D:(t % 2 + 1) * D],
                                        [(hh[:, e, t * P:(t + 1) * P], shared[:, e, 2 * DC * H1:]) for e in range(ES)],
                                        h_dn)
                        pe.wait_ge(r_sel, 1)
                        for t in range(TT):
                            product(pe, ps[:, 7, t * E:(t + 1) * E],
                                    [(ones[:, :], tmp[:, 0, q, :]) for q in range(t)] + [(tri[:, :], tmp[:, 0, t, :])])
                        product(pe, ps[:, 7, TT * E:(TT + 1) * E],
                                [(ones[:, :], tmp[:, 0, q, :]) for q in range(TT)], r_cum)

                    @block.scalar
                    def _(act):
                        act.wait_ge(r_ex, 1)
                        act.activation(pb[:, :, :], pb[:, :, :], ACT.Exp, scale=scale).then_inc(r_ex, 1)
                        act.wait_ge(r_tr, TT * DC)
                        act.activation(rows[:, 0:2, :], ps[:, 0, :].rearrange("p (t d) -> p t d", t=2),
                                       ACT.Copy).then_inc(r_ra, 1)
                        act.activation(rows[:, 2:4, :], ps[:, 1, :].rearrange("p (t d) -> p t d", t=2),
                                       ACT.Copy).then_inc(r_rd, 1)
                        if shared is not None:
                            for e in range(ES):
                                act.wait_ge(h_up, 2 * e + 1)
                                act.activation(si[:, e, :], ps[:, 2 + 2 * e, :], ACT.Silu).then_inc(h_si, 1)
                            act.wait_ge(h_xt, TT * DC)
                            for i in range(2):
                                act.activation(res[:, 2 * i:2 * i + 2, :], ps[:, i, :].rearrange("p (t d) -> p t d", t=2),
                                               ACT.Copy).then_inc(h_st, 1)

                    @block.vector
                    def _(dve):
                        ch = Chain(dve, r_st)
                        dve.wait_ge(r_lg, TT)
                        logits = ps[:, 6, 0:TT * E].rearrange("p (t e) -> p t e", t=TT)
                        if bias is not None:
                            ch.link(dve.tensor_tensor(lg[:, :, :], logits, bias.unsqueeze(1).to_broadcast([P, TT, E]),
                                                      ALU.add))
                            logits = lg[:, :, :]
                        choose(dve, ch, r_ex, logits, pb[:, :, :], tmp, srt, small, E, K)
                        finish_choice(dve, ch, tmp, small, E, K)
                        dve.tensor_tensor(wgt[:, :, :], tmp[:, 0], pb[:, :, :], ALU.mult).then_inc(r_sel, 1)
                        if shared is not None:
                            for e in range(ES):
                                dve.wait_ge(h_si, e + 1)
                                dve.wait_ge(h_up, 2 * e + 2)
                                dve.tensor_tensor(hh[:, e, :], si[:, e, :], ps[:, 3 + 2 * e, :], ALU.mult).then_inc(h_hh, 1)
                        dve.wait_ge(r_sel, 1)
                        if renorm:
                            ch.link(dve.tensor_reduce(small[:, 3, :], wgt[:, :, :], X, ALU.add))
                            ch.link(dve.tensor_scalar(small[:, 3, :], small[:, 3, :], GATE_EPS, None, ALU.add))
                            ch.link(dve.reciprocal(small[:, 3, :], small[:, 3, :]))
                            ch.link(dve.tensor_tensor(wgt[:, :, :], wgt[:, :, :],
                                                      small[:, 3, :].unsqueeze(2).to_broadcast([P, TT, E]), ALU.mult))
                        dve.wait_ge(r_cum, 1)
                        counts = ps[:, 7, 0:TT * E].rearrange("p (t e) -> p t e", t=TT)
                        ch.link(dve.tensor_tensor(tmp[:, 1], counts,
                                                  carry[:, 0:E].unsqueeze(1).to_broadcast([P, TT, E]), ALU.add))
                        ch.step(dve.tensor_tensor(carry[:, 0:E], carry[:, 0:E], ps[:, 7, TT * E:(TT + 1) * E], ALU.add))
                        if limit:
                            ch.link(dve.tensor_scalar(tmp[:, 2], tmp[:, 1], float(M.cap), None, ALU.is_le))
                            ch.link(dve.tensor_tensor(tmp[:, 0], tmp[:, 0], tmp[:, 2], ALU.mult))
                            ch.link(dve.tensor_tensor(wgt[:, :, :], wgt[:, :, :], tmp[:, 2], ALU.mult))
                        ch.link(dve.tensor_tensor(tmp[:, 1], tmp[:, 1], base.unsqueeze(1).to_broadcast([P, TT, E]),
                                                  ALU.add))
                        ch.link(dve.tensor_scalar(tmp[:, 1], tmp[:, 1], -1.0, float(M.none), ALU.mult, ALU.add))
                        ch.link(dve.tensor_tensor(tmp[:, 1], tmp[:, 1], tmp[:, 0], ALU.mult))
                        for t in range(TT):
                            ch.step(dve.max(srt[:, t, :], tmp[:, 1, t, :]))
                        ch.all_but(0)
                        ch.link(dve.tensor_scalar(pl[:, :, :], srt[:, :, 0:K], -1.0, float(M.none), ALU.mult, ALU.add))
                        dve.tensor_copy(toki[:, :], tok[:, :]).then_inc(r_pl, 1)
                        dve.tensor_copy(pli[:, :, :], pl[:, :, :]).then_inc(r_pl, 1)
                        dve.wait_ge(r_pl, 1)
                        ch.step(dve.tensor_scalar(tok[:, :], tok[:, :], float(T), None, ALU.add))
                        for k in range(K):
                            ch.link(dve.tensor_tensor(tmp[:, 2], tmp[:, 1], srt[:, :, k:k + 1].to_broadcast([P, TT, E]),
                                                      ALU.is_equal))
                            ch.link(dve.tensor_tensor(tmp[:, 2], tmp[:, 2], wgt[:, :, :], ALU.mult))
                            dve.tensor_reduce(pw[:, :, k], tmp[:, 2], X, ALU.add).then_inc(r_pl, 1)
                            dve.wait_ge(r_pl, k + 3)
                        if shared is not None:
                            dve.wait_ge(h_st, 2)
                            for i in range(2):
                                dve.wait_ge(h_dn, 2 * i + 2)
                                dve.tensor_tensor(res[:, 2 * i:2 * i + 2, :], res[:, 2 * i:2 * i + 2, :],
                                                  ps[:, 4 + i, :].rearrange("p (t d) -> p t d", t=2),
                                                  ALU.add).then_inc(h_acc, 1)

                    @block.gpsimd
                    def _(pool):
                        pool.wait_ge(r_pl, 2)
                        for t in range(TT):
                            for k in range(K):
                                pool.indirect_dma_start(M.list, bass.IndirectOffsetOnAxis(pli[:, t, k:k + 1], 0),
                                                        toki[:, t:t + 1], None).then_inc(M.listed, 16)
                        pool.wait_ge(M.listed, b * (16 * TT * K) + 16 * TT * K)

                    @block.sync
                    def _(sp):
                        sp.wait_ge(r_ra, 1)
                        sp.wait_ge(r_rd, 1)
                        sp.dma_start(M.rows.rearrange("(b t p) d -> b p t d", b=B, p=P)[b], rows[:, :, :]).then_inc(r_out, 16)
                        sp.wait_ge(r_pl, 2 + K)
                        sp.dma_start(M.place[b], pl[:, :, :].rearrange("p t k -> p (t k)")).then_inc(r_out, 16)
                        sp.dma_start(M.weight[b], pw[:, :, :].rearrange("p t k -> p (t k)")).then_inc(r_out, 16)
                        if shared is not None:
                            sp.wait_ge(h_acc, 2)
                            sp.dma_start(resd[b], res[:, :, :]).then_inc(r_out, 16)
                        sp.wait_ge(r_out, 16 * (4 if shared is not None else 3))

        def experts(M, wu, wd, wname, biases=None):
            E, NT = M.E, M.tiles
            width = wu.shape[3]
            JK = wd.shape[2]
            with ExitStack() as st:
                nt = sb("nt", [P, E], scope=st)
                cmpn = sb("cmpn", [P, E, M.region // P], scope=st)
                ends = sb("ends", [P, E], scope=st)
                le = sb("le", [1, NT, E], scope=st)
                ti = sb("ti", [1, 4, NT], scope=st)
                idt = sb("idt", [P, 4], I32, scope=st)
                hold = sb("hold", [1, 1], scope=st)
                xg = sb("xg", [P, 4, D], scope=st)
                xT = sb("xT", [P, 2, D], scope=st)
                pre = sb("pre", [P, 2, width], scope=st)
                hd = sb("hd", [P, 2, JK * P], scope=st)
                hT = sb("hT", [P, 2, JK * P], scope=st)
                og = sb("og", [P, 4, D], scope=st)
                with nc.Block() as block:
                    @block.sync
                    def _(sp):
                        for dst, src in wname:
                            sp.dma_start(dst, src).then_inc(t_ld, 16)
                        sp.wait_ge(t_ld, 16 * len(wname))

                    @block.vector
                    def _(dve):
                        ch = Chain(dve, t_st)
                        J = M.region // P
                        ch.link(dve.tensor_tensor(cmpn[:, :, :], carry[:, 0:E].unsqueeze(2).to_broadcast([P, E, J]),
                                                  steps[:, 0:J].unsqueeze(1).to_broadcast([P, E, J]), ALU.is_gt))
                        ch.link(dve.tensor_reduce(nt[:, :], cmpn[:, :, :], X, ALU.add))
                        ch.link(dve.tensor_tensor_scan(ends[:, :], nt[:, :], nt[:, :], 0.0, ALU.add, ALU.max))
                        ch.link(dve.tensor_tensor(le[:, :, :], ends[0:1, :].unsqueeze(1).to_broadcast([1, NT, E]),
                                                  tile_no[0:1, 0:NT].unsqueeze(2).to_broadcast([1, NT, E]), ALU.is_le))
                        ch.link(dve.tensor_reduce(ti[:, 0, :], le[:, :, :], X, ALU.add))
                        ch.link(dve.tensor_tensor(le[:, :, :], le[:, :, :],
                                                  nt[0:1, :].unsqueeze(1).to_broadcast([1, NT, E]), ALU.mult))
                        ch.link(dve.tensor_reduce(ti[:, 1, :], le[:, :, :], X, ALU.add))
                        ch.link(dve.tensor_tensor(ti[:, 1, :], tile_no[0:1, 0:NT], ti[:, 1, :], ALU.subtract))
                        ch.link(dve.tensor_scalar(ti[:, 2, :], ti[:, 0, :], float(E), None, ALU.is_equal))
                        ch.link(dve.tensor_scalar(ti[:, 1, :], ti[:, 1, :], float(P), None, ALU.mult))
                        ch.link(dve.scalar_tensor_tensor(out=ti[:, 1, :], in0=ti[:, 0, :], scalar=float(M.region),
                                                         in1=ti[:, 1, :], op0=ALU.mult, op1=ALU.add))
                        ch.link(dve.tensor_tensor(ti[:, 0, :], ti[:, 0, :], ti[:, 2, :], ALU.subtract))
                        ch.step(dve.tensor_scalar(closer[:, 1:E], nt[:, 0:E - 1], float(P), -float(M.region),
                                                  ALU.mult, ALU.add))
                        ch.step(dve.memset(closer[:, 0:1], 0.0))
                        dve.tensor_copy(tab_e[:, 0:NT], ti[:, 0, :]).then_inc(t_tb, 1)
                        dve.tensor_copy(tab_r[:, 0:NT], ti[:, 1, :]).then_inc(t_tb, 1)

                def pipeline(eng, last, *stages):
                    lead = 8
                    for k in range(lead):
                        for lag, stage in stages:
                            if k >= lag:
                                stage(k - lag, (k - lag) // 4, (k - lag) % 4)
                    with eng.Fori(lead // 4, NT // 4) as i:
                        for g in range(4):
                            for lag, stage in stages:
                                stage(i * 4 + (g - lag), i + (g - lag) // 4, (g - lag) % 4)
                    for k in range(NT, NT + last):
                        for lag, stage in stages:
                            if k - lag < NT:
                                stage(k - lag, (k - lag) // 4, (k - lag) % 4)

                def reuse(eng, s, value):
                    if not isinstance(value, int) or value > 0:
                        eng.wait_ge(s, value)

                def entry(eng, table, tile, most):
                    return eng.value_load(table[0:1, bass.ds(tile, 1)], min_val=0, max_val=most)

                gated = biases is None
                up_read = e_hid if gated else e_pre
                with nc.Block() as block:
                    @block.sync
                    def _(sp):
                        def load(t, r, s):
                            reuse(sp, M.gathered[s], r * 16)
                            row = entry(sp, tab_r, t, M.none - P)
                            sp.dma_start(idt[:, s:s + 1], M.list[bass.ds(row, P), :]).then_inc(e_id[s], 16)

                        def store(t, r, s):
                            sp.wait_ge(e_od, t + 1)
                            sp.dma_start(M.outs[bass.ds(t * P, P), :], og[:, s, :]).then_inc(e_o[s], 16)

                        pipeline(sp, 8, (0, load), (8, store))
                        for s in range(4):
                            sp.wait_ge(e_o[s], 16 * (NT // 4))

                    @block.gpsimd
                    def _(pool):
                        def gather(t, r, s):
                            pool.wait_ge(e_id[s], r * 16 + 16)
                            reuse(pool, e_tx, t - 3)
                            pool.wait_ge(e_hold, t + 1)
                            pool.tensor_tensor(hold[:, :], hold[:, :], hold[:, :], ALU.mult).then_inc(e_hold, 1)
                            pool.indirect_dma_start(xg[:, s, :], None, M.rows,
                                                    bass.IndirectOffsetOnAxis(idt[:, s:s + 1], 0)).then_inc(M.gathered[s], 16)

                        pool.memset(hold[:, :], 0.0).then_inc(e_hold, 1)
                        pipeline(pool, 0, (0, gather))

                    @block.tensor
                    def _(pe):
                        def turn_rows(t, r, s):
                            pe.wait_ge(M.gathered[s], r * 16 + 16)
                            reuse(pe, e_cx, t - 1)
                            for j in range(DC):
                                ins = pe.transpose(ps[:, s % 2, j * P:(j + 1) * P], xg[:, s, j * P:(j + 1) * P], ident[:, :])
                            ins.then_inc(e_tx, 1)

                        def up(t, r, s):
                            e = entry(pe, tab_e, t, E - 1)
                            pe.wait_ge(e_cx, t + 1)
                            reuse(pe, up_read, t - 1)
                            product(pe, ps[:, 2 + s % 2, 0:width], [(xT[:, s % 2, k * P:(k + 1) * P], wu[:, e, k, :])
                                                                    for k in range(DC)], e_up)

                        def turn_hidden(t, r, s):
                            pe.wait_ge(e_hid, t + 1)
                            reuse(pe, e_ch, t - 1)
                            for j in range(JK):
                                ins = pe.transpose(ps[:, 4 + s % 2, j * P:(j + 1) * P], hd[:, s % 2, j * P:(j + 1) * P],
                                                   ident[:, :])
                            ins.then_inc(e_th, 1)

                        def down(t, r, s):
                            e = entry(pe, tab_e, t, E - 1)
                            pe.wait_ge(e_ch, t + 1)
                            reuse(pe, e_od, t - 1)
                            product(pe, ps[:, 6 + s % 2, 0:D], [(hT[:, s % 2, j * P:(j + 1) * P], wd[:, e, j, :])
                                                                for j in range(JK)], e_dn)

                        pipeline(pe, 4, (0, turn_rows), (1, up), (3, turn_hidden), (4, down))

                    @block.scalar
                    def _(act):
                        def copy_rows(t, r, s):
                            act.wait_ge(e_tx, t + 1)
                            reuse(act, e_up, t - 1)
                            act.activation(xT[:, s % 2, :], ps[:, s % 2, 0:D], ACT.Copy).then_inc(e_cx, 1)

                        def silu(t, r, s):
                            act.wait_ge(e_up, t + 1)
                            reuse(act, e_hid, t - 1)
                            act.activation(pre[:, s % 2, 0:H1], ps[:, 2 + s % 2, 0:H1], ACT.Silu).then_inc(e_act, 1)

                        def gelu(t, r, s):
                            act.wait_ge(e_pre, t + 1)
                            reuse(act, e_th, t - 1)
                            act.activation(hd[:, s % 2, :], pre[:, s % 2, :], ACT.Gelu).then_inc(e_hid, 1)

                        def copy_hidden(t, r, s):
                            act.wait_ge(e_th, t + 1)
                            reuse(act, e_dn, t - 1)
                            act.activation(hT[:, s % 2, :], ps[:, 4 + s % 2, 0:JK * P], ACT.Copy).then_inc(e_ch, 1)

                        pipeline(act, 3, (0, copy_rows), (1, silu if gated else gelu), (3, copy_hidden))

                    @block.vector
                    def _(dve):
                        def gate(t, r, s):
                            dve.wait_ge(e_act, t + 1)
                            reuse(dve, e_th, t - 1)
                            dve.tensor_tensor(hd[:, s % 2, :], pre[:, s % 2, 0:H1], ps[:, 2 + s % 2, H1:2 * H1],
                                              ALU.mult).then_inc(e_hid, 1)

                        def add_bias(t, r, s):
                            e = entry(dve, tab_e, t, E - 1)
                            dve.wait_ge(e_up, t + 1)
                            reuse(dve, e_hid, t - 1)
                            dve.tensor_tensor(pre[:, s % 2, :], ps[:, 2 + s % 2, 0:width], biases[0][:, e, :],
                                              ALU.add).then_inc(e_pre, 1)

                        def finish(t, r, s):
                            if not gated:
                                e = entry(dve, tab_e, t, E - 1)
                            dve.wait_ge(e_dn, t + 1)
                            reuse(dve, e_o[s], r * 16)
                            if gated:
                                ins = dve.tensor_copy(og[:, s, :], ps[:, 6 + s % 2, 0:D])
                            else:
                                ins = dve.tensor_tensor(og[:, s, :], ps[:, 6 + s % 2, 0:D], biases[1][:, e, :], ALU.add)
                            ins.then_inc(e_od, 1)

                        pipeline(dve, 4, (1, gate if gated else add_bias), (4, finish))

        def rows_of(dve, ch, M, places, past, shift):
            shape = [P, TT * M.K, M.E]
            base = off[:, 0:E0] if M is M0 else off[:, E0:]
            ch.link(dve.tensor_tensor(past[:, :, :], places.unsqueeze(2).to_broadcast(shape),
                                      base.unsqueeze(1).to_broadcast(shape), ALU.is_gt))
            ch.link(dve.tensor_tensor(past[:, :, :], past[:, :, :], closer[:, 0:M.E].unsqueeze(1).to_broadcast(shape),
                                      ALU.mult))
            ch.link(dve.tensor_reduce(shift[:, :], past[:, :, :], X, ALU.add))
            ch.link(dve.tensor_tensor(shift[:, :], shift[:, :], places, ALU.add))
            ch.link(dve.tensor_scalar(shift[:, :], shift[:, :], float(M.dropped), None, ALU.min))

        def combine_first(b):
            M = M0
            with ExitStack() as st:
                pl = sb("qpl", [P, TT, M.K], scope=st)
                past = sb("qpast", [P, TT * M.K, M.E], scope=st)
                shift = sb("qshift", [P, TT * M.K], scope=st)
                row = sb("qrow", [P, TT, M.K], I32, scope=st)
                pw = sb("qpw", [P, TT, M.K], scope=st)
                rg = sb("qrg", [P, TT, M.K, D], scope=st)
                acc = sb("qacc", [P, TT, D], scope=st)
                with nc.Block() as block:
                    @block.sync
                    def _(sp):
                        sp.dma_start(pl[:, :, :].rearrange("p t k -> p (t k)"), M.place[b]).then_inc(q_pl, 16)
                        sp.dma_start(pw[:, :, :].rearrange("p t k -> p (t k)"), M.weight[b]).then_inc(q_ld, 16)
                        sp.dma_start(x[:, :, :], x1d[b]).then_inc(q_ld, 16)
                        sp.dma_start(ids[0:1, 0:1], a["subject"][b]).then_inc(q_ld, 16)

                    @block.gpsimd
                    def _(pool):
                        pool.wait_ge(q_row, 1)
                        for t in range(TT):
                            for k in range(M.K):
                                pool.indirect_dma_start(rg[:, t, k, :], None, M.outs,
                                                        bass.IndirectOffsetOnAxis(row[:, t, k:k + 1], 0)).then_inc(M.fetched[t], 16)

                    @block.vector
                    def _(dve):
                        ch = Chain(dve, q_st)
                        dve.wait_ge(q_pl, 16)
                        rows_of(dve, ch, M, pl[:, :, :].rearrange("p t k -> p (t k)"), past, shift)
                        dve.tensor_copy(row[:, :, :].rearrange("p t k -> p (t k)"), shift[:, :]).then_inc(q_row, 1)
                        dve.wait_ge(q_ld, 48)
                        for t in range(TT):
                            dve.wait_ge(M.fetched[t], b * (16 * M.K) + 16 * M.K)
                            ch.link(dve.tensor_scalar(acc[:, t, :], rg[:, t, 0, :], pw[:, t, 0:1], None, ALU.mult))
                            dve.scalar_tensor_tensor(out=acc[:, t, :], in0=rg[:, t, 1, :], scalar=pw[:, t, 1:2],
                                                     in1=acc[:, t, :], op0=ALU.mult, op1=ALU.add).then_inc(q_acc, 1)
                        dve.wait_ge(q_tr, TT * DC)
                        for j in range(DC):
                            ch.step(dve.tensor_tensor(x[:, j, :], x[:, j, :], ps[:, j, :], ALU.add))

                    @block.tensor
                    def _(pe):
                        for t in range(TT):
                            pe.wait_ge(q_acc, t + 1)
                            for j in range(DC):
                                pe.transpose(ps[:, j, t * P:(t + 1) * P], acc[:, t, j * P:(j + 1) * P],
                                             ident[:, :]).then_inc(q_tr, 1)

        def combine_second(b):
            M = M1
            with ExitStack() as st:
                pl = sb("qpl", [P, TT, M.K], scope=st)
                past = sb("qpast", [P, TT * M.K, M.E], scope=st)
                shift = sb("qshift", [P, TT * M.K], scope=st)
                row = sb("qrow", [P, TT, M.K], I32, scope=st)
                pw = sb("qpw", [P, TT, M.K], scope=st)
                rg = sb("qrg", [P, TT, M.K, D], scope=st)
                acc = sb("qacc", [P, TT, D], scope=st)
                with nc.Block() as block:
                    @block.sync
                    def _(sp):
                        sp.dma_start(pl[:, :, :].rearrange("p t k -> p (t k)"), M.place[b]).then_inc(q_pl, 16)
                        sp.dma_start(pw[:, :, :].rearrange("p t k -> p (t k)"), M.weight[b]).then_inc(q_ld, 16)
                        sp.dma_start(acc[:, :, :], resd[b]).then_inc(q_ld, 16)
                        sp.wait_ge(q_acc, TT)
                        sp.dma_start(out.rearrange("b (t p) d -> b p t d", p=P)[b], acc[:, :, :]).then_inc(q_st, 16)
                        sp.wait_ge(q_st, 16)

                    @block.gpsimd
                    def _(pool):
                        pool.wait_ge(q_row, 1)
                        for t in range(TT):
                            for k in range(M.K):
                                pool.indirect_dma_start(rg[:, t, k, :], None, M.outs,
                                                        bass.IndirectOffsetOnAxis(row[:, t, k:k + 1], 0)).then_inc(M.fetched[t], 16)

                    @block.vector
                    def _(dve):
                        ch = Chain(dve, q_tr)
                        dve.wait_ge(q_pl, 16)
                        rows_of(dve, ch, M, pl[:, :, :].rearrange("p t k -> p (t k)"), past, shift)
                        dve.tensor_copy(row[:, :, :].rearrange("p t k -> p (t k)"), shift[:, :]).then_inc(q_row, 1)
                        dve.wait_ge(q_ld, 32)
                        for t in range(TT):
                            dve.wait_ge(M.fetched[t], b * (16 * M.K) + 16 * M.K)
                            for k in range(M.K):
                                ins = dve.scalar_tensor_tensor(out=acc[:, t, :], in0=rg[:, t, k, :],
                                                               scalar=pw[:, t, k:k + 1], in1=acc[:, t, :],
                                                               op0=ALU.mult, op1=ALU.add)
                                if k < M.K - 1:
                                    ch.link(ins)
                                else:
                                    ins.then_inc(q_acc, 1)

        def lora_feed_forward(b):
            with ExitStack() as st:
                hid = sb("lhid", [P, JF, T], scope=st)
                with nc.Block() as block:
                    @block.sync
                    def _(sp):
                        subject = sp.value_load(ids[0:1, 0:1], min_val=0, max_val=7)
                        sp.dma_start(Ai[:, :, R:2 * R], a["Aie"][subject]).then_inc(l_w, 16)
                        sp.dma_start(Bi[R:2 * R, :], a["Bie"][subject]).then_inc(l_w, 16)
                        sp.dma_start(Ao[:, :, R:2 * R], a["Aoe"][subject]).then_inc(l_w, 16)
                        sp.dma_start(Bo[R:2 * R, :], a["Boe"][subject]).then_inc(l_w, 16)

                    @block.tensor
                    def _(pe):
                        pe.wait_ge(l_w, 64)
                        product(pe, ps[0:2 * R, 0, :], [(Ai[:, k, :], x[:, k, :]) for k in range(DC)], l_lo)
                        pe.wait_ge(l_lc, 1)
                        for f in range(JF):
                            if f == 7:
                                pe.wait_ge(l_r, 1)
                            product(pe, ps[:, 1 + f % 7, :],
                                    [(wi[:, k, f * P:(f + 1) * P], x[:, k, :]) for k in range(DC)]
                                    + [(Bi[:, f * P:(f + 1) * P], low[:, 0, :])], l_h)
                        pe.wait_ge(l_r, JF)
                        product(pe, ps[0:2 * R, 0, :], [(Ao[:, k, :], hid[:, k, :]) for k in range(JF)], l_lo)
                        pe.wait_ge(l_lc, 2)
                        for j in range(DC):
                            product(pe, ps[:, 2 + j, :],
                                    [(wo[:, k, j * P:(j + 1) * P], hid[:, k, :]) for k in range(JF)]
                                    + [(Bo[:, j * P:(j + 1) * P], low[:, 1, :])], l_o)

                    @block.scalar
                    def _(act):
                        act.wait_ge(l_lo, 1)
                        act.activation(low[0:2 * R, 0, :], ps[0:2 * R, 0, :], ACT.Copy, scale=2.0).then_inc(l_lc, 1)
                        for f in range(JF):
                            act.wait_ge(l_h, f + 1)
                            act.activation(hid[:, f, :], ps[:, 1 + f % 7, :], ACT.Relu).then_inc(l_r, 1)
                        act.wait_ge(l_lo, 2)
                        act.activation(low[0:2 * R, 1, :], ps[0:2 * R, 0, :], ACT.Copy, scale=2.0).then_inc(l_lc, 1)
                        for j in range(DC):
                            act.wait_ge(l_o, j + 1)
                            act.activation(y[:, j, :], ps[:, 2 + j, :], ACT.Copy).then_inc(l_oc, 1)

        def attention(b):
            with ExitStack() as st:
                Qz = sb("Qz", [P, NH, T], scope=st)
                Kt = sb("Kt", [P, NH // 2, T], scope=st)
                V = sb("V", [P, TT, NH * D], scope=st)
                with nc.Block() as block:
                    @block.gpsimd
                    def _(pool):
                        for h in range(NH):
                            o = RH * (1 - h % 2)
                            pool.memset(Qz[o:o + RH, h, :], 0.0).then_inc(a_z, 1)

                    @block.tensor
                    def _(pe):
                        for j in range(NH // 2):
                            product(pe, ps[:, j, :], [(Wq[:, k, j * P:(j + 1) * P], y[:, k, :])
                                                      for k in range(DC)], a_pj)
                        for j in range(NH // 2):
                            product(pe, ps[:, 4 + j, :], [(Wk[:, k, j * P:(j + 1) * P], y[:, k, :])
                                                          for k in range(DC)], a_pj)
                        for i in range(4 * TT):
                            t, n = i // 4, i % 4
                            if i < 4:
                                pe.wait_ge(a_ea, 2 * (i + 1))
                            elif i < 8:
                                pe.wait_ge(a_ev, i - 4 + 1)
                            elif (i - 8) % 2 == 0:
                                pe.wait_ge(a_ea, NH + (i - 8) // 2 + 1)
                            else:
                                pe.wait_ge(a_ev, NH // 2 + (i - 8) // 2 + 1)
                            product(pe, ps[:, i % 8, :], [(y[:, k, t * P:(t + 1) * P], Wv[:, k, n * 512:(n + 1) * 512])
                                                          for k in range(DC)], a_pj)

                    @block.scalar
                    def _(act):
                        for h in range(NH):
                            o = RH * (h % 2)
                            act.wait_ge(a_pj, h // 2 + 1)
                            act.activation(Qz[o:o + RH, h, :], ps[o:o + RH, h // 2, :], ACT.Copy).then_inc(a_ea, 1)
                        for i in range(0, 4 * TT, 2):
                            t, n = i // 4, i % 4
                            act.wait_ge(a_pj, NH + i + 1)
                            act.activation(V[:, t, n * 512:(n + 1) * 512], ps[:, i % 8, :], ACT.Copy).then_inc(a_ea, 1)

                    @block.vector
                    def _(dve):
                        for j in range(NH // 2):
                            dve.wait_ge(a_pj, NH // 2 + j + 1)
                            dve.tensor_copy(Kt[:, j, :], ps[:, 4 + j, :]).then_inc(a_ev, 1)
                        for i in range(1, 4 * TT, 2):
                            t, n = i // 4, i % 4
                            dve.wait_ge(a_pj, NH + i + 1)
                            dve.tensor_copy(V[:, t, n * 512:(n + 1) * 512], ps[:, i % 8, :]).then_inc(a_ev, 1)
                with ExitStack() as st2:
                    pp = sb("pp", [P, 2, TT, T], scope=st2)
                    pT = sb("pT", [P, 2, TT, T], scope=st2)
                    mx = sb("mx", [P, 2, TT], scope=st2)
                    nm = sb("nm", [P, 2, TT], scope=st2)
                    sm = sb("sm", [P, 2, TT], scope=st2)
                    rs = sb("rs", [P, 2, TT], scope=st2)
                    with nc.Block() as block:
                        @block.tensor
                        def _(pe):
                            def scores(h):
                                if h:
                                    pe.wait_ge(p_ex, TT * h)
                                for t in range(TT):
                                    product(pe, ps[:, t, :], [(Qz[:, h, t * P:(t + 1) * P], Kt[:, h // 2, :])], p_s)

                            def turn(h, m):
                                i = TT * h + m
                                pe.wait_ge(p_nm, TT * (h + 1))
                                if i >= 2:
                                    pe.wait_ge(p_ta if m % 2 == 0 else p_td, (i - 2) // 2 + 1)
                                for t in range(TT):
                                    ins = pe.transpose(ps[:, 4 + m % 2, t * P:(t + 1) * P],
                                                       pp[:, h % 2, t, m * P:(m + 1) * P], ident[:, :])
                                ins.then_inc(p_tp, 1)

                            def values(h):
                                pe.wait_ge(p_ta, 2 * (h + 1))
                                pe.wait_ge(p_td, 2 * (h + 1))
                                for j in range(DC):
                                    for m in range(TT):
                                        ins = pe.matmul(ps[:, 6 + j, :], V[:, m, h * D + j * P:h * D + (j + 1) * P],
                                                        pT[:, h % 2, m, :], start=(h == 0 and m == 0),
                                                        stop=(h == NH - 1 and m == TT - 1))
                                ins.then_inc(p_pv, 1)

                            scores(0)
                            for h in range(NH):
                                if h + 1 < NH:
                                    scores(h + 1)
                                turn(h, 0)
                                turn(h, 1)
                                if h:
                                    values(h - 1)
                                turn(h, 2)
                                turn(h, 3)
                            values(NH - 1)

                        @block.scalar
                        def _(act):
                            def exps(h):
                                act.wait_ge(p_mx, h + 1)
                                if h >= 2:
                                    act.wait_ge(p_tp, TT * (h - 1))
                                for t in range(TT):
                                    act.activation(pp[:, h % 2, t, :], ps[:, t, :], ACT.Exp, bias=nm[:, h % 2, t:t + 1],
                                                   accum_out=sm[:, h % 2, t:t + 1]).then_inc(p_ex, 1)

                            exps(0)
                            for h in range(NH):
                                if h + 1 < NH:
                                    exps(h + 1)
                                for m in (0, 2):
                                    act.wait_ge(p_tp, TT * h + m + 1)
                                    if h >= 2:
                                        act.wait_ge(p_pv, h - 1)
                                    act.activation(pT[:, h % 2, m, :], ps[:, 4, :], ACT.Copy).then_inc(p_ta, 1)

                        @block.vector
                        def _(dve):
                            ch = Chain(dve, p_st)

                            def maxima(h):
                                dve.wait_ge(p_s, TT * (h + 1))
                                if h >= 2:
                                    dve.wait_ge(p_ex, TT * (h - 1))
                                ch.link(dve.tensor_reduce(mx[:, h % 2, :], ps[:, 0:TT, :], X, ALU.max))
                                dve.tensor_scalar(nm[:, h % 2, :], mx[:, h % 2, :], -1.0, None, ALU.mult).then_inc(p_mx, 1)

                            def normalise(h):
                                dve.wait_ge(p_ex, TT * (h + 1))
                                if h >= 2:
                                    dve.wait_ge(p_nm, TT * (h - 1))
                                ch.link(dve.reciprocal(rs[:, h % 2, :], sm[:, h % 2, :]))
                                for t in range(TT):
                                    dve.tensor_scalar(pp[:, h % 2, t, :], pp[:, h % 2, t, :], rs[:, h % 2, t:t + 1],
                                                      None, ALU.mult).then_inc(p_nm, 1)

                            maxima(0)
                            normalise(0)
                            for h in range(NH):
                                if h + 1 < NH:
                                    maxima(h + 1)
                                dve.wait_ge(p_tp, TT * h + 2)
                                if h >= 2:
                                    dve.wait_ge(p_pv, h - 1)
                                dve.tensor_copy(pT[:, h % 2, 1, :], ps[:, 5, :]).then_inc(p_td, 1)
                                if h + 1 < NH:
                                    normalise(h + 1)
                                dve.wait_ge(p_tp, TT * h + 4)
                                dve.tensor_copy(pT[:, h % 2, 3, :], ps[:, 5, :]).then_inc(p_td, 1)
                            dve.wait_ge(p_pv, NH)
                            for j in range(DC):
                                ch.step(dve.tensor_tensor(x[:, j, :], x[:, j, :], ps[:, 6 + j, :], ALU.add))

        def adapter(b):
            with ExitStack() as st:
                wa = sb("wa", [P, DC * P + D + 7], scope=st)
                z = sb("az", [P, T], scope=st)
                yy = sb("ayy", [P, DC, T], scope=st)
                yc = sb("ayc", [P, DC, T], scope=st)
                sq = sb("asq", [P, DC, T], scope=st)
                sd = sb("asd", [P, T], scope=st)
                rstd = sb("arstd", [P, T], scope=st)
                down = wa[:, 0:DC * P].rearrange("p (k m) -> p k m", k=DC)
                up = wa[:, DC * P:DC * P + D]
                v = wa[:, DC * P + D:]
                bd, bu, lng, lnb = v[:, 0:1], v[:, 1:3], v[:, 3:5], v[:, 5:7]
                with nc.Block() as block:
                    @block.sync
                    def _(sp):
                        sp.dma_start(ids[0:1, 1:2], a["profile"][b]).then_inc(d_id, 16)
                        sp.wait_ge(d_id, 16)
                        profile = sp.value_load(ids[0:1, 1:2], min_val=0, max_val=7)
                        sp.dma_start(wa[:, :], a["Wad"][profile]).then_inc(d_w, 16)

                    @block.tensor
                    def _(pe):
                        pe.wait_ge(d_w, 16)
                        product(pe, ps[:, 0, :], [(down[:, k, :], x[:, k, :]) for k in range(DC)], d_z)
                        pe.wait_ge(d_za, 1)
                        for j in range(DC):
                            product(pe, ps[:, 1 + j, :], [(up[:, j * P:(j + 1) * P], z[:, :])], d_u)
                        pe.wait_ge(d_y, DC)
                        product(pe, ps[:, 3, :], [(mean[:, :], yy[:, k, :]) for k in range(DC)], d_mn)
                        pe.wait_ge(d_sq, DC)
                        product(pe, ps[:, 4, :], [(mean[:, :], sq[:, k, :]) for k in range(DC)], d_var)

                    @block.scalar
                    def _(act):
                        act.wait_ge(d_z, 1)
                        act.activation(z[:, :], ps[:, 0, :], ACT.Relu, bias=bd).then_inc(d_za, 1)
                        for j in range(DC):
                            act.wait_ge(d_yc, j + 1)
                            act.activation(sq[:, j, :], yc[:, j, :], ACT.Square).then_inc(d_sq, 1)
                        act.wait_ge(d_var, 1)
                        act.activation(sd[:, :], ps[:, 4, :], ACT.Sqrt, bias=epst[:, :]).then_inc(d_sd, 1)

                    @block.vector
                    def _(dve):
                        ch = Chain(dve, d_st)
                        for j in range(DC):
                            dve.wait_ge(d_u, j + 1)
                            dve.scalar_tensor_tensor(out=yy[:, j, :], in0=ps[:, 1 + j, :], scalar=bu[:, j:j + 1],
                                                     in1=x[:, j, :], op0=ALU.add, op1=ALU.add).then_inc(d_y, 1)
                        dve.wait_ge(d_mn, 1)
                        for j in range(DC):
                            dve.wait_ge(d_y, j + 1)
                            dve.tensor_tensor(yc[:, j, :], yy[:, j, :], ps[:, 3, :], ALU.subtract).then_inc(d_yc, 1)
                        dve.wait_ge(d_sd, 1)
                        dve.wait_ge(d_yc, DC)
                        ch.link(dve.reciprocal(rstd[:, :], sd[:, :]))
                        for j in range(DC):
                            ch.step(dve.scalar_tensor_tensor(out=y[:, j, :], in0=yc[:, j, :], scalar=lng[:, j:j + 1],
                                                             in1=rstd[:, :], op0=ALU.mult, op1=ALU.mult))
                        for j in range(DC):
                            ch.all_but(1)
                            ch.step(dve.tensor_scalar(y[:, j, :], y[:, j, :], lnb[:, j:j + 1], None, ALU.add))

        loop_sems = range(first_sem, len(sems))

        def clear_semaphores():
            with nc.Block() as block:
                @block.sync
                def _(sp):
                    sp.sem_clear(range(sems[loop_sems.start].num, sems[loop_sems.stop - 1].num + 1))

        with ExitStack() as st:
            (Wg, Wn1, Wn2r, Wsoma, Wtemp, WoutC, Win, Wxd, Wxbc, Wdt, Wo, Wg0, bg0, vec, cw, An, alpha, bn2,
             blend, sel, h1, dts) = load_first(st)
            bg, bsoma, btemp, gamma, beta = (vec[:, DC * i:DC * (i + 1)] for i in range(5))
            bn1 = vec[:, 5 * DC:5 * DC + 1]
            convb, bdt, Dv = (vec[:, 5 * DC + 1 + JI * i:5 * DC + 1 + JI * (i + 1)] for i in range(3))
            with nc.Fori(0, B) as b:
                conditioner(b)
                mixer(b)
                subject_layer(b)
                route(b, M0, Wg0, 1.0 / TEMP, bias=bg0[:, :], renorm=True)
                clear_semaphores()
        with ExitStack() as st:
            W0u = sb("W0u", [P, E0, DC, H0], scope=st)
            W0d = sb("W0d", [P, E0, JH, D], scope=st)
            b1 = sb("b1", [P, E0, H0], scope=st)
            b2 = sb("b2", [P, E0, D], scope=st)
            experts(M0, W0u, W0d, [(W0u[:, :, :, :], a["W0u"]), (W0d[:, :, :, :], a["W0d"]),
                                   (b1[:, :, :].rearrange("p e h -> p (e h)"), a["b1"].partition_broadcast(P)),
                                   (b2[:, :, :].rearrange("p e h -> p (e h)"), a["b2"].partition_broadcast(P))],
                    biases=(b1, b2))
            clear_semaphores()
        with ExitStack() as st:
            wi, wo, Ai, Bi, Ao, Bo, Wg1, Wq, Wk, Wv, Wsh, low = load_second(st)
            with nc.Fori(0, B) as b:
                combine_first(b)
                lora_feed_forward(b)
                attention(b)
                adapter(b)
                route(b, M1, Wg1, 1.0, limit=True, shared=Wsh)
                clear_semaphores()
        with ExitStack() as st:
            W1u = sb("W1u", [P, E1, DC, 2 * H1], scope=st)
            W1d = sb("W1d", [P, E1, 1, D], scope=st)
            experts(M1, W1u, W1d, [(W1u[:, :, :, :], a["W1u"]), (W1d[:, :, :, :], a["W1d"])])
            clear_semaphores()
        with nc.Fori(0, B) as b:
            combine_second(b)
            clear_semaphores()


def kxm(w):
    w = np.asarray(w)
    return np.ascontiguousarray(w.reshape(w.shape[0] // P, P, w.shape[1]).transpose(1, 0, 2))


def cols(v):
    return np.asarray(v).reshape(-1, P).T


def arrays_of(i):
    g = {k: np.asarray(v) for k, v in i.items()}
    pad = lambda v: np.concatenate([v.reshape(-1, 1), np.zeros((P - v.size, 1), np.float32)])
    flat = lambda *ws: np.concatenate([w.reshape(P, -1) for w in ws], 1)
    h = {
        "x": g["x"].transpose(0, 2, 1).reshape(B, DC, P, T).transpose(0, 2, 1, 3),
        "Wg": kxm(g["L0_cond_Wg"].T), "Wn1": kxm(g["L0_cond_Wn1"].T), "Wn2": g["cond_256"].T,
        "Wsoma": kxm(g["L0_cond_Wsoma"].T), "Wtemp": kxm(g["L0_cond_Wtemp"].T), "Wout": kxm(g["L0_cond_Wout"].T),
        "Win": kxm(g["L0_attn_W_in"].T), "Wxd": kxm(g["L0_attn_W_x"][:DTR].T), "Wxbc": kxm(g["L0_attn_W_x"][DTR:].T),
        "Wdt": g["L0_attn_W_dt"].T, "Wo": kxm(g["L0_attn_W_out"].T),
        "wi": kxm(g["L1_cond_wi"].T), "wo": kxm(g["L1_cond_wo"].T),
        "Aic": kxm(g["L1_cond_common_wi_a"].T), "Bic": g["L1_cond_common_wi_b"].T,
        "Aoc": kxm(g["L1_cond_common_wo_a"].T), "Boc": g["L1_cond_common_wo_b"].T,
        "Aie": np.stack([kxm(w.T) for w in g["L1_cond_experts_wi_a"]]),
        "Bie": g["L1_cond_experts_wi_b"].transpose(0, 2, 1),
        "Aoe": np.stack([kxm(w.T) for w in g["L1_cond_experts_wo_a"]]),
        "Boe": g["L1_cond_experts_wo_b"].transpose(0, 2, 1),
        "Wq": kxm(g["L1_attn_Wq"].T), "Wk": kxm(g["L1_attn_Wk"].T), "Wv": kxm(g["L1_attn_Wv"].T),
        "Wg0": kxm(g["L0_ffn_Wg"]), "Wg1": kxm(g["L1_ffn_Wg"]), "b2": g["L0_ffn_b2"].reshape(-1),
        "b1": g["L0_ffn_b1"].reshape(-1), "bg0": g["L0_ffn_bg"],
        "vec": np.concatenate([cols(g["L0_cond_" + n]) for n in ("bg", "bsoma", "btemp", "gamma", "beta")]
                              + [pad(g["L0_cond_bn1"])]
                              + [cols(g["L0_attn_" + n]) for n in ("conv_b", "b_dt", "D")], 1),
        "cw": g["L0_attn_conv_w"].reshape(JI, P, 4).transpose(1, 0, 2),
        "Araw": g["L0_attn_A_raw"].reshape(NS, JI, P).transpose(2, 1, 0),
        "tau": g["condB_tauraws"], "tau_ctx": g["L0_cond_tau_ctx"].reshape(1), "bn2": g["condB_bn2"],
        "blend": g["cond_1024"].reshape(NTR, DC, P).transpose(2, 1, 0),
        "subject": g["itok_B_0_7"].reshape(B, 1, 1), "profile": g["itok_B_0_6"].reshape(B, 1, 1),
        "Wsub": np.stack([flat(kxm(w.T), cols(v)) for w, v in zip(g["L0_cond2_weight"], g["L0_cond2_bias"])]),
        "W0u": np.stack([kxm(w) for w in g["L0_ffn_W1"]]).transpose(1, 0, 2, 3),
        "W0d": np.stack([kxm(w) for w in g["L0_ffn_W2"]]).transpose(1, 0, 2, 3),
        "Wad": np.stack([flat(kxm(g["L1_cond2_down_w"][e]), g["L1_cond2_up_w"][e],
                              *(cols(g["L1_cond2_" + n][e]) for n in ("down_b", "up_b", "ln_g", "ln_b")))
                         for e in range(8)]),
        "W1u": np.stack([kxm(np.concatenate([w1, w3], 1)) for w1, w3 in
                         zip(g["L1_ffn_W1"], g["L1_ffn_W3"])]).transpose(1, 0, 2, 3),
        "W1d": g["L1_ffn_W2"].transpose(1, 0, 2).reshape(P, E1, 1, D),
        "Wsh": np.stack([flat(kxm(g["L1_ffn_Ws1"][:, H1 * s:H1 * (s + 1)]), kxm(g["L1_ffn_Ws3"][:, H1 * s:H1 * (s + 1)]),
                              g["L1_ffn_Ws2"][H1 * s:H1 * (s + 1)]) for s in range(ES)], 1),
    }
    return {k: np.ascontiguousarray(v) for k, v in h.items()}


def kernel(**inputs):
    import concourse.bacc as bacc
    from concourse.bass_utils import run_bass_kernel_spmd

    nc = bacc.Bacc("TRN2", target_bir_lowering=False, num_devices=1)
    arrays = {f"in_{k}": v for k, v in arrays_of(inputs).items()}
    aps = {k[3:]: nc.dram_tensor(k, v.shape, mybir.dt.from_np(v.dtype), kind="ExternalInput").ap()
           for k, v in arrays.items()}
    out = nc.dram_tensor("out", (B, T, D), F32, kind="ExternalOutput").ap()
    build(nc, aps, out)
    r = run_bass_kernel_spmd(nc, [arrays], core_ids=[0])
    return r.results[0]["out"]
```

```python
from contextlib import ExitStack

import numpy as np

import concourse.bass as bass
from concourse import mybir

F32 = mybir.dt.float32
BF16 = mybir.dt.bfloat16
I32 = mybir.dt.int32
ALU = mybir.AluOpType
ACT = mybir.ActivationFunctionType
X = mybir.AxisListType.X

P = 128
B = 8
T = 512
TT = T // P
D = 256
DC = D // P
NTR = 8
HN = 64
DI = 512
JI = DI // P
NS = 16
DTR = 64
E0, K0, H0 = 8, 2, 512
JH = H0 // P
FF = 1024
JF = FF // P
R = 16
NH, RH = 8, 64
E1, K1, H1 = 32, 4, 128
ES = 2
N = B * T
CAP = 4 * (B * T * K1) // E1
EPS = 1e-5
GR = 4
GATE_EPS = 1e-9
TEMP = 5.0


class Mixture:

    def __init__(self, experts, chosen, most):
        self.E, self.K = experts, chosen
        self.cap = most
        self.region = most
        tiles = N * chosen // P + experts
        self.tiles = (tiles + 3) // 4 * 4
        self.spare = experts * most
        self.none = self.spare + self.tiles * P
        self.places = self.none + P * TT * K1
        self.dropped = self.tiles * P


M0 = Mixture(E0, K0, N)
M1 = Mixture(E1, K1, CAP)


class Tensors:
    pass


class Chain:

    def __init__(self, eng, sem):
        self.eng, self.sem, self.n = eng, sem, 0

    def step(self, ins):
        ins.then_inc(self.sem, 1)
        self.n += 1

    def all_but(self, k):
        if self.n > k:
            self.eng.wait_ge(self.sem, self.n - k)

    def link(self, ins):
        self.step(ins)
        self.eng.wait_ge(self.sem, self.n)


def build(nc, a, out):
    with ExitStack() as ctx:
        uses = {}

        def sb(name, shape, dt=F32, scope=ctx):
            uses[name] = uses.get(name, 0) + 1
            return scope.enter_context(nc.sbuf_tensor(f"{name}_{uses[name]}", shape, dt))

        sems = []

        def sem(name):
            s = ctx.enter_context(nc.semaphore(name))
            sems.append(s)
            return s

        ps = ctx.enter_context(nc.psum_tensor("ps", [P, 8, 512], F32))

        ident = sb("ident", [P, P])
        ones = sb("ones", [P, P])
        mean = sb("mean", [P, P])
        tri = sb("tri", [P, P])
        epst = sb("epst", [P, 1])
        zero_ids = sb("zero_ids", [P, M1.places // P // 4], I32)
        zero_row = sb("zero_row", [1, D])
        off = sb("off", [P, E0 + E1])
        steps = sb("steps", [P, N // P])
        tile_no = sb("tile_no", [P, M1.tiles])
        own = sb("own", [P, TT, K1])
        tok = sb("tok", [P, TT])
        new_tok = sb("new_tok", [P, TT], I32)
        new_pl = sb("new_pl", [P, TT, K1], I32)
        closer = sb("closer", [P, E1])
        carry = sb("carry", [P, E1])
        x = sb("x", [P, DC, T])
        y = sb("y", [P, DC, T])
        ids = sb("ids", [1, 2], I32)
        tab_e = sb("tab_e", [1, M1.tiles], I32)
        tab_r = sb("tab_r", [1, M1.tiles], I32)

        def dram(name, shape, dt=F32):
            return nc.dram_tensor(name, shape, dt).ap()

        for M, n in ((M0, "0"), (M1, "1")):
            M.rows = dram("rows" + n, [N, D])
            M.list = dram("list" + n, [M.places, 1], I32)
            M.outs = dram("outs" + n, [M.dropped + 1, D])
            M.place = dram("place" + n, [B, P, TT * M.K])
            M.weight = dram("weight" + n, [B, P, TT * M.K])
        x1d = dram("x1d", [B, P, DC, T])
        resd = dram("resd", [B, P, TT, D])

        masks = sem("masks_made")
        scratch = sem("scratch_cleared")
        with nc.Block() as block:
            @block.gpsimd
            def _(pool):
                for t, v in ((epst, EPS), (ones, 1.0), (mean, 1.0 / D), (ident, 0.0), (tri, 1.0), (carry, 0.0),
                             (zero_row, 0.0)):
                    pool.memset(t[:], v).then_inc(masks, 1)
                pool.memset(zero_ids[:], 0).then_inc(masks, 1)
                pool.memset(new_tok[:], 0).then_inc(masks, 1)
                pool.wait_ge(masks, 9)
                pool.affine_select(out=ident[:, :], in_=ident[:, :], compare_op=ALU.not_equal, fill=1.0,
                                   base=0, pattern=[[-1, P]], channel_multiplier=1).then_inc(masks, 1)
                pool.affine_select(out=tri[:, :], in_=tri[:, :], compare_op=ALU.is_ge, fill=0.0,
                                   base=0, pattern=[[1, P]], channel_multiplier=-1).then_inc(masks, 1)
                pairs = dict(pattern=[[K1, TT], [1, K1]], channel_multiplier=TT * K1)
                pool.iota(new_pl[:, :, :], base=M0.none, **pairs).then_inc(masks, 1)
                small = dict(allow_small_or_imprecise_dtypes=True)
                pool.iota(off[:, 0:E0], pattern=[[M0.region, E0]], base=-1, channel_multiplier=0, **small).then_inc(masks, 1)
                pool.iota(off[:, E0:], pattern=[[M1.region, E1]], base=-1, channel_multiplier=0, **small).then_inc(masks, 1)
                pool.iota(steps[:, :], pattern=[[P, N // P]], base=0, channel_multiplier=0, **small).then_inc(masks, 1)
                pool.iota(tile_no[:, :], pattern=[[1, M1.tiles]], base=0, channel_multiplier=0, **small).then_inc(masks, 1)
                pool.iota(own[:, :, :], base=0, **pairs, **small).then_inc(masks, 1)
                pool.iota(tok[:, :], pattern=[[P, TT]], base=0, channel_multiplier=1, **small).then_inc(masks, 1)

            @block.sync
            def _(sp):
                sp.wait_ge(masks, 8)
                for M in (M0, M1):
                    for q in range(4):
                        sp.dma_start(M.list.rearrange("(q p f) o -> q p (f o)", q=4, p=P)[q],
                                     zero_ids[:, 0:M.places // P // 4]).then_inc(scratch, 16)
                    sp.dma_start(M.outs[M.dropped:M.dropped + 1, :], zero_row[:, :]).then_inc(scratch, 16)
                sp.wait_ge(scratch, 160)

        def load_first(st):
            def sb(name, shape, dt=F32):
                return st.enter_context(nc.sbuf_tensor("w_" + name, shape, dt))
            Wg = sb("Wg", [P, 4, D])
            Wn1 = sb("Wn1", [P, DC, HN])
            Wn2 = sb("Wn2", [P, NTR])
            Wn2r = sb("Wn2r", [P, NTR, P])
            Wsoma = sb("Wsoma", [P, DC, D])
            Wtemp = sb("Wtemp", [P, DC, D])
            WoutC = sb("WoutC", [P, DC, D])
            Win = sb("Win", [P, DC, 2 * DI])
            Wxd = sb("Wxd", [P, JI, DTR])
            Wxbc = sb("Wxbc", [P, JI, 3, 2 * NS])
            Wdt = sb("Wdt", [P, DI])
            Wo = sb("Wo", [P, JI, D])
            Wg0 = sb("Wg0", [P, DC, E0])
            bg0 = sb("bg0", [P, E0])
            vec = sb("vec", [P, 11 + 3 * JI])
            cw = sb("cw", [P, JI, 4])
            An = sb("An", [P, JI, NS])
            tau = sb("tau", [P, NTR + 1])
            alpha = sb("alpha", [P, NTR + 1])
            bn2 = sb("bn2", [P, NTR])
            blend = sb("blend", [P, DC, NTR])
            mix = sb("mix", [P, DC, NTR, P])
            bl1 = sb("bl1", [P, DC])
            sel = sb("sel", [96, 2 * NS, P], BF16)
            h1 = sb("h1", [P, T])
            dts = sb("dts", [P, T])
            loads = [(Wg, "Wg"), (Wn1, "Wn1"), (Wsoma, "Wsoma"), (Wtemp, "Wtemp"), (WoutC, "Wout"), (Win, "Win"),
                     (Wxd, "Wxd"), (Wxbc[:, :, 0, :], "Wxbc"), (Wo, "Wo"), (Wg0, "Wg0"),
                     (vec, "vec"), (cw, "cw"), (An, "Araw"), (blend, "blend")]
            ld = sem("weights_loaded")
            clear = sem("padding_cleared")
            su = sem("setup_step")
            exps = sem("setup_exps")
            with nc.Block() as block:
                @block.gpsimd
                def _(pool):
                    for t in (Wn2, Wdt, h1, dts, sel):
                        pool.memset(t[:], 0.0).then_inc(clear, 1)
                    for g in range(3):
                        pool.wait_ge(clear, 5 + g)
                        pool.affine_select(out=sel[:, :, :], in_=sel[:, :, :], compare_op=ALU.not_equal, fill=1.0,
                                           base=-32 * g, pattern=[[-1, 2 * NS], [0, P]],
                                           channel_multiplier=1).then_inc(clear, 1)

                @block.sync
                def _(sp):
                    for t, name in loads:
                        sp.dma_start(t if isinstance(t, bass.AP) else t[:], a[name]).then_inc(ld, 16)
                    sp.dma_start(tau[:, 0:NTR], a["tau"].partition_broadcast(P)).then_inc(ld, 16)
                    sp.dma_start(tau[:, NTR:NTR + 1], a["tau_ctx"].partition_broadcast(P)).then_inc(ld, 16)
                    sp.dma_start(bn2[:, :], a["bn2"].partition_broadcast(P)).then_inc(ld, 16)
                    sp.dma_start(bg0[:, :], a["bg0"].partition_broadcast(P)).then_inc(ld, 16)
                    sp.wait_ge(clear, 2)
                    sp.dma_start(Wn2[0:HN, :], a["Wn2"]).then_inc(ld, 16)
                    sp.dma_start(Wdt[0:DTR, :], a["Wdt"]).then_inc(ld, 16)
                    sp.wait_ge(ld, 16 * (len(loads) + 6))

                @block.scalar
                def _(act):
                    act.wait_ge(ld, 16 * (len(loads) + 6))
                    act.wait_ge(exps, 1)
                    act.activation(alpha[:, :], tau[:, :], ACT.Exp).then_inc(exps, 1)
                    act.activation(An[:, :, :], An[:, :, :], ACT.Exp).then_inc(exps, 1)
                    act.wait_ge(exps, 4)
                    act.activation(blend[:, :, :], blend[:, :, :], ACT.Exp).then_inc(exps, 1)

                @block.vector
                def _(dve):
                    ch = Chain(dve, su)
                    dve.wait_ge(ld, 16 * (len(loads) + 6))
                    dve.tensor_scalar(tau[:, :], tau[:, :], 87.0, None, ALU.min).then_inc(exps, 1)
                    for k in (1, 2):
                        ch.step(dve.tensor_copy(Wxbc[:, :, k, :], Wxbc[:, :, 0, :]))
                    ch.step(dve.tensor_copy(Wn2r[:, :, :], Wn2[:, :].unsqueeze(2).to_broadcast([P, NTR, P])))
                    ch.link(dve.tensor_reduce(bl1[:, :], WoutC[:, :, :], X, ALU.add))
                    ch.link(dve.tensor_scalar(bl1[:, :], bl1[:, :], 1.0 / D, None, ALU.mult))
                    for j in range(DC):
                        ch.link(dve.tensor_scalar(WoutC[:, j, :], WoutC[:, j, :], bl1[:, j:j + 1], None, ALU.subtract))
                    ch.link(dve.tensor_reduce(bl1[:, :], blend[:, :, :], X, ALU.max))
                    dve.wait_ge(exps, 3)
                    dve.tensor_tensor(blend[:, :, :], blend[:, :, :],
                                      bl1[:, :].unsqueeze(2).to_broadcast([P, DC, NTR]), ALU.subtract).then_inc(exps, 1)
                    ch.link(dve.tensor_scalar(alpha[:, :], alpha[:, :], 1.0, None, ALU.add))
                    ch.link(dve.reciprocal(alpha[:, :], alpha[:, :]))
                    ch.link(dve.tensor_scalar(An[:, :, :], An[:, :, :], -1.0, None, ALU.mult))
                    dve.wait_ge(exps, 5)
                    ch.link(dve.tensor_reduce(bl1[:, :], blend[:, :, :], X, ALU.add))
                    ch.link(dve.reciprocal(bl1[:, :], bl1[:, :]))
                    ch.link(dve.tensor_tensor(blend[:, :, :], blend[:, :, :],
                                              bl1[:, :].unsqueeze(2).to_broadcast([P, DC, NTR]), ALU.mult))
                    for j in range(DC):
                        for d in range(NTR):
                            ch.step(dve.tensor_scalar(mix[:, j, d, :], ident[:, :], blend[:, j, d:d + 1], None, ALU.mult))
            return (Wg, Wn1, Wn2r, Wsoma, Wtemp, WoutC, Win, Wxd, Wxbc, Wdt, Wo, Wg0, bg0, vec, cw, An, alpha, bn2,
                    mix, sel, h1, dts)

        def load_second(st):
            def sb(name, shape, dt=F32):
                return st.enter_context(nc.sbuf_tensor("w_" + name, shape, dt))
            wi = sb("wi", [P, DC, FF])
            wo = sb("wo", [P, JF, D])
            Ai = sb("Ai", [P, D])
            Bi = sb("Bi", [P, FF])
            Ao = sb("Ao", [P, FF])
            Bo = sb("Bo", [P, D])
            Wg1 = sb("Wg1", [P, DC, E1])
            Wq = sb("Wq", [P, DC, NH * RH])
            Wk = sb("Wk", [P, DC, NH * RH])
            Wv = sb("Wv", [P, DC, NH * D])
            Wsh = sb("Wsh", [P, ES, 2 * DC * H1 + D])
            ld = sem("second_weights_loaded")
            clear = sem("second_padding_cleared")
            with nc.Block() as block:
                @block.gpsimd
                def _(pool):
                    for t in (Ai, Ao, Bi, Bo, carry):
                        pool.memset(t[:], 0.0).then_inc(clear, 1)
                    pool.iota(new_pl[:, :, :], pattern=[[K1, TT], [1, K1]], base=M1.none,
                              channel_multiplier=TT * K1).then_inc(clear, 1)
                    pool.iota(tok[:, :], pattern=[[P, TT]], base=0, channel_multiplier=1,
                              allow_small_or_imprecise_dtypes=True).then_inc(clear, 1)

                @block.sync
                def _(sp):
                    for t, name in ((wi, "wi"), (wo, "wo"), (Wg1, "Wg1"),
                                    (Wq, "Wq"), (Wk, "Wk"), (Wv, "Wv"), (Wsh, "Wsh")):
                        sp.dma_start(t if isinstance(t, bass.AP) else t[:], a[name]).then_inc(ld, 16)
                    sp.wait_ge(clear, 4)
                    sp.dma_start(Ai[0:R, :], a["Aic"]).then_inc(ld, 16)
                    sp.dma_start(Ao[0:R, :], a["Aoc"]).then_inc(ld, 16)
                    sp.dma_start(Bi[0:R, :], a["Bic"]).then_inc(ld, 16)
                    sp.dma_start(Bo[0:R, :], a["Boc"]).then_inc(ld, 16)
            return wi, wo, Ai, Bi, Ao, Bo, Wg1, Wq, Wk, Wv, Wsh, ld

        for M, n in ((M0, "first"), (M1, "second")):
            M.loaded = sem(f"expert_weights_loaded_{n}")
            M.listed = sem(f"tokens_listed_{n}")
            M.gathered = [sem(f"rows_gathered_{n}_{i}") for i in range(4)]
            M.fetched = [sem(f"outputs_fetched_{n}_{t}") for t in range(TT)]

        first_sem = len(sems)
        c_in = sem("cond_x_loaded")
        c_ctx = sem("cond_context_ready")
        c_h1, c_soma, c_gate, c_mod, c_tg, c_out, c_var = (
            sem("cond_" + n) for n in ("hidden_product", "soma_product", "gate_product", "mod_product",
                                       "temporal_product", "out_product", "variance_product"))
        c_act = sem("cond_act_step")
        c_dve = sem("cond_dve_step")
        c_tempo = sem("cond_temporal_ready")
        c_oc, s_x = sem("cond_out_copied"), sem("scan_x_loaded")
        c_tr, c_sum = sem("cond_trace_ready"), sem("cond_trace_added")
        c_sg = sem("cond_soma_gated")
        m_xz, m_dt, m_bc, m_dl = (sem("mix_" + n) for n in ("in_product", "dt_product", "bc_product", "delta_product"))
        m_act = sem("mix_act_step")
        m_dve = sem("mix_dve_step")
        m_conv = sem("mix_conv_ready")
        m_split = sem("mix_bc_split")
        m_abs = sem("mix_delta_magnitude")
        s_b, s_c = sem("scan_b_spread"), sem("scan_c_spread")
        s_da = sem("scan_decay_ready")
        s_bm, s_h = sem("scan_input_ready"), sem("scan_state_ready")
        s_pd = sem("scan_product_ready")
        s_acc = sem("scan_accumulated")
        s_y = sem("scan_y_ready")
        s_yd = sem("scan_y_step")
        s_o = sem("scan_out_product")
        f_id, f_w, f_y, f_ya = (sem("subject_" + n) for n in ("loaded", "weights", "product", "ready"))
        r_lg, r_st, r_ex, r_sel, r_cum = (sem("route_" + n) for n in ("logits", "dve_step", "exp", "selected", "counted"))
        r_tr, r_ra, r_rd, r_out = (sem("route_" + n) for n in ("rows_turned", "rows_copied_act", "rows_copied_dve", "stored"))
        r_pl = sem("route_places_ready")
        h_up, h_si, h_hh, h_dn, h_acc, h_xt, h_st = (sem("shared_" + n) for n in ("up", "silu", "hidden", "down", "accumulated",
                                                                            "x_turned", "stored"))
        t_st, t_tb = (sem("tiles_" + n) for n in ("table_step", "table_ready"))
        e_id = [sem(f"tile_tokens_{i}") for i in range(4)]
        e_o = [sem(f"tile_stored_{i}") for i in range(4)]
        e_hold, e_tx, e_cx, e_up, e_pre, e_act, e_hid, e_th, e_ch, e_dn, e_od = (
            sem("tile_" + n) for n in ("gather_step", "rows_turned", "rows_copied", "up", "biased", "activated", "hidden",
                                       "hidden_turned", "hidden_copied", "down", "out_ready"))
        q_res, q_out = [sem(f"combine_loaded_{r}") for r in range(GR)], sem("combine_out_stored")
        n_row = sem("next_row_found")
        l_wi, l_do, l_wo = sem("l_first_weight_ready"), sem("l_second_product"), sem("l_second_weight_ready")
        q_x, l_id = sem("combine_x_ready"), sem("l_subject_loaded")
        q_pl, q_row, q_ld, q_acc, q_tr, q_st = (sem("combine_" + n) for n in ("places_loaded", "rows_found", "loaded", "summed", "turned", "step"))
        l_w, l_lo, l_h, l_r = (sem("l_" + n) for n in ("lora_loaded", "first_product", "hidden_product",
                                                             "hidden_relu"))
        l_o, l_oc = sem("l_out_product"), sem("l_out_copied")
        a_pj, a_ea = sem("a_projected"), sem("a_copied")
        a_z = sem("a_padding_cleared")
        d_id, d_w, d_z, d_za, d_u, d_y = (sem("d_" + n) for n in ("profile_loaded", "weights", "down_product", "relu",
                                                                 "up_product", "sum_ready"))
        d_mn, d_yc, d_sq, d_var, d_sd, d_st = (sem("d_" + n) for n in ("mean", "centred", "squares", "variance",
                                                                      "deviation", "dve_step"))
        p_s, p_mx, p_ex, p_nm, p_st = (sem("p_" + n) for n in ("scores", "maxima", "exps", "normalised", "dve_step"))
        p_tp, p_ta, p_td, p_pv = (sem("p_" + n) for n in ("turned", "copied_act", "copied_dve", "values"))

        def product(pe, dst, pairs, done=None):
            for i, (lhsT, rhs) in enumerate(pairs):
                last = pe.matmul(dst, lhsT, rhs, start=(i == 0), stop=(i == len(pairs) - 1))
            if done is not None:
                last.then_inc(done, 1)

        def choose(dve, ch, gate_exp, logits, probs, tmp, srt, small, E, K):
            def wide(t):
                return t.unsqueeze(2).to_broadcast([P, TT, E])
            ch.link(dve.tensor_reduce(small[:, 0, :], logits, X, ALU.max))
            dve.tensor_tensor(probs, logits, wide(small[:, 0, :]), ALU.subtract).then_inc(gate_exp, 1)
            dve.wait_ge(gate_exp, 2)
            ch.link(dve.tensor_reduce(small[:, 1, :], probs, X, ALU.add))
            ch.link(dve.reciprocal(small[:, 1, :], small[:, 1, :]))
            ch.link(dve.tensor_tensor(probs, probs, wide(small[:, 1, :]), ALU.mult))
            for t in range(TT):
                ch.step(dve.max(srt[:, t, :], probs[:, t, :]))
            ch.all_but(0)
            kth = srt[:, :, K - 1:K].to_broadcast([P, TT, E])
            ch.link(dve.tensor_tensor(tmp[:, 0], probs, kth, ALU.is_gt))
            ch.link(dve.tensor_tensor(tmp[:, 1], probs, kth, ALU.is_equal))
            ch.link(dve.tensor_reduce(small[:, 2, :], tmp[:, 0], X, ALU.add))
            for t in range(TT):
                ch.step(dve.tensor_tensor_scan(tmp[:, 2, t, :], tmp[:, 1, t, :], tmp[:, 1, t, :], 0.0,
                                               ALU.add, ALU.max))
            ch.all_but(0)

        def list_tokens(pool, M, row):
            for t in range(TT):
                for k in range(M.K):
                    pool.indirect_dma_start(M.list, bass.IndirectOffsetOnAxis(new_pl[:, t, k:k + 1], 0),
                                            new_tok[:, t:t + 1], None).then_inc(M.listed, 16)
            pool.wait_ge(M.listed, row * (16 * TT * M.K) + 16 * TT * M.K)

        def finish_choice(dve, ch, tmp, small, E, K):
            ch.link(dve.tensor_scalar(small[:, 2, :], small[:, 2, :], -1.0, float(K), ALU.mult, ALU.add))
            ch.link(dve.tensor_tensor(tmp[:, 2], tmp[:, 2], small[:, 2, :].unsqueeze(2).to_broadcast([P, TT, E]),
                                      ALU.is_le))
            ch.link(dve.tensor_tensor(tmp[:, 1], tmp[:, 1], tmp[:, 2], ALU.mult))
            ch.link(dve.tensor_tensor(tmp[:, 0], tmp[:, 0], tmp[:, 1], ALU.add))

        def route_tensors(M, st):
            E, K = M.E, M.K
            v = Tensors()
            v.pb = sb("pb", [P, TT, E], scope=st)
            v.lg = sb("lg", [P, TT, E], scope=st)
            v.wgt = sb("wgt", [P, TT, E], scope=st)
            v.tmp = sb("tmp", [P, 3, TT, E], scope=st)
            v.srt = sb("srt", [P, TT, 8], scope=st)
            v.small = sb("small", [P, 4, TT], scope=st)
            v.pl = sb("pl", [P, TT, K], scope=st)
            v.pw = sb("pw", [P, TT, K], scope=st)
            v.rows = sb("rows", [P, TT, D], scope=st)
            return v

        def route_logits(pe, M, bank, src, Wr):
            for t in range(TT):
                product(pe, ps[:, bank, t * M.E:(t + 1) * M.E], [(src[:, k, t * P:(t + 1) * P], Wr[:, k, :])
                                                                 for k in range(DC)], r_lg)

        def turn(pe, bank, src, done):
            for t in range(TT):
                for j in range(DC):
                    pe.transpose(ps[:, bank + t // 2, (t % 2) * D + j * P:(t % 2) * D + (j + 1) * P],
                                 src[:, j, t * P:(t + 1) * P], ident[:, :]).then_inc(done, 1)

        def halves(bank):
            return ps[:, bank, :].rearrange("p (t d) -> p t d", t=2)

        def count_choices(pe, M, v, bank):
            E = M.E
            pe.wait_ge(r_sel, 1)
            for t in range(TT):
                product(pe, ps[:, bank, t * E:(t + 1) * E],
                        [(ones[:, :], v.tmp[:, 0, q, :]) for q in range(t)] + [(tri[:, :], v.tmp[:, 0, t, :])])
            product(pe, ps[:, bank, TT * E:(TT + 1) * E],
                    [(ones[:, :], v.tmp[:, 0, q, :]) for q in range(TT)], r_cum)

        def select(dve, ch, M, v, bank, bias=None):
            E, K = M.E, M.K
            dve.wait_ge(r_lg, TT)
            logits = ps[:, bank, 0:TT * E].rearrange("p (t e) -> p t e", t=TT)
            if bias is not None:
                ch.link(dve.tensor_tensor(v.lg[:, :, :], logits, bias.unsqueeze(1).to_broadcast([P, TT, E]), ALU.add))
                logits = v.lg[:, :, :]
            choose(dve, ch, r_ex, logits, v.pb[:, :, :], v.tmp, v.srt, v.small, E, K)
            finish_choice(dve, ch, v.tmp, v.small, E, K)
            dve.tensor_tensor(v.wgt[:, :, :], v.tmp[:, 0], v.pb[:, :, :], ALU.mult).then_inc(r_sel, 1)

        def renormalise(dve, ch, M, v):
            ch.link(dve.tensor_reduce(v.small[:, 3, :], v.wgt[:, :, :], X, ALU.add))
            ch.link(dve.tensor_scalar(v.small[:, 3, :], v.small[:, 3, :], GATE_EPS, None, ALU.add))
            ch.link(dve.reciprocal(v.small[:, 3, :], v.small[:, 3, :]))
            ch.link(dve.tensor_tensor(v.wgt[:, :, :], v.wgt[:, :, :],
                                      v.small[:, 3, :].unsqueeze(2).to_broadcast([P, TT, M.E]), ALU.mult))

        def place_pairs(dve, ch, M, v, bank, limit=False):
            E, K = M.E, M.K
            base = off[:, 0:E0] if M is M0 else off[:, E0:]
            pb, wgt, tmp, srt, small, pl, pw = v.pb, v.wgt, v.tmp, v.srt, v.small, v.pl, v.pw
            dve.wait_ge(r_cum, 1)
            counts = ps[:, bank, 0:TT * E].rearrange("p (t e) -> p t e", t=TT)
            ch.link(dve.tensor_tensor(tmp[:, 1], counts,
                                      carry[:, 0:E].unsqueeze(1).to_broadcast([P, TT, E]), ALU.add))
            ch.step(dve.tensor_tensor(carry[:, 0:E], carry[:, 0:E], ps[:, bank, TT * E:(TT + 1) * E], ALU.add))
            if limit:
                ch.link(dve.tensor_scalar(tmp[:, 2], tmp[:, 1], float(M.cap), None, ALU.is_le))
                ch.link(dve.tensor_tensor(tmp[:, 0], tmp[:, 0], tmp[:, 2], ALU.mult))
                ch.link(dve.tensor_tensor(wgt[:, :, :], wgt[:, :, :], tmp[:, 2], ALU.mult))
            ch.link(dve.tensor_tensor(tmp[:, 1], tmp[:, 1], base.unsqueeze(1).to_broadcast([P, TT, E]),
                                      ALU.add))
            ch.link(dve.tensor_scalar(tmp[:, 1], tmp[:, 1], -1.0, float(M.none), ALU.mult, ALU.add))
            ch.link(dve.tensor_tensor(tmp[:, 1], tmp[:, 1], tmp[:, 0], ALU.mult))
            for t in range(TT):
                ch.step(dve.max(srt[:, t, :], tmp[:, 1, t, :]))
            ch.all_but(0)
            ch.link(dve.tensor_scalar(pl[:, :, :], srt[:, :, 0:K], -1.0, float(M.none), ALU.mult, ALU.add))
            dve.tensor_copy(new_tok[:, :], tok[:, :]).then_inc(r_pl, 1)
            ch.link(dve.scalar_tensor_tensor(out=pw[:, :, :], in0=pl[:, :, :], scalar=float(M.none),
                                             in1=own[:, :, 0:K], op0=ALU.is_equal, op1=ALU.mult))
            dve.tensor_tensor(new_pl[:, :, 0:K], pl[:, :, :], pw[:, :, :], ALU.add).then_inc(r_pl, 1)
            dve.wait_ge(r_pl, 1)
            ch.step(dve.tensor_scalar(tok[:, :], tok[:, :], float(T), None, ALU.add))
            for k in range(K):
                ch.link(dve.tensor_tensor(tmp[:, 2], tmp[:, 1], srt[:, :, k:k + 1].to_broadcast([P, TT, E]),
                                          ALU.is_equal))
                ch.link(dve.tensor_tensor(tmp[:, 2], tmp[:, 2], wgt[:, :, :], ALU.mult))
                dve.tensor_reduce(pw[:, :, k], tmp[:, 2], X, ALU.add).then_inc(r_pl, 1)
                dve.wait_ge(r_pl, k + 3)

        def store_route(sp, b, M, v, more=()):
            sp.wait_ge(r_ra, 1)
            sp.wait_ge(r_rd, 1)
            sp.dma_start(M.rows.rearrange("(b t p) d -> b p t d", b=B, p=P)[b], v.rows[:, :, :]).then_inc(r_out, 16)
            sp.wait_ge(r_pl, 2 + M.K)
            sp.dma_start(M.place[b], v.pl[:, :, :].rearrange("p t k -> p (t k)")).then_inc(r_out, 16)
            sp.dma_start(M.weight[b], v.pw[:, :, :].rearrange("p t k -> p (t k)")).then_inc(r_out, 16)

        def second_tensors(st):
            v = route_tensors(M1, st)
            v.si = sb("si", [P, ES, T], scope=st)
            v.hh = sb("hh", [P, ES, T], scope=st)
            v.res = sb("res", [P, TT, D], scope=st)
            return v

        def shared_up(pe, e):
            for n in range(2):
                w = Wsh[:, e, n * DC * H1:(n + 1) * DC * H1].rearrange("p (k m) -> p k m", k=DC)
                product(pe, ps[:, 4 + 2 * e + n, :], [(w[:, k, :], ya[:, k, :]) for k in range(DC)], h_up)

        def second_pe(pe, v, part):
            if part == 0:
                route_logits(pe, M1, 7, ya, Wg1)
                turn(pe, 4, ya, r_tr)
            elif part == 1:
                pe.wait_ge(r_ra, 1)
                pe.wait_ge(r_rd, 1)
                shared_up(pe, 0)
            elif part == 2:
                pe.wait_ge(r_ex, 1)
                shared_up(pe, 1)
            elif part == 3:
                pe.wait_ge(h_hh, 1)
                turn(pe, 4, xa, h_xt)
            elif part == 4:
                pe.wait_ge(h_hh, ES)
                count_choices(pe, M1, v, 7)
            else:
                pe.wait_ge(h_st, 2)
                for t in range(TT):
                    product(pe, ps[:, 4 + t // 2, (t % 2) * D:(t % 2 + 1) * D],
                            [(v.hh[:, e, t * P:(t + 1) * P], Wsh[:, e, 2 * DC * H1:]) for e in range(ES)], h_dn)

        def second_act(act, v, part):
            if part == 0:
                act.wait_ge(r_ex, 1)
                act.activation(v.pb[:, :, :], v.pb[:, :, :], ACT.Exp).then_inc(r_ex, 1)
                act.wait_ge(r_tr, TT * DC)
                act.activation(v.rows[:, 0:2, :], halves(4), ACT.Copy).then_inc(r_ra, 1)
                act.activation(v.rows[:, 2:4, :], halves(5), ACT.Copy).then_inc(r_rd, 1)
            elif part <= ES:
                e = part - 1
                act.wait_ge(h_up, 2 * e + 1)
                act.activation(v.si[:, e, :], ps[:, 4 + 2 * e, :], ACT.Silu).then_inc(h_si, 1)
            else:
                act.wait_ge(h_xt, TT * DC)
                for i in range(2):
                    act.activation(v.res[:, 2 * i:2 * i + 2, :], halves(4 + i), ACT.Copy).then_inc(h_st, 1)

        def second_dve(dve, v):
            ch = Chain(dve, r_st)
            select(dve, ch, M1, v, 7)
            for e in range(ES):
                dve.wait_ge(h_si, e + 1)
                dve.wait_ge(h_up, 2 * e + 2)
                dve.tensor_tensor(v.hh[:, e, :], v.si[:, e, :], ps[:, 5 + 2 * e, :], ALU.mult).then_inc(h_hh, 1)
            place_pairs(dve, ch, M1, v, 7, limit=True)
            for i in range(2):
                dve.wait_ge(h_dn, 2 * i + 2)
                dve.tensor_tensor(v.res[:, 2 * i:2 * i + 2, :], v.res[:, 2 * i:2 * i + 2, :], halves(4 + i),
                                  ALU.add).then_inc(h_acc, 1)

        def second_store(sp, b, v):
            store_route(sp, b, M1, v)
            sp.wait_ge(h_acc, 2)
            sp.dma_start(resd[b], v.res[:, :, :]).then_inc(r_out, 16)
            sp.wait_ge(r_out, 64)

        def route_second_last(b):
            with ExitStack() as st:
                v = second_tensors(st)
                with nc.Block() as block:
                    @block.tensor
                    def _(pe):
                        for part in range(6):
                            second_pe(pe, v, part)

                    @block.scalar
                    def _(act):
                        for part in range(4):
                            second_act(act, v, part)

                    @block.vector
                    def _(dve):
                        second_dve(dve, v)

                    @block.sync
                    def _(sp):
                        second_store(sp, b, v)

        def subject_product(pe):
            for j in range(DC):
                product(pe, ps[:, 6 + j, :], [(ws[:, k * D + j * P:k * D + (j + 1) * P], xm[:, k, :]) for k in range(DC)],
                        f_y)

        def subject_bias(act, ys):
            for j in range(DC):
                act.wait_ge(f_y, j + 1)
                act.activation(ys[:, j, :], ps[:, 6 + j, :], ACT.Identity,
                               bias=ws[:, DC * D + j:DC * D + j + 1]).then_inc(f_ya, 1)

        def route_exp(act, v, bank):
            act.wait_ge(r_ex, 1)
            act.activation(v.pb[:, :, :], v.pb[:, :, :], ACT.Exp, scale=1.0 / TEMP).then_inc(r_ex, 1)
            act.wait_ge(r_tr, TT * DC)
            act.activation(v.rows[:, 0:2, :], halves(bank), ACT.Copy).then_inc(r_ra, 1)
            act.activation(v.rows[:, 2:4, :], halves(bank + 1), ACT.Copy).then_inc(r_rd, 1)

        def route_pe(pe, n, v, beside):
            if n == 0:
                subject_product(pe)
            elif n == 2:
                pe.wait_ge(f_ya, DC)
                if beside:
                    pe.wait_ge(c_act, 2)
                route_logits(pe, M0, 7, v.ys, Wg0)
            elif n == 3:
                pe.wait_ge(r_ex, 1)
                if beside:
                    pe.wait_ge(c_act, 3)
                turn(pe, 6, v.ys, r_tr)
            elif n == 4:
                pe.wait_ge(r_ra, 1)
                count_choices(pe, M0, v, 6)

        def route_act(act, n, v):
            if n == 0:
                subject_bias(act, v.ys)
            elif n == 3:
                route_exp(act, v, 6)

        def route_dve(dve, n, v, ch):
            if n == 3:
                select(dve, ch, M0, v, 7, bg0[:, :])
                dve.wait_ge(r_sel, 1)
                renormalise(dve, ch, M0, v)
            elif n == 5:
                place_pairs(dve, ch, M0, v, 6)

        def cond_tensors(st, scope_tempo=None, scope_out=None):
            c = Tensors()
            c.cx = sb("cx", [P, DC, T], scope=st)
            c.soma = sb("soma", [P, DC, T], scope=st)
            c.wg = sb("wg", [P, DC, T], scope=st)
            c.gated = sb("gated", [P, DC, T], scope=st)
            c.mod = sb("mod", [P, NTR, T], scope=st)
            c.gm = sb("gm", [P, DC, T], scope=st)
            tr = sb("tr", [P, 2, DC, T], scope=st)
            c.tr = [tr[:, 0], tr[:, 1], c.mod[:, 0:2, :], c.mod[:, 2:4, :]]
            c.tempo = scope_tempo if scope_tempo is not None else sb("tempo", [P, DC, T], scope=st)
            c.oc = scope_out if scope_out is not None else sb("oc", [P, DC, T], scope=st)
            c.tg, c.sg, c.sq = c.wg, c.gated, c.gm
            c.std, c.rstd = c.cx[:, 0, :], c.cx[:, 1, :]
            return c

        def cond_pe(pe, n, c, routed):
            if n == 1:
                pe.wait_ge(c_in, 16)
                if routed:
                    pe.wait_ge(f_ya, DC)
                product(pe, ps[0:HN, 6, :], [(Wn1[:, k, :], x[:, k, :]) for k in range(DC)], c_h1)
                product(pe, ps[:, 7, :], [(Wsoma[:, k, 0:P], x[:, k, :]) for k in range(DC)], c_soma)
            elif n == 2:
                pe.wait_ge(c_act, 1)
                product(pe, ps[:, 6, :], [(Wsoma[:, k, P:2 * P], x[:, k, :]) for k in range(DC)], c_soma)
            elif n in (4, 5):
                pe.wait_ge(c_ctx, DC)
                pe.wait_ge(c_act, 2 if n == 4 else 4)
                if routed:
                    pe.wait_ge(r_rd, 1)
                j = n - 4
                product(pe, ps[:, 7, :],
                        [(Wg[:, k, j * P:(j + 1) * P], x[:, k, :]) for k in range(DC)]
                        + [(Wg[:, DC + k, j * P:(j + 1) * P], c.cx[:, k, :]) for k in range(DC)], c_gate)
            elif n in (6, 7):
                for d in range(4 * (n - 6), 4 * (n - 5)):
                    if d == 0:
                        pe.wait_ge(c_act, 3)
                        if routed:
                            pe.wait_ge(r_pl, 1)
                    else:
                        pe.wait_ge(c_act, d + 4)
                    product(pe, ps[:, 6 + d % 2, :], [(Wn2r[:, d, :], h1[:, :])], c_mod)
            elif n in (8, 9, 10, 11):
                pe.wait_ge(c_act, 5 + NTR)
                for d in (2 * (n - 8), 2 * (n - 8) + 1):
                    pe.wait_ge(c_tr, d + 1)
                    for j in range(DC):
                        ins = pe.matmul(ps[:, 6 + j, :], mix[:, j, d, :], c.tr[d % 4][:, j, :],
                                        start=(d == 0), stop=(d == NTR - 1))
                    ins.then_inc(c_sum, 1)
            elif n == 12:
                pe.wait_ge(c_tempo, DC)
                for j in range(DC):
                    product(pe, ps[:, 6 + j, :], [(Wtemp[:, k, j * P:(j + 1) * P], c.tempo[:, k, :])
                                                  for k in range(DC)], c_tg)
            elif n == 14:
                pe.wait_ge(c_sg, DC)
                for j in range(DC):
                    product(pe, ps[:, 6 + j, :], [(WoutC[:, k, j * P:(j + 1) * P], c.sg[:, k, :])
                                                  for k in range(DC)], c_out)
            elif n == NS:
                pe.wait_ge(c_act, 5 + NTR + DC + DC)
                pe.wait_ge(c_oc, DC)
                product(pe, ps[:, 6, :], [(mean[:, :], c.sq[:, k, :]) for k in range(DC)], c_var)

        def cond_act(act, n, c, routed):
            if n == 1:
                act.wait_ge(c_h1, 1)
                act.activation(h1[0:HN, :], ps[0:HN, 6, :], ACT.Gelu, bias=bn1[0:HN, :]).then_inc(c_act, 1)
            if n in (1, 2):
                j = n - 1
                act.wait_ge(c_soma, j + 1)
                act.activation(c.soma[:, j, :], ps[:, 7 - j, :], ACT.Gelu, bias=bsoma[:, j:j + 1]).then_inc(c_act, 1)
            elif n in (4, 5):
                j = n - 4
                act.wait_ge(c_gate, j + 1)
                act.activation(c.wg[:, j, :], ps[:, 7, :], ACT.Sigmoid, bias=bg[:, j:j + 1]).then_inc(c_act, 1)
            elif n in (6, 7):
                for d in range(4 * (n - 6), 4 * (n - 5)):
                    act.wait_ge(c_mod, d + 1)
                    act.activation(c.mod[:, d, :], ps[:, 6 + d % 2, :], ACT.Sigmoid,
                                   bias=bn2[:, d:d + 1]).then_inc(c_act, 1)
            elif n == 11:
                act.wait_ge(c_sum, NTR)
                for j in range(DC):
                    act.activation(c.tempo[:, j, :], ps[:, 6 + j, :], ACT.Copy).then_inc(c_tempo, 1)
            elif n == 12:
                for j in range(DC):
                    act.wait_ge(c_tg, j + 1)
                    act.activation(c.tg[:, j, :], ps[:, 6 + j, :], ACT.Sigmoid, bias=btemp[:, j:j + 1]).then_inc(c_act, 1)
            elif n == 14:
                if routed:
                    act.wait_ge(r_out, 64)
                for j in range(DC):
                    act.wait_ge(c_out, j + 1)
                    act.activation(c.oc[:, j, :], ps[:, 6 + j, :], ACT.Copy).then_inc(c_oc, 1)
                    act.activation(c.sq[:, j, :], ps[:, 6 + j, :], ACT.Square).then_inc(c_act, 1)
            elif n == NS:
                act.wait_ge(c_var, 1)
                act.activation(c.std, ps[:, 6, :], ACT.Sqrt, bias=epst[:, :]).then_inc(c_act, 1)

        def cond_dve(dve, n, c, ch):
            if n == 1:
                dve.wait_ge(c_in, 16)
                for j in range(DC):
                    dve.tensor_tensor_scan(c.cx[:, j, :], alpha[:, NTR:NTR + 1].to_broadcast([P, T]), x[:, j, :],
                                           0.0, ALU.mult, ALU.add).then_inc(c_ctx, 1)
            elif n == 6:
                dve.wait_ge(c_act, 3 + DC)
                ch.step(dve.tensor_tensor(c.gated[:, :, :], x[:, :, :], c.wg[:, :, :], ALU.mult))
            elif n in (7, 8, 9, 10):
                for d in (2 * (n - 7), 2 * (n - 7) + 1):
                    dve.wait_ge(c_act, 5 + d + 1)
                    ch.all_but(0)
                    if d:
                        dve.wait_ge(c_tr, d)
                    ch.link(dve.scalar_tensor_tensor(out=c.gm[:, :, :],
                                                     in0=c.mod[:, d, :].unsqueeze(1).to_broadcast([P, DC, T]),
                                                     scalar=0.5, in1=c.gated[:, :, :], op0=ALU.add, op1=ALU.mult))
                    if d >= 4:
                        dve.wait_ge(c_sum, d - 3)
                    for j in range(DC):
                        ins = dve.tensor_tensor_scan(c.tr[d % 4][:, j, :], alpha[:, d:d + 1].to_broadcast([P, T]),
                                                     c.gm[:, j, :], 0.0, ALU.mult, ALU.add)
                        if j < DC - 1:
                            ch.step(ins)
                    ins.then_inc(c_tr, 1)
            elif n == 13:
                dve.wait_ge(c_act, 5 + NTR + DC)
                dve.wait_ge(c_tr, NTR)
                for j in range(DC):
                    dve.tensor_tensor(c.sg[:, j, :], c.soma[:, j, :], c.tg[:, j, :], ALU.mult).then_inc(c_sg, 1)

        def cond_norm(dve, c, ch):
            dve.wait_ge(c_act, 5 + NTR + 2 * DC + 1)
            dve.wait_ge(c_oc, DC)
            ch.link(dve.reciprocal(c.rstd, c.std))
            for j in range(DC):
                ch.step(dve.scalar_tensor_tensor(out=y[:, j, :], in0=c.oc[:, j, :], scalar=gamma[:, j:j + 1],
                                                 in1=c.rstd, op0=ALU.mult, op1=ALU.mult))
            for j in range(DC):
                ch.all_but(1)
                ch.step(dve.tensor_scalar(y[:, j, :], y[:, j, :], beta[:, j:j + 1], None, ALU.add))

        def conditioner_first():
            with ExitStack() as st:
                c = cond_tensors(st)
                with nc.Block() as block:
                    @block.sync
                    def _(sp):
                        sp.dma_start(x[:, :, :], a["x"][0]).then_inc(c_in, 16)

                    @block.tensor
                    def _(pe):
                        for n in range(NS + 1):
                            cond_pe(pe, n, c, False)

                    @block.scalar
                    def _(act):
                        for n in range(NS + 1):
                            cond_act(act, n, c, False)

                    @block.vector
                    def _(dve):
                        ch = Chain(dve, c_dve)
                        for n in range(NS):
                            cond_dve(dve, n, c, ch)
                        cond_norm(dve, c, ch)

        def load_experts(sp, M, loads):
            for dst, src in loads:
                sp.dma_start(dst, src).then_inc(M.loaded, 16)

        def route_last(b, loads):
            M = M0
            with ExitStack() as st:
                v = route_tensors(M, st)
                v.ys = sb("ys", [P, DC, T], scope=st)
                with nc.Block() as block:
                    @block.sync
                    def _(sp):
                        sp.dma_start(x1d[b], xm[:, :, :]).then_inc(r_out, 16)
                        load_experts(sp, M, loads)
                        store_route(sp, b, M, v)
                        sp.wait_ge(r_out, 64)

                    @block.tensor
                    def _(pe):
                        for n in range(5):
                            route_pe(pe, n, v, False)

                    @block.scalar
                    def _(act):
                        for n in range(4):
                            route_act(act, n, v)

                    @block.vector
                    def _(dve):
                        rt = Chain(dve, r_st)
                        for n in range(6):
                            route_dve(dve, n, v, rt)

        def mixer(b, behind, before):
            with ExitStack() as st:
                xs = sb("xs", [P, JI, T], scope=st)
                sz = sb("sz", [P, JI, T], scope=st)
                dl = sb("dl", [P, JI, T], scope=st)
                u = sb("u", [P, JI, T], scope=st)
                bc = sb("bc", [96, T], BF16, scope=st)
                with ExitStack() as st1:
                    cv = sb("cv", [P, JI, T], scope=st1)
                    r1 = sb("r1", [P, T], scope=st1)
                    pre = sb("pre", [P, JI, T], scope=st1)
                    ab = sb("ab", [P, JI, T], scope=st1)
                    with nc.Block() as block:
                        @block.tensor
                        def _(pe):
                            for j in range(2 * JI):
                                product(pe, ps[:, j, :], [(Win[:, k, j * P:(j + 1) * P], y[:, k, :]) for k in range(DC)],
                                        m_xz)
                            pe.wait_ge(m_act, 3 * JI)
                            product(pe, ps[0:DTR, 0, :], [(Wxd[:, k, :], xs[:, k, :]) for k in range(JI)], m_dt)
                            product(pe, ps[0:96, 1, :], [(Wxbc[:, k, :, :].rearrange("p a b -> p (a b)"), xs[:, k, :])
                                                         for k in range(JI)], m_bc)
                            pe.wait_ge(m_act, 3 * JI + 1)
                            for j in range(JI):
                                product(pe, ps[:, 2 + j, :], [(Wdt[:, j * P:(j + 1) * P], dts[:, :])], m_dl)

                        @block.scalar
                        def _(act):
                            for j in range(JI):
                                act.wait_ge(m_xz, j + 1)
                                act.activation(cv[:, j, :], ps[:, j, :], ACT.Identity, bias=convb[:, j:j + 1],
                                               scale=cw[:, j, 3:4]).then_inc(m_act, 1)
                            for j in range(JI):
                                act.wait_ge(m_xz, JI + j + 1)
                                act.activation(sz[:, j, :], ps[:, JI + j, :], ACT.Silu).then_inc(m_act, 1)
                            for j in range(JI):
                                act.wait_ge(m_conv, j + 1)
                                act.activation(xs[:, j, :], cv[:, j, :], ACT.Silu).then_inc(m_act, 1)
                            act.wait_ge(m_dt, 1)
                            act.activation(dts[0:DTR, :], ps[0:DTR, 0, :], ACT.Copy).then_inc(m_act, 1)
                            for j in range(JI):
                                act.wait_ge(m_dl, j + 1)
                                act.activation(ab[:, j, :], ps[:, 2 + j, :], ACT.Abs, bias=bdt[:, j:j + 1]).then_inc(m_abs, 1)
                            act.wait_ge(m_abs, JI)
                            act.activation(ab[:, :, :], ab[:, :, :], ACT.Exp, scale=-1.0).then_inc(m_act, 1)
                            act.wait_ge(m_act, 3 * JI + 2)
                            act.activation(ab[:, :, :], ab[:, :, :], ACT.Ln, bias=1.0).then_inc(m_act, 1)

                        @block.vector
                        def _(dve):
                            ch = Chain(dve, m_dve)
                            for j0 in range(0, JI, 2):
                                dve.wait_ge(m_act, j0 + 2)
                                for s in (1, 2, 3):
                                    for j in (j0, j0 + 1):
                                        ch.all_but(1 if s < 3 or j == j0 else 0)
                                        ins = dve.scalar_tensor_tensor(
                                            out=cv[:, j, s:T], in0=ps[:, j, 0:T - s], scalar=cw[:, j, 3 - s:4 - s],
                                            in1=cv[:, j, s:T], op0=ALU.mult, op1=ALU.add)
                                        if s < 3:
                                            ch.step(ins)
                                        else:
                                            ins.then_inc(m_conv, 1)
                            dve.wait_ge(m_bc, 1)
                            ch.link(dve.tensor_copy(bc[:, :], ps[0:96, 1, :]))
                            ch.link(dve.tensor_tensor(r1[0:96, :], ps[0:96, 1, :], bc[:, :], ALU.subtract))
                            ch.step(dve.tensor_copy(bc[32:64, :], r1[32:64, :]))
                            ch.link(dve.tensor_copy(bc[64:96, :], r1[64:96, :]))
                            ch.link(dve.tensor_tensor(r1[64:96, :], r1[64:96, :], bc[64:96, :], ALU.subtract))
                            dve.tensor_copy(bc[64:96, :], r1[64:96, :]).then_inc(m_split, 1)
                            for j in range(JI):
                                dve.wait_ge(m_abs, j + 1)
                                ins = dve.tensor_scalar(pre[:, j, :], ps[:, 2 + j, :], bdt[:, j:j + 1], None, ALU.add)
                                ch.step(ins)
                            ch.all_but(0)
                            dve.wait_ge(m_act, 3 * JI + 3)
                            ch.link(dve.scalar_tensor_tensor(out=dl[:, :, :], in0=pre[:, :, :], scalar=0.0,
                                                             in1=ab[:, :, :], op0=ALU.max, op1=ALU.add))
                            ch.step(dve.tensor_tensor(u[:, :, :], dl[:, :, :], xs[:, :, :], ALU.mult))
                with ExitStack() as st2:
                    dA = sb("dA", [P, 2, JI, T], scope=st2)
                    hs = sb("hs", [P, 2, JI, T], scope=st2)
                    pr = sb("pr", [P, 2, JI, T], scope=st2)
                    v = c = None
                    if before is not None:
                        v = route_tensors(M0, st2)
                        v.ys = sb("ys", [P, DC, T], scope=st2)
                    if behind is not None:
                        c = cond_tensors(st2, v and v.ys, v and v.rows[:, :, :].rearrange("p t d -> p (t d)").rearrange(
                            "p (c t) -> p c t", c=DC))
                    with nc.Block() as block:
                        @block.sync
                        def _(sp):
                            if c:
                                sp.dma_start(x[:, :, :], a["x"][behind]).then_inc(c_in, 16)
                            if v:
                                sp.dma_start(x1d[before], xm[:, :, :]).then_inc(r_out, 16)
                                sp.wait_ge(r_out, 16)
                                sp.wait_ge(f_ya, DC)
                            sp.dma_start(xm[:, :, :], a["x"][b]).then_inc(s_x, 16)
                            sp.dma_start(ids[0:1, 0:1], a["subject"][b]).then_inc(f_id, 16)
                            sp.wait_ge(f_id, 16)
                            subject = sp.value_load(ids[0:1, 0:1], min_val=0, max_val=7)
                            sp.dma_start(ws[:, :], a["Wsub"][subject]).then_inc(f_w, 16)
                            if v:
                                store_route(sp, before, M0, v)
                                sp.wait_ge(r_out, 64)
                            sp.wait_ge(f_w, 16)

                        @block.gpsimd
                        def _(pool):
                            if v:
                                pool.wait_ge(r_pl, 2)
                                list_tokens(pool, M0, before)

                        @block.tensor
                        def _(pe):
                            def spread_b(n):
                                if n:
                                    pe.wait_ge(s_bm, n)
                                pe.matmul(ps[:, 4, :], sel[:, n, :], bc[:, :], start=True, stop=True).then_inc(s_b, 1)

                            def spread_c(n):
                                if n:
                                    pe.wait_ge(s_pd, n)
                                pe.matmul(ps[:, 5, :], sel[:, NS + n, :], bc[:, :], start=True,
                                          stop=True).then_inc(s_c, 1)

                            def add_up(n):
                                pe.wait_ge(s_pd, n + 1)
                                for j in range(JI):
                                    ins = pe.matmul(ps[:, j, :], ident[:, :], pr[:, n % 2, j, :],
                                                    start=(n == 0), stop=(n == NS - 1))
                                ins.then_inc(s_acc, 1)

                            spread_b(0)
                            spread_c(0)
                            spread_b(1)
                            for n in range(NS):
                                if n + 2 < NS:
                                    spread_b(n + 2)
                                if c and n != 4:
                                    cond_pe(pe, n, c, v is not None)
                                if v:
                                    route_pe(pe, n, v, c is not None)
                                if c and n == 4:
                                    cond_pe(pe, n, c, v is not None)
                                if n + 1 < NS:
                                    spread_c(n + 1)
                                add_up(n)
                            if c:
                                cond_pe(pe, NS, c, v is not None)
                            pe.wait_ge(s_y, JI)
                            for j in range(DC):
                                product(pe, ps[:, 4 + j, :], [(Wo[:, k, j * P:(j + 1) * P], u[:, k, :])
                                                              for k in range(JI)], s_o)

                        @block.scalar
                        def _(act):
                            def decays(n):
                                if n >= 2:
                                    act.wait_ge(s_h, n - 1)
                                for j in range(JI):
                                    act.activation(dA[:, n % 2, j, :], dl[:, j, :], ACT.Exp,
                                                   scale=An[:, j, n:n + 1]).then_inc(s_da, 1)

                            decays(0)
                            decays(1)
                            for n in range(NS):
                                if n + 2 < NS:
                                    decays(n + 2)
                                if v:
                                    route_act(act, n, v)
                                if c:
                                    cond_act(act, n, c, v is not None)
                            if c:
                                cond_act(act, NS, c, v is not None)

                        @block.vector
                        def _(dve):
                            cc, rt = Chain(dve, c_dve), Chain(dve, r_st)

                            def into(n):
                                dve.wait_ge(s_b, n + 1)
                                if n >= 2:
                                    dve.wait_ge(s_pd, n - 1)
                                dve.tensor_tensor(hs[:, n % 2], u[:, :, :],
                                                  ps[:, 4, :].unsqueeze(1).to_broadcast([P, JI, T]),
                                                  ALU.mult).then_inc(s_bm, 1)

                            def scan(n):
                                dve.wait_ge(s_da, JI * (n + 1))
                                dve.wait_ge(s_bm, n + 1)
                                for j in range(JI):
                                    ins = dve.tensor_tensor_scan(hs[:, n % 2, j, :], dA[:, n % 2, j, :],
                                                                 hs[:, n % 2, j, :], 0.0, ALU.mult, ALU.add)
                                ins.then_inc(s_h, 1)

                            def out(n):
                                dve.wait_ge(s_h, n + 1)
                                dve.wait_ge(s_c, n + 1)
                                if n >= 2:
                                    dve.wait_ge(s_acc, n - 1)
                                dve.tensor_tensor(pr[:, n % 2], hs[:, n % 2],
                                                  ps[:, 5, :].unsqueeze(1).to_broadcast([P, JI, T]),
                                                  ALU.mult).then_inc(s_pd, 1)

                            into(0)
                            for n in range(NS):
                                scan(n)
                                if n >= 1:
                                    out(n - 1)
                                if n + 1 < NS:
                                    into(n + 1)
                                if v:
                                    route_dve(dve, n, v, rt)
                                if c:
                                    cond_dve(dve, n, c, cc)
                            out(NS - 1)
                            dve.wait_ge(s_acc, NS)
                            ch = Chain(dve, s_yd)
                            for j in range(JI):
                                ch.step(dve.scalar_tensor_tensor(out=pr[:, 0, j, :], in0=xs[:, j, :],
                                                                 scalar=Dv[:, j:j + 1], in1=ps[:, j, :],
                                                                 op0=ALU.mult, op1=ALU.add))
                            dve.wait_ge(s_bm, NS)
                            for j in range(JI):
                                dve.wait_ge(s_yd, j + 1)
                                dve.tensor_tensor(u[:, j, :], pr[:, 0, j, :], sz[:, j, :], ALU.mult).then_inc(s_y, 1)
                            if c:
                                cond_norm(dve, c, cc)
                            dve.wait_ge(s_x, 16)
                            for j in range(DC):
                                dve.wait_ge(s_o, j + 1)
                                ch.step(dve.tensor_tensor(xm[:, j, :], xm[:, j, :], ps[:, 4 + j, :], ALU.add))

        def experts(M, wu, wd, loads, biases=None):
            E, NT = M.E, M.tiles
            width = wu.shape[3]
            JK = wd.shape[2]
            with ExitStack() as st:
                nt = sb("nt", [P, E], scope=st)
                cmpn = sb("cmpn", [P, E, M.region // P], scope=st)
                ends = sb("ends", [P, E], scope=st)
                le = sb("le", [1, NT, E], BF16, scope=st)
                ti = sb("ti", [1, 4, NT], scope=st)
                with nc.Block() as block:
                    @block.sync
                    def _(sp):
                        sp.wait_ge(M.loaded, 16 * len(loads))

                    @block.gpsimd
                    def _(pool):
                        list_tokens(pool, M, B - 1 if M is M0 else B)

                    @block.vector
                    def _(dve):
                        ch = Chain(dve, t_st)
                        J = M.region // P
                        ch.link(dve.tensor_tensor(cmpn[:, :, :], carry[:, 0:E].unsqueeze(2).to_broadcast([P, E, J]),
                                                  steps[:, 0:J].unsqueeze(1).to_broadcast([P, E, J]), ALU.is_gt))
                        ch.link(dve.tensor_reduce(nt[:, :], cmpn[:, :, :], X, ALU.add))
                        ch.link(dve.tensor_tensor_scan(ends[:, :], nt[:, :], nt[:, :], 0.0, ALU.add, ALU.max))
                        ch.link(dve.tensor_tensor(le[:, :, :], ends[0:1, :].unsqueeze(1).to_broadcast([1, NT, E]),
                                                  tile_no[0:1, 0:NT].unsqueeze(2).to_broadcast([1, NT, E]), ALU.is_le))
                        ch.link(dve.tensor_reduce(ti[:, 0, :], le[:, :, :], X, ALU.add))
                        ch.link(dve.tensor_tensor(le[:, :, :], le[:, :, :],
                                                  nt[0:1, :].unsqueeze(1).to_broadcast([1, NT, E]), ALU.mult))
                        ch.link(dve.tensor_reduce(ti[:, 1, :], le[:, :, :], X, ALU.add))
                        ch.link(dve.tensor_tensor(ti[:, 1, :], tile_no[0:1, 0:NT], ti[:, 1, :], ALU.subtract))
                        ch.link(dve.tensor_scalar(ti[:, 2, :], ti[:, 0, :], float(E), None, ALU.is_equal))
                        ch.link(dve.tensor_scalar(ti[:, 1, :], ti[:, 1, :], float(P), None, ALU.mult))
                        ch.link(dve.scalar_tensor_tensor(out=ti[:, 1, :], in0=ti[:, 0, :], scalar=float(M.region),
                                                         in1=ti[:, 1, :], op0=ALU.mult, op1=ALU.add))
                        ch.link(dve.tensor_tensor(ti[:, 0, :], ti[:, 0, :], ti[:, 2, :], ALU.subtract))
                        ch.step(dve.tensor_scalar(closer[:, 1:E], nt[:, 0:E - 1], float(P), -float(M.region),
                                                  ALU.mult, ALU.add))
                        ch.step(dve.memset(closer[:, 0:1], 0.0))
                        dve.tensor_copy(tab_e[:, 0:NT], ti[:, 0, :]).then_inc(t_tb, 1)
                        dve.tensor_copy(tab_r[:, 0:NT], ti[:, 1, :]).then_inc(t_tb, 1)

            with ExitStack() as st:
                idt = sb("idt", [P, 4], I32, scope=st)
                hold = sb("hold", [1, 1], scope=st)
                xg = sb("xg", [P, 4, D], scope=st)
                xT = sb("xT", [P, 2, D], scope=st)
                pre = sb("pre", [P, 2, width], scope=st)
                hd = sb("hd", [P, 2, JK * P], scope=st)
                hT = sb("hT", [P, 2, JK * P], scope=st)
                og = sb("og", [P, 4, D], scope=st)

                def pipeline(eng, last, look, *stages):
                    lead = 8
                    back = max([lag for lag, stage in stages if look and lag <= 4], default=0)
                    for k0 in range(0, lead, 4):
                        entry = look(k0, -min(k0, back), 4) if look else {}
                        for k in range(k0, k0 + 4):
                            for lag, stage in stages:
                                if k >= lag:
                                    stage(k - lag, (k - lag) // 4, (k - lag) % 4, entry.get(k - k0 - lag))
                    with eng.Fori(lead // 4, NT // 4) as i:
                        entry = look(i * 4, -back, 4) if look else {}
                        for g in range(4):
                            for lag, stage in stages:
                                stage(i * 4 + (g - lag), i + (g - lag) // 4, (g - lag) % 4, entry.get(g - lag))
                    entry = look(NT, -back, 0) if look and back else {}
                    for k in range(NT, NT + last):
                        for lag, stage in stages:
                            if k - lag < NT:
                                stage(k - lag, (k - lag) // 4, (k - lag) % 4, entry.get(k - NT - lag))

                def reuse(eng, s, value):
                    if not isinstance(value, int) or value > 0:
                        eng.wait_ge(s, value)

                def reader(eng, table, most):
                    regs = [eng.alloc_register(f"entry_{i}_{E}") for i in range(8)]

                    def look(k, low, high):
                        eng.reg_load(regs[4 + low:4 + high], table[0:1, bass.ds(k + low, high - low)])
                        return {o: eng.snap(regs[4 + o], min_val=0, max_val=most)
                                for o in range(low, high)}
                    return look

                gated = biases is None
                up_read = e_hid if gated else e_pre
                with nc.Block() as block:
                    @block.sync
                    def _(sp):
                        def load(t, r, s, _):
                            reuse(sp, M.gathered[s], r * 16)
                            row = sp.value_load(tab_r[0:1, bass.ds(t, 1)], min_val=0, max_val=M.none - P)
                            sp.dma_start(idt[:, s:s + 1], M.list[bass.ds(row, P), :]).then_inc(e_id[s], 16)

                        def store(t, r, s, _):
                            sp.wait_ge(e_od, t + 1)
                            sp.dma_start(M.outs[bass.ds(t * P, P), :], og[:, s, :]).then_inc(e_o[s], 16)

                        pipeline(sp, 8, None, (0, load), (8, store))
                        for s in range(4):
                            sp.wait_ge(e_o[s], 16 * (NT // 4))

                    @block.gpsimd
                    def _(pool):
                        def gather(t, r, s, _):
                            pool.wait_ge(e_id[s], r * 16 + 16)
                            reuse(pool, e_tx, t - 3)
                            pool.wait_ge(e_hold, t + 1)
                            pool.tensor_tensor(hold[:, :], hold[:, :], hold[:, :], ALU.mult).then_inc(e_hold, 1)
                            pool.indirect_dma_start(xg[:, s, :], None, M.rows,
                                                    bass.IndirectOffsetOnAxis(idt[:, s:s + 1], 0)).then_inc(M.gathered[s], 16)

                        pool.memset(hold[:, :], 0.0).then_inc(e_hold, 1)
                        pipeline(pool, 0, None, (0, gather))

                    @block.tensor
                    def _(pe):
                        def turn_rows(t, r, s, _):
                            pe.wait_ge(M.gathered[s], r * 16 + 16)
                            reuse(pe, e_cx, t - 1)
                            for j in range(DC):
                                ins = pe.transpose(ps[:, s % 2, j * P:(j + 1) * P], xg[:, s, j * P:(j + 1) * P], ident[:, :])
                            ins.then_inc(e_tx, 1)

                        def up(t, r, s, e):
                            pe.wait_ge(e_cx, t + 1)
                            reuse(pe, up_read, t - 1)
                            product(pe, ps[:, 2 + s % 2, 0:width], [(xT[:, s % 2, k * P:(k + 1) * P], wu[:, e, k, :])
                                                                    for k in range(DC)], e_up)

                        def turn_hidden(t, r, s, _):
                            pe.wait_ge(e_hid, t + 1)
                            reuse(pe, e_ch, t - 1)
                            for j in range(JK):
                                ins = pe.transpose(ps[:, 4 + s % 2, j * P:(j + 1) * P], hd[:, s % 2, j * P:(j + 1) * P],
                                                   ident[:, :])
                            ins.then_inc(e_th, 1)

                        def down(t, r, s, e):
                            pe.wait_ge(e_ch, t + 1)
                            reuse(pe, e_od, t - 1)
                            product(pe, ps[:, 6 + s % 2, 0:D], [(hT[:, s % 2, j * P:(j + 1) * P], wd[:, e, j, :])
                                                                for j in range(JK)], e_dn)

                        pipeline(pe, 4, reader(pe, tab_e, E - 1), (0, turn_rows), (1, up), (3, turn_hidden), (4, down))

                    @block.scalar
                    def _(act):
                        def copy_rows(t, r, s, _):
                            act.wait_ge(e_tx, t + 1)
                            reuse(act, e_up, t - 1)
                            act.activation(xT[:, s % 2, :], ps[:, s % 2, 0:D], ACT.Copy).then_inc(e_cx, 1)

                        def silu(t, r, s, _):
                            act.wait_ge(e_up, t + 1)
                            reuse(act, e_hid, t - 1)
                            act.activation(pre[:, s % 2, 0:H1], ps[:, 2 + s % 2, 0:H1], ACT.Silu).then_inc(e_act, 1)

                        def gelu(t, r, s, _):
                            act.wait_ge(e_pre, t + 1)
                            reuse(act, e_th, t - 1)
                            act.activation(hd[:, s % 2, :], pre[:, s % 2, :], ACT.Gelu).then_inc(e_hid, 1)

                        def copy_hidden(t, r, s, _):
                            act.wait_ge(e_th, t + 1)
                            reuse(act, e_dn, t - 1)
                            act.activation(hT[:, s % 2, :], ps[:, 4 + s % 2, 0:JK * P], ACT.Copy).then_inc(e_ch, 1)

                        pipeline(act, 3, None, (0, copy_rows), (1, silu if gated else gelu), (3, copy_hidden))

                    @block.vector
                    def _(dve):
                        def gate(t, r, s, _):
                            dve.wait_ge(e_act, t + 1)
                            reuse(dve, e_th, t - 1)
                            dve.tensor_tensor(hd[:, s % 2, :], pre[:, s % 2, 0:H1], ps[:, 2 + s % 2, H1:2 * H1],
                                              ALU.mult).then_inc(e_hid, 1)

                        def add_bias(t, r, s, e):
                            dve.wait_ge(e_up, t + 1)
                            reuse(dve, e_hid, t - 1)
                            dve.tensor_tensor(pre[:, s % 2, :], ps[:, 2 + s % 2, 0:width], biases[0][:, e, :],
                                              ALU.add).then_inc(e_pre, 1)

                        def finish(t, r, s, e):
                            dve.wait_ge(e_dn, t + 1)
                            reuse(dve, e_o[s], r * 16)
                            if gated:
                                ins = dve.tensor_copy(og[:, s, :], ps[:, 6 + s % 2, 0:D])
                            else:
                                ins = dve.tensor_tensor(og[:, s, :], ps[:, 6 + s % 2, 0:D], biases[1][:, e, :], ALU.add)
                            ins.then_inc(e_od, 1)

                        pipeline(dve, 4, None if gated else reader(dve, tab_e, E - 1), (1, gate if gated else add_bias), (4, finish))

        def rows_of(dve, ch, M, places, past, shift):
            shape = [P, B * TT * M.K, M.E]
            base = off[:, 0:E0] if M is M0 else off[:, E0:]
            ch.link(dve.tensor_tensor(past[:, :, :], places.unsqueeze(2).to_broadcast(shape),
                                      base.unsqueeze(1).to_broadcast(shape), ALU.is_gt))
            ch.link(dve.tensor_tensor(past[:, :, :], past[:, :, :], closer[:, 0:M.E].unsqueeze(1).to_broadcast(shape),
                                      ALU.mult))
            ch.link(dve.tensor_reduce(shift[:, :], past[:, :, :], X, ALU.add))
            ch.link(dve.tensor_tensor(shift[:, :], shift[:, :], places, ALU.add))
            ch.link(dve.tensor_scalar(shift[:, :], shift[:, :], float(M.dropped), None, ALU.min))

        def find_rows(st, M):
            C = TT * M.K
            find = sb("find", [P, B + 1, C], I32, scope=st)
            pws = sb("pws", [P, B + 1, C], scope=st)
            with ExitStack() as st1:
                pl = sb("qpl", [P, B * C], scope=st1)
                past = sb("qpast", [P, B * C, M.E], scope=st1)
                shift = sb("qshift", [P, B * C], scope=st1)
                with nc.Block() as block:
                    @block.sync
                    def _(sp):
                        sp.dma_start(pl[:, :].rearrange("p (b c) -> p b c", b=B),
                                     M.place.rearrange("b p c -> p b c")).then_inc(q_pl, 16)
                        sp.dma_start(pws[:, 0:B, :], M.weight.rearrange("b p c -> p b c")).then_inc(q_ld, 16)
                        sp.wait_ge(q_ld, 16)

                    @block.vector
                    def _(dve):
                        ch = Chain(dve, q_st)
                        ch.step(dve.memset(find[:, B, :], 0))
                        ch.step(dve.memset(pws[:, B, :], 0.0))
                        dve.wait_ge(q_pl, 16)
                        rows_of(dve, ch, M, pl[:, :], past, shift)
                        dve.tensor_copy(find[:, 0:B, :].rearrange("p b c -> p (b c)"), shift[:, :]).then_inc(q_row, 1)
            return find, pws

        def fetch(pool, M, dst, row):
            for c in range(TT * M.K):
                pool.indirect_dma_start(dst[:, c, :], None, M.outs,
                                        bass.IndirectOffsetOnAxis(row[:, c:c + 1], 0)).then_inc(M.fetched[c // M.K], 16)

        def combine_second(group):
            M = M1
            C = TT * M.K
            with ExitStack() as st:
                row = sb("qrow", [P, GR, C], I32, scope=st)
                pw = sb("qpw", [P, GR, C], scope=st)
                rg = sb("qrg", [P, GR, C, D], scope=st)
                acc = sb("qacc", [P, GR, TT, D], scope=st)
                with nc.Block() as block:
                    @block.sync
                    def _(sp):
                        for r in range(GR):
                            sp.dma_start(acc[:, r], resd[group * GR + r]).then_inc(q_res[r], 16)
                        for r in range(GR):
                            sp.wait_ge(q_acc, TT * (r + 1))
                            sp.dma_start(out.rearrange("b (t p) d -> b p t d", p=P)[group * GR + r],
                                         acc[:, r]).then_inc(q_out, 16)
                        sp.wait_ge(q_out, 16 * GR)

                    @block.gpsimd
                    def _(pool):
                        pool.wait_ge(q_row, 1)
                        for r in range(GR):
                            for c in range(C):
                                pool.indirect_dma_start(rg[:, r, c, :], None, M.outs,
                                                        bass.IndirectOffsetOnAxis(row[:, r, c:c + 1], 0)
                                                        ).then_inc(M.fetched[r], 16)

                    @block.vector
                    def _(dve):
                        ch = Chain(dve, q_st)
                        dve.tensor_copy(row[:, :, :], find[:, bass.ds(group * GR, GR), :]).then_inc(q_row, 1)
                        ch.step(dve.tensor_copy(pw[:, :, :], pws[:, bass.ds(group * GR, GR), :]))
                        ch.all_but(0)
                        for r in range(GR):
                            dve.wait_ge(M.fetched[r], group * (16 * C) + 16 * C)
                            dve.wait_ge(q_res[r], 16)
                            base = ch.n
                            for k in range(M.K):
                                for t in range(TT):
                                    if k:
                                        dve.wait_ge(q_st, base + TT * (k - 1) + t + 1)
                                    c = M.K * t + k
                                    ins = dve.scalar_tensor_tensor(out=acc[:, r, t, :], in0=rg[:, r, c, :],
                                                                   scalar=pw[:, r, c:c + 1], in1=acc[:, r, t, :],
                                                                   op0=ALU.mult, op1=ALU.add)
                                    if k < M.K - 1:
                                        ch.step(ins)
                                    else:
                                        ins.then_inc(q_acc, 1)

        def adapter_tensors(st):
            v = Tensors()
            v.z = sb("az", [P, T], scope=st)
            v.yy = sb("ayy", [P, DC, T], scope=st)
            v.yc = sb("ayc", [P, DC, T], scope=st)
            v.sq = sb("asq", [P, DC, T], scope=st)
            v.sd = sb("asd", [P, T], scope=st)
            v.rstd = sb("arstd", [P, T], scope=st)
            return v

        def adapter_pe(pe, v, part):
            if part == 0:
                product(pe, ps[:, 5, :], [(wa[:, k * P:(k + 1) * P], xa[:, k, :]) for k in range(DC)], d_z)
            elif part == 1:
                pe.wait_ge(d_za, 1)
                for j in range(DC):
                    product(pe, ps[:, 6 + j, :], [(wa[:, DC * P + j * P:DC * P + (j + 1) * P], v.z[:, :])], d_u)
            elif part == 2:
                pe.wait_ge(d_y, DC)
                product(pe, ps[:, 5, :], [(mean[:, :], v.yy[:, k, :]) for k in range(DC)], d_mn)
            else:
                pe.wait_ge(d_sq, DC)
                product(pe, ps[:, 6, :], [(mean[:, :], v.sq[:, k, :]) for k in range(DC)], d_var)

        def adapter_act(act, v, part):
            vec2 = wa[:, DC * P + D:]
            if part == 0:
                act.wait_ge(d_z, 1)
                act.activation(v.z[:, :], ps[:, 5, :], ACT.Relu, bias=vec2[:, 0:1]).then_inc(d_za, 1)
            elif part == 1:
                for j in range(DC):
                    act.wait_ge(d_yc, j + 1)
                    act.activation(v.sq[:, j, :], v.yc[:, j, :], ACT.Square).then_inc(d_sq, 1)
            else:
                act.wait_ge(d_var, 1)
                act.activation(v.sd[:, :], ps[:, 6, :], ACT.Sqrt, bias=epst[:, :]).then_inc(d_sd, 1)

        def adapter_sum(dve, v):
            bu = wa[:, DC * P + D + 1:DC * P + D + 3]
            for j in range(DC):
                dve.wait_ge(d_u, j + 1)
                dve.scalar_tensor_tensor(out=v.yy[:, j, :], in0=ps[:, 6 + j, :], scalar=bu[:, j:j + 1],
                                         in1=xa[:, j, :], op0=ALU.add, op1=ALU.add).then_inc(d_y, 1)
            dve.wait_ge(d_mn, 1)
            for j in range(DC):
                dve.wait_ge(d_y, j + 1)
                dve.tensor_tensor(v.yc[:, j, :], v.yy[:, j, :], ps[:, 5, :], ALU.subtract).then_inc(d_yc, 1)

        def adapter_norm(dve, v):
            ch = Chain(dve, d_st)
            lng, lnb = wa[:, DC * P + D + 3:DC * P + D + 5], wa[:, DC * P + D + 5:]
            dve.wait_ge(d_sd, 1)
            dve.wait_ge(d_yc, DC)
            ch.link(dve.reciprocal(v.rstd[:, :], v.sd[:, :]))
            for j in range(DC):
                ch.step(dve.scalar_tensor_tensor(out=ya[:, j, :], in0=v.yc[:, j, :], scalar=lng[:, j:j + 1],
                                                 in1=v.rstd[:, :], op0=ALU.mult, op1=ALU.mult))
            for j in range(DC):
                ch.all_but(1)
                ch.step(dve.tensor_scalar(ya[:, j, :], ya[:, j, :], lnb[:, j:j + 1], None, ALU.add))

        def adapter_last(loads):
            with ExitStack() as st:
                v = adapter_tensors(st)
                with nc.Block() as block:
                    @block.sync
                    def _(sp):
                        load_experts(sp, M1, loads)

                    @block.tensor
                    def _(pe):
                        for part in range(4):
                            adapter_pe(pe, v, part)

                    @block.scalar
                    def _(act):
                        for part in range(3):
                            adapter_act(act, v, part)

                    @block.vector
                    def _(dve):
                        adapter_sum(dve, v)
                        adapter_norm(dve, v)

        def load_lora(sp, b):
            sp.dma_start(ids[0:1, 0:1], a["subject"][b]).then_inc(l_id, 16)
            sp.wait_ge(l_id, 16)
            subject = sp.value_load(ids[0:1, 0:1], min_val=0, max_val=7)
            sp.dma_start(Ai[R:2 * R, :], a["Aie"][subject]).then_inc(l_w, 16)
            sp.dma_start(Bi[R:2 * R, :], a["Bie"][subject]).then_inc(l_w, 16)
            sp.dma_start(Ao[R:2 * R, :], a["Aoe"][subject]).then_inc(l_w, 16)
            sp.dma_start(Bo[R:2 * R, :], a["Boe"][subject]).then_inc(l_w, 16)
            sp.wait_ge(l_w, 64)

        def combine_and_feed(b, before):
            M = M0
            with ExitStack() as st:
                acc = sb("qacc", [P, TT, D], scope=st)
                hid = sb("lhid", [P, JF, T], scope=st)
                wie = sb("wie", [P, DC, FF], scope=st)
                woe = sb("woe", [P, JF, D], scope=st)
                INB = [2, 3, 4, 7]
                if before is not None:
                    v = adapter_tensors(st)
                with nc.Block() as block:
                    @block.sync
                    def _(sp):
                        sp.dma_start(x[:, :, :], x1d[b]).then_inc(q_ld, 16)

                    @block.tensor
                    def _(pe):
                        if before is not None:
                            adapter_pe(pe, v, 0)
                        for i in range(4):
                            k, n = i // 2, i % 2
                            product(pe, ps[:, INB[i], :], [(Ai[:, k * P:(k + 1) * P], Bi[:, n * 512:(n + 1) * 512])], l_lo)
                        for t in range(TT):
                            pe.wait_ge(q_acc, t + 1)
                            for j in range(DC):
                                pe.transpose(ps[:, j, t * P:(t + 1) * P], acc[:, t, j * P:(j + 1) * P],
                                             ident[:, :]).then_inc(q_tr, 1)
                        pe.wait_ge(l_wi, 4)
                        if before is not None:
                            adapter_pe(pe, v, 1)
                        pe.wait_ge(q_x, DC)
                        for f in range(JF):
                            if f >= 4:
                                pe.wait_ge(l_r, f - 3)
                            product(pe, ps[:, 1 + f % 4, :], [(wie[:, k, f * P:(f + 1) * P], x[:, k, :])
                                                              for k in range(DC)], l_h)
                            if before is not None and f in (1, 4):
                                adapter_pe(pe, v, 2 + f // 4)
                            if f in (2, 3, 5, 6):
                                i = (2, 3, 5, 6).index(f)
                                if i >= 2:
                                    pe.wait_ge(l_wo, i - 1)
                                elif i == 1 and before is not None:
                                    pe.wait_ge(d_y, DC)
                                for h in range(2):
                                    k = 2 * i + h
                                    product(pe, ps[:, 7 * (i % 2), h * D:(h + 1) * D],
                                            [(Ao[:, k * P:(k + 1) * P], Bo[:, :])], l_do)
                        pe.wait_ge(l_wo, 4)
                        for k in range(JF):
                            pe.wait_ge(l_r, k + 1)
                            for j in range(DC):
                                ins = pe.matmul(ps[:, 6 + j, :], woe[:, k, j * P:(j + 1) * P], hid[:, k, :],
                                                start=(k == 0), stop=(k == JF - 1))
                        ins.then_inc(l_o, 1)

                    @block.scalar
                    def _(act):
                        if before is not None:
                            adapter_act(act, v, 0)
                        for f in range(JF):
                            act.wait_ge(l_h, f + 1)
                            act.activation(hid[:, f, :], ps[:, 1 + f % 4, :], ACT.Relu).then_inc(l_r, 1)
                            if before is not None and f in (2, 5):
                                adapter_act(act, v, 1 + f // 4)
                        act.wait_ge(l_o, 1)
                        for j in range(DC):
                            act.activation(y[:, j, :], ps[:, 6 + j, :], ACT.Copy).then_inc(l_oc, 1)

                    @block.vector
                    def _(dve):
                        ch = Chain(dve, q_st)
                        for t in range(TT):
                            dve.wait_ge(M.fetched[t], b * (16 * M.K) + 16 * M.K)
                            ch.link(dve.tensor_scalar(acc[:, t, :], rg[:, 2 * t, :], pw[:, 2 * t:2 * t + 1], None, ALU.mult))
                            dve.scalar_tensor_tensor(out=acc[:, t, :], in0=rg[:, 2 * t + 1, :],
                                                     scalar=pw[:, 2 * t + 1:2 * t + 2],
                                                     in1=acc[:, t, :], op0=ALU.mult, op1=ALU.add).then_inc(q_acc, 1)
                        for i in range(4):
                            k, n = i // 2, i % 2
                            dve.wait_ge(l_lo, i + 1)
                            dve.scalar_tensor_tensor(out=wie[:, k, n * 512:(n + 1) * 512], in0=ps[:, INB[i], :],
                                                     scalar=2.0, in1=wi[:, k, n * 512:(n + 1) * 512],
                                                     op0=ALU.mult, op1=ALU.add).then_inc(l_wi, 1)
                        dve.wait_ge(q_ld, 16)
                        dve.wait_ge(q_tr, TT * DC)
                        for j in range(DC):
                            dve.tensor_tensor(x[:, j, :], x[:, j, :], ps[:, j, :], ALU.add).then_inc(q_x, 1)

                        def add_out(i):
                            dve.wait_ge(l_do, 2 * i + 2)
                            dve.scalar_tensor_tensor(out=woe[:, 2 * i:2 * i + 2, :], in0=halves(7 * (i % 2)), scalar=2.0,
                                                     in1=wo[:, 2 * i:2 * i + 2, :], op0=ALU.mult,
                                                     op1=ALU.add).then_inc(l_wo, 1)

                        if before is not None:
                            adapter_sum(dve, v)
                        add_out(0)
                        add_out(1)
                        if before is not None:
                            adapter_norm(dve, v)
                        add_out(2)
                        add_out(3)

        def attention(b, before):
            with ExitStack() as st:
                Qz = sb("Qz", [P, NH, T], scope=st)
                Kt = sb("Kt", [P, NH // 2, T], scope=st)
                V = sb("V", [P, TT, NH * D], scope=st)
                with ExitStack() as st1:
                    v = second_tensors(st1) if before is not None else None
                    parts = {1: 1, 4: 2, 6: 3, 10: 4, 12: 5} if before is not None else {}
                    with nc.Block() as block:
                        @block.sync
                        def _(sp):
                            if before is not None:
                                second_store(sp, before, v)

                        @block.gpsimd
                        def _(pool):
                            for h in range(NH):
                                o = RH * (1 - h % 2)
                                pool.memset(Qz[o:o + RH, h, :], 0.0).then_inc(a_z, 1)

                        @block.tensor
                        def _(pe):
                            if before is not None:
                                second_pe(pe, v, 0)
                            for i in range(NH + 4 * TT):
                                if i >= 4:
                                    pe.wait_ge(a_ea, 2 * (i - 3) if i < 8 else i + 1)
                                if i < NH:
                                    W, j = (Wq, i) if i < NH // 2 else (Wk, i - NH // 2)
                                    pairs = [(W[:, k, j * P:(j + 1) * P], y[:, k, :]) for k in range(DC)]
                                else:
                                    t, n = (i - NH) // 4, (i - NH) % 4
                                    pairs = [(y[:, k, t * P:(t + 1) * P], Wv[:, k, n * 512:(n + 1) * 512])
                                             for k in range(DC)]
                                product(pe, ps[:, i % 4, :], pairs, a_pj)
                                if i in parts:
                                    second_pe(pe, v, parts[i])

                        @block.scalar
                        def _(act):
                            if before is not None:
                                second_act(act, v, 0)
                            for i in range(NH + 4 * TT):
                                act.wait_ge(a_pj, i + 1)
                                if i < NH // 2:
                                    for h in (2 * i, 2 * i + 1):
                                        o = RH * (h % 2)
                                        act.activation(Qz[o:o + RH, h, :], ps[o:o + RH, i % 4, :],
                                                       ACT.Copy).then_inc(a_ea, 1)
                                elif i < NH:
                                    act.activation(Kt[:, i - NH // 2, :], ps[:, i % 4, :], ACT.Copy).then_inc(a_ea, 1)
                                else:
                                    t, n = (i - NH) // 4, (i - NH) % 4
                                    act.activation(V[:, t, n * 512:(n + 1) * 512], ps[:, i % 4, :],
                                                   ACT.Copy).then_inc(a_ea, 1)
                                if parts.get(i, 4) < 4:
                                    second_act(act, v, parts[i])

                        @block.vector
                        def _(dve):
                            if before is not None:
                                second_dve(dve, v)
                with ExitStack() as st2:
                    pp = sb("pp", [P, 2, TT, T], scope=st2)
                    pT = sb("pT", [P, 2, TT, T], scope=st2)
                    mx = sb("mx", [P, 2, TT], scope=st2)
                    nm = sb("nm", [P, 2, TT], scope=st2)
                    sm = sb("sm", [P, 2, TT], scope=st2)
                    rs = sb("rs", [P, 2, TT], scope=st2)
                    with nc.Block() as block:
                        @block.gpsimd
                        def _(pool):
                            pool.wait_ge(n_row, 1)
                            fetch(pool, M0, rg, row)
                            list_tokens(pool, M1, b)

                        @block.sync
                        def _(sp):
                            sp.dma_start(ids[0:1, 1:2], a["profile"][b]).then_inc(d_id, 16)
                            sp.wait_ge(d_id, 16)
                            profile = sp.value_load(ids[0:1, 1:2], min_val=0, max_val=7)
                            sp.dma_start(wa[:, :], a["Wad"][profile]).then_inc(d_w, 16)
                            sp.wait_ge(d_w, 16)
                            load_lora(sp, b + 1)

                        @block.tensor
                        def _(pe):
                            def scores(h):
                                if h:
                                    pe.wait_ge(p_ex, TT * h)
                                for t in range(TT):
                                    product(pe, ps[:, t, :], [(Qz[:, h, t * P:(t + 1) * P], Kt[:, h // 2, :])], p_s)

                            def turn(h, m):
                                i = TT * h + m
                                pe.wait_ge(p_nm, TT * (h + 1))
                                if i >= 2:
                                    pe.wait_ge(p_ta if m % 2 == 0 else p_td, (i - 2) // 2 + 1)
                                for t in range(TT):
                                    ins = pe.transpose(ps[:, 4 + m % 2, t * P:(t + 1) * P],
                                                       pp[:, h % 2, t, m * P:(m + 1) * P], ident[:, :])
                                ins.then_inc(p_tp, 1)

                            def values(h):
                                pe.wait_ge(p_ta, 2 * (h + 1))
                                pe.wait_ge(p_td, 2 * (h + 1))
                                for j in range(DC):
                                    for m in range(TT):
                                        ins = pe.matmul(ps[:, 6 + j, :], V[:, m, h * D + j * P:h * D + (j + 1) * P],
                                                        pT[:, h % 2, m, :], start=(h == 0 and m == 0),
                                                        stop=(h == NH - 1 and m == TT - 1))
                                ins.then_inc(p_pv, 1)

                            scores(0)
                            for h in range(NH):
                                if h + 1 < NH:
                                    scores(h + 1)
                                turn(h, 0)
                                turn(h, 1)
                                if h:
                                    values(h - 1)
                                turn(h, 2)
                                turn(h, 3)
                            values(NH - 1)

                        @block.scalar
                        def _(act):
                            def exps(h):
                                act.wait_ge(p_mx, h + 1)
                                if h >= 2:
                                    act.wait_ge(p_tp, TT * (h - 1))
                                for t in range(TT):
                                    act.activation(pp[:, h % 2, t, :], ps[:, t, :], ACT.Exp, bias=nm[:, h % 2, t:t + 1],
                                                   accum_out=sm[:, h % 2, t:t + 1]).then_inc(p_ex, 1)

                            exps(0)
                            for h in range(NH):
                                if h + 1 < NH:
                                    exps(h + 1)
                                for m in (0, 2):
                                    act.wait_ge(p_tp, TT * h + m + 1)
                                    if h >= 2:
                                        act.wait_ge(p_pv, h - 1)
                                    act.activation(pT[:, h % 2, m, :], ps[:, 4, :], ACT.Copy).then_inc(p_ta, 1)

                        @block.vector
                        def _(dve):
                            ch = Chain(dve, p_st)

                            def maxima(h):
                                dve.wait_ge(p_s, TT * (h + 1))
                                if h >= 2:
                                    dve.wait_ge(p_ex, TT * (h - 1))
                                ch.link(dve.tensor_reduce(mx[:, h % 2, :], ps[:, 0:TT, :], X, ALU.max))
                                dve.tensor_scalar(nm[:, h % 2, :], mx[:, h % 2, :], -1.0, None, ALU.mult).then_inc(p_mx, 1)

                            def normalise(h):
                                dve.wait_ge(p_ex, TT * (h + 1))
                                if h >= 2:
                                    dve.wait_ge(p_nm, TT * (h - 1))
                                ch.link(dve.reciprocal(rs[:, h % 2, :], sm[:, h % 2, :]))
                                for t in range(TT):
                                    dve.tensor_scalar(pp[:, h % 2, t, :], pp[:, h % 2, t, :], rs[:, h % 2, t:t + 1],
                                                      None, ALU.mult).then_inc(p_nm, 1)

                            dve.tensor_copy(row[:, :], find[:, bass.ds(b + 1, 1), :].rearrange("p b c -> p (b c)")
                                            ).then_inc(n_row, 1)
                            ch.step(dve.tensor_copy(pw[:, :], pws[:, bass.ds(b + 1, 1), :].rearrange("p b c -> p (b c)")))
                            maxima(0)
                            normalise(0)
                            for h in range(NH):
                                if h + 1 < NH:
                                    maxima(h + 1)
                                dve.wait_ge(p_tp, TT * h + 2)
                                if h >= 2:
                                    dve.wait_ge(p_pv, h - 1)
                                dve.tensor_copy(pT[:, h % 2, 1, :], ps[:, 5, :]).then_inc(p_td, 1)
                                if h + 1 < NH:
                                    normalise(h + 1)
                                dve.wait_ge(p_tp, TT * h + 4)
                                dve.tensor_copy(pT[:, h % 2, 3, :], ps[:, 5, :]).then_inc(p_td, 1)
                            dve.wait_ge(p_pv, NH)
                            for j in range(DC):
                                ch.step(dve.tensor_tensor(xa[:, j, :], x[:, j, :], ps[:, 6 + j, :], ALU.add))

        loop_sems = range(first_sem, len(sems))

        def clear_semaphores():
            with nc.Block() as block:
                @block.sync
                def _(sp):
                    sp.sem_clear(range(sems[loop_sems.start].num, sems[loop_sems.stop - 1].num + 1))

        with ExitStack() as st:
            ws = sb("ws", [P, DC * D + DC], scope=st)
            xm = sb("xm", [P, DC, T], scope=st)
            (Wg, Wn1, Wn2r, Wsoma, Wtemp, WoutC, Win, Wxd, Wxbc, Wdt, Wo, Wg0, bg0, vec, cw, An, alpha, bn2,
             mix, sel, h1, dts) = load_first(st)
            bg, bsoma, btemp, gamma, beta = (vec[:, DC * i:DC * (i + 1)] for i in range(5))
            bn1 = vec[:, 5 * DC:5 * DC + 1]
            convb, bdt, Dv = (vec[:, 5 * DC + 1 + JI * i:5 * DC + 1 + JI * (i + 1)] for i in range(3))
            conditioner_first()
            clear_semaphores()
            mixer(0, 1, None)
            clear_semaphores()
            with nc.Fori(1, B - 1) as b:
                mixer(b, b + 1, b - 1)
                clear_semaphores()
            mixer(B - 1, None, B - 2)
            clear_semaphores()
            W0u = sb("W0u", [P, E0, DC, H0], scope=st)
            W0d = sb("W0d", [P, E0, JH, D], scope=st)
            b1 = sb("b1", [P, E0, H0], scope=st)
            b2 = sb("b2", [P, E0, D], scope=st)
            loads = [(W0u[:, :, :, :], a["W0u"]), (W0d[:, :, :, :], a["W0d"]),
                     (b1[:, :, :].rearrange("p e h -> p (e h)"), a["b1"].partition_broadcast(P)),
                     (b2[:, :, :].rearrange("p e h -> p (e h)"), a["b2"].partition_broadcast(P))]
            route_last(B - 1, loads)
            clear_semaphores()
            experts(M0, W0u, W0d, loads, biases=(b1, b2))
            clear_semaphores()
        with ExitStack() as st:
            wi, wo, Ai, Bi, Ao, Bo, Wg1, Wq, Wk, Wv, Wsh, weights_in = load_second(st)
            wa = sb("wa", [P, DC * P + D + 7], scope=st)
            xa = sb("xa", [P, DC, T], scope=st)
            ya = sb("ya", [P, DC, T], scope=st)
            row = sb("row", [P, TT * K0], I32, scope=st)
            pw = sb("pw_next", [P, TT * K0], scope=st)
            rg = sb("rg", [P, TT * K0, D], scope=st)
            find, pws = find_rows(st, M0)
            with nc.Block() as block:
                @block.vector
                def _(dve):
                    dve.tensor_copy(row[:, :], find[:, 0, :]).then_inc(n_row, 1)
                    dve.tensor_copy(pw[:, :], pws[:, 0, :]).then_inc(n_row, 1)

                @block.gpsimd
                def _(pool):
                    pool.wait_ge(n_row, 2)
                    fetch(pool, M0, rg, row)

                @block.sync
                def _(sp):
                    load_lora(sp, 0)
                    sp.wait_ge(weights_in, 16 * 11)
            clear_semaphores()
            combine_and_feed(0, None)
            attention(0, None)
            clear_semaphores()
            with nc.Fori(1, B) as b:
                combine_and_feed(b, b - 1)
                attention(b, b - 1)
                clear_semaphores()
            W1u = sb("W1u", [P, E1, DC, 2 * H1], scope=st)
            W1d = sb("W1d", [P, E1, 1, D], scope=st)
            loads = [(W1u[:, :, :, :], a["W1u"]), (W1d[:, :, :, :], a["W1d"])]
            adapter_last(loads)
            route_second_last(B - 1)
            clear_semaphores()
            experts(M1, W1u, W1d, loads)
            clear_semaphores()
        with ExitStack() as st:
            find, pws = find_rows(st, M1)
            clear_semaphores()
            with nc.Fori(0, B // GR) as group:
                combine_second(group)
                clear_semaphores()


def kxm(w):
    w = np.asarray(w)
    return np.ascontiguousarray(w.reshape(w.shape[0] // P, P, w.shape[1]).transpose(1, 0, 2))


def cols(v):
    return np.asarray(v).reshape(-1, P).T


def arrays_of(i):
    g = {k: np.asarray(v) for k, v in i.items()}
    pad = lambda v: np.concatenate([v.reshape(-1, 1), np.zeros((P - v.size, 1), np.float32)])
    flat = lambda *ws: np.concatenate([w.reshape(P, -1) for w in ws], 1)
    h = {
        "x": g["x"].transpose(0, 2, 1).reshape(B, DC, P, T).transpose(0, 2, 1, 3),
        "Wg": kxm(g["L0_cond_Wg"].T), "Wn1": kxm(g["L0_cond_Wn1"].T), "Wn2": g["cond_256"].T,
        "Wsoma": kxm(g["L0_cond_Wsoma"].T), "Wtemp": kxm(g["L0_cond_Wtemp"].T), "Wout": kxm(g["L0_cond_Wout"].T),
        "Win": kxm(g["L0_attn_W_in"].T), "Wxd": kxm(g["L0_attn_W_x"][:DTR].T), "Wxbc": kxm(g["L0_attn_W_x"][DTR:].T),
        "Wdt": g["L0_attn_W_dt"].T, "Wo": kxm(g["L0_attn_W_out"].T),
        "wi": kxm(g["L1_cond_wi"].T), "wo": kxm(g["L1_cond_wo"].T),
        "Aic": g["L1_cond_common_wi_a"], "Bic": g["L1_cond_common_wi_b"].T,
        "Aoc": g["L1_cond_common_wo_a"], "Boc": g["L1_cond_common_wo_b"].T,
        "Aie": g["L1_cond_experts_wi_a"],
        "Bie": g["L1_cond_experts_wi_b"].transpose(0, 2, 1),
        "Aoe": g["L1_cond_experts_wo_a"],
        "Boe": g["L1_cond_experts_wo_b"].transpose(0, 2, 1),
        "Wq": kxm(g["L1_attn_Wq"].T), "Wk": kxm(g["L1_attn_Wk"].T), "Wv": kxm(g["L1_attn_Wv"].T),
        "Wg0": kxm(g["L0_ffn_Wg"]), "Wg1": kxm(g["L1_ffn_Wg"]), "b2": g["L0_ffn_b2"].reshape(-1),
        "b1": g["L0_ffn_b1"].reshape(-1), "bg0": g["L0_ffn_bg"],
        "vec": np.concatenate([cols(g["L0_cond_" + n]) for n in ("bg", "bsoma", "btemp", "gamma", "beta")]
                              + [pad(g["L0_cond_bn1"])]
                              + [cols(g["L0_attn_" + n]) for n in ("conv_b", "b_dt", "D")], 1),
        "cw": g["L0_attn_conv_w"].reshape(JI, P, 4).transpose(1, 0, 2),
        "Araw": g["L0_attn_A_raw"].reshape(NS, JI, P).transpose(2, 1, 0),
        "tau": g["condB_tauraws"], "tau_ctx": g["L0_cond_tau_ctx"].reshape(1), "bn2": g["condB_bn2"],
        "blend": g["cond_1024"].reshape(NTR, DC, P).transpose(2, 1, 0),
        "subject": np.concatenate([g["itok_B_0_7"], np.zeros(1, np.int32)]).reshape(B + 1, 1, 1), "profile": g["itok_B_0_6"].reshape(B, 1, 1),
        "Wsub": np.stack([flat(kxm(w.T), cols(v)) for w, v in zip(g["L0_cond2_weight"], g["L0_cond2_bias"])]),
        "W0u": np.stack([kxm(w) for w in g["L0_ffn_W1"]]).transpose(1, 0, 2, 3),
        "W0d": np.stack([kxm(w) for w in g["L0_ffn_W2"]]).transpose(1, 0, 2, 3),
        "Wad": np.stack([flat(kxm(g["L1_cond2_down_w"][e]), g["L1_cond2_up_w"][e],
                              *(cols(g["L1_cond2_" + n][e]) for n in ("down_b", "up_b", "ln_g", "ln_b")))
                         for e in range(8)]),
        "W1u": np.stack([kxm(np.concatenate([w1, w3], 1)) for w1, w3 in
                         zip(g["L1_ffn_W1"], g["L1_ffn_W3"])]).transpose(1, 0, 2, 3),
        "W1d": g["L1_ffn_W2"].transpose(1, 0, 2).reshape(P, E1, 1, D),
        "Wsh": np.stack([flat(kxm(g["L1_ffn_Ws1"][:, H1 * s:H1 * (s + 1)]), kxm(g["L1_ffn_Ws3"][:, H1 * s:H1 * (s + 1)]),
                              g["L1_ffn_Ws2"][H1 * s:H1 * (s + 1)]) for s in range(ES)], 1),
    }
    return {k: np.ascontiguousarray(v) for k, v in h.items()}


def kernel(**inputs):
    import concourse.bacc as bacc
    from concourse.bass_utils import run_bass_kernel_spmd

    nc = bacc.Bacc("TRN2", target_bir_lowering=False, num_devices=1)
    arrays = {f"in_{k}": v for k, v in arrays_of(inputs).items()}
    aps = {k[3:]: nc.dram_tensor(k, v.shape, mybir.dt.from_np(v.dtype), kind="ExternalInput").ap()
           for k, v in arrays.items()}
    out = nc.dram_tensor("out", (B, T, D), F32, kind="ExternalOutput").ap()
    build(nc, aps, out)
    r = run_bass_kernel_spmd(nc, [arrays], core_ids=[0])
    return r.results[0]["out"]
```
